# Optimizing a Trainium2 kernel written in Bass

```python
import numpy as np
import jax
import jax.numpy as jnp

def _softmax(x, axis=-1):
    return jax.nn.softmax(x, axis=axis)

def _gelu(x):
    return jax.nn.gelu(x, approximate=True)

def _silu(x):
    return jax.nn.silu(x)

def _sigmoid(x):
    return jax.nn.sigmoid(x)

def _layernorm(x, axis=-1, eps=1e-05):
    m = jnp.mean(x, axis=axis, keepdims=True)
    v = jnp.var(x, axis=axis, keepdims=True)
    return (x - m) / jnp.sqrt(v + eps)

def _scatter_add(tgt, idx, src, axis=0):
    return tgt.at[idx].add(src)

def _segment_sum(src, seg, n):
    return jax.ops.segment_sum(src, seg, n)
kernel_name = 'mk_gnn_preln_d4_gnn_r8_f192fe'

def setup_inputs(seed: int=0):
    np.random.seed(seed)
    _w = jnp.asarray

    def _rec_inputs():
        import jax
        import jax.numpy as jnp
        _gk = jax.random.key(seed)
        x = -0.0004776 + 1.001 * jax.random.normal(jax.random.fold_in(_gk, 1), (1250, 1024), jnp.float32)
        src = jax.random.randint(jax.random.fold_in(_gk, 2), (20000,), 0, 1250, jnp.int32)
        dst = jax.random.randint(jax.random.fold_in(_gk, 3), (20000,), 0, 1250, jnp.int32)
        _o = jnp.argsort(dst, stable=True)
        src = src[_o]
        dst = dst[_o]
        edge_weight = -0.000130211 + 0.031236 * jax.random.normal(jax.random.fold_in(_gk, 13), (20000,), jnp.float32)
        return (x, src, dst, edge_weight)
    x, src, dst, edge_weight = _rec_inputs()

    def _L0_gnn_setup():
        import jax, jax.numpy as jnp
        import numpy as np
        N_DIM = 1024
        NHID = 512
        NUM_K = 4
        DIA_LEN = [50] * 60
        N_NODES = sum(DIA_LEN)

        def _build_edge_index(dia_len):
            pieces = []
            off = 0
            for L in dia_len:
                idx = np.arange(off, off + L)
                src = np.repeat(idx, L)
                dst = np.tile(idx, L)
                m = src != dst
                pieces.append(np.stack([src[m], dst[m]], axis=0))
                off += L
            return np.concatenate(pieces, axis=1).astype(np.int32)

        def _graph_gcn(x, row, col, gw, gb, n_nodes):
            deg = jax.ops.segment_sum(jnp.ones(row.shape[0], x.dtype), col, num_segments=n_nodes)
            dis = jnp.maximum(deg, 1.0) ** (-0.5)
            norm = dis[row] * dis[col]
            x_i = x[col]
            x_j = x[row]
            alpha = jnp.tanh(x_i @ gw[:x.shape[1]] + x_j @ gw[x.shape[1]:] + gb)
            msg = norm[:, None] * alpha * x_j
            return jax.ops.segment_sum(msg, col, num_segments=n_nodes)
        key = jax.random.key(seed)
        ks = jax.random.split(key, 6)
        emotions_feat = jax.random.normal(ks[0], (N_NODES, N_DIM), dtype=jnp.float32)
        qmask = jax.random.uniform(ks[1], (max(DIA_LEN), len(DIA_LEN), 2), dtype=jnp.float32)
        edge_index = jnp.asarray(_build_edge_index(DIA_LEN))
        s1 = 1.0 / np.sqrt(N_DIM)
        W1 = jax.random.uniform(ks[2], (N_DIM, NHID), minval=-s1, maxval=s1, dtype=jnp.float32)
        b1 = jax.random.uniform(ks[3], (NHID,), minval=-s1, maxval=s1, dtype=jnp.float32)
        s2 = 1.0 / np.sqrt(2 * NHID)
        gate_w = jax.random.uniform(ks[4], (NUM_K, 2 * NHID, 1), minval=-s2, maxval=s2, dtype=jnp.float32)
        gate_b = jax.random.uniform(ks[5], (NUM_K, 1), minval=-s2, maxval=s2, dtype=jnp.float32)
        return {'emotions_feat': emotions_feat, 'qmask': qmask, 'edge_index': edge_index, 'epoch': 0, 'W1': W1, 'b1': b1, 'gate_w': gate_w, 'gate_b': gate_b}
    _L0_gnn_all = _L0_gnn_setup()
    _L0_gnn_in = {k: v for k, v in _L0_gnn_all.items() if k in ('qmask', 'W1', 'b1', 'gate_w', 'gate_b')}
    del _L0_gnn_all

    def _L1_gnn_setup():
        import jax, jax.numpy as jnp
        import numpy as np
        INDIM = 1024
        OUTDIM = 1024
        NNZ = 8192
        N = 6250
        key = jax.random.key(seed)
        k1, k2, k3, k4, k5 = jax.random.split(key, 5)
        x = jax.random.normal(k1, (N, INDIM), dtype=jnp.float32)
        stdv = np.sqrt(6.0 / (INDIM + OUTDIM))
        nnz_weight = jax.random.uniform(k2, (NNZ,), dtype=jnp.float32, minval=-stdv, maxval=stdv)
        bias = jax.random.normal(k3, (OUTDIM,), dtype=jnp.float32) * 0.02
        row = jax.random.randint(k4, (NNZ,), 0, OUTDIM, dtype=jnp.int64)
        col = jax.random.randint(k5, (NNZ,), 0, INDIM, dtype=jnp.int64)
        edge_index = jnp.stack([row, col])
        return {'x': x, 'nnz_weight': nnz_weight, 'bias': bias, 'edge_index': edge_index}
    _L1_gnn_all = _L1_gnn_setup()
    _L1_gnn_in = {k: v for k, v in _L1_gnn_all.items() if k in ('bias',)}
    del _L1_gnn_all

    def _L2_gnn_setup():
        import jax, jax.numpy as jnp
        import numpy as np
        N_NODES = 1250
        N_EDGES = 20000
        DIM = 1024
        key = jax.random.key(seed)
        k1, k2, k3 = jax.random.split(key, 3)
        x = jax.random.normal(k1, (N_NODES, DIM), dtype=jnp.float32)
        edge_index = jax.random.randint(k2, (2, N_EDGES), 0, N_NODES, dtype=jnp.int64)
        W = jax.random.normal(k3, (DIM, DIM), dtype=jnp.float32) * (1.0 / np.sqrt(DIM))
        b = jnp.zeros((DIM,), dtype=jnp.float32)
        return {'x': x, 'edge_index': edge_index, 'W': W, 'b': b}
    _L2_gnn_all = _L2_gnn_setup()
    _L2_gnn_in = {k: v for k, v in _L2_gnn_all.items() if k in ('W', 'b')}
    del _L2_gnn_all

    def _L3_gnn_setup():
        import jax, jax.numpy as jnp
        import numpy as np
        NEG_SLOPE = 0.1
        EPS = 1e-05
        key = jax.random.key(seed)
        k1, k2, k3, k4, k5 = jax.random.split(key, 5)
        N, E, DIN, DOUT = (1250, 20000, 1024, 1024)
        x = jax.random.normal(k1, (N, DIN), dtype=jnp.float32)
        W = jax.random.normal(k2, (DIN, DOUT), dtype=jnp.float32) * 0.02
        a = jax.random.normal(k3, (1, 2 * DOUT), dtype=jnp.float32) * 0.02
        src = jax.random.randint(k4, (E,), 0, N, dtype=jnp.int64)
        dst = jax.random.randint(k5, (E,), 0, N, dtype=jnp.int64)
        return {'x': x, 'W': W, 'a': a, 'src': src, 'dst': dst}
    _L3_gnn_all = _L3_gnn_setup()
    _L3_gnn_in = {k: v for k, v in _L3_gnn_all.items() if k in ('W', 'a')}
    del _L3_gnn_all
    return {'x': x, 'src': src, 'dst': dst, 'edge_weight': edge_weight, 'L0_gnn_qmask': _L0_gnn_in['qmask'], 'L0_gnn_W1': _L0_gnn_in['W1'], 'L0_gnn_b1': _L0_gnn_in['b1'], 'L0_gnn_gate_w': _L0_gnn_in['gate_w'], 'L0_gnn_gate_b': _L0_gnn_in['gate_b'], 'L1_gnn_bias': _L1_gnn_in['bias'], 'L2_gnn_W': _L2_gnn_in['W'], 'L2_gnn_b': _L2_gnn_in['b'], 'L3_gnn_W': _L3_gnn_in['W'], 'L3_gnn_a': _L3_gnn_in['a']}

def reference(x, src, dst, edge_weight, L0_gnn_qmask, L0_gnn_W1, L0_gnn_b1, L0_gnn_gate_w, L0_gnn_gate_b, L1_gnn_bias, L2_gnn_W, L2_gnn_b, L3_gnn_W, L3_gnn_a):
    import jax
    import jax.numpy as jnp

    def _L0_gnn_ref(emotions_feat, qmask, edge_index, epoch, W1, b1, gate_w, gate_b):
        import jax, jax.numpy as jnp
        import numpy as np
        N_DIM = 1024
        NHID = 512
        NUM_K = 4
        DIA_LEN = [50] * 60
        N_NODES = sum(DIA_LEN)

        def _build_edge_index(dia_len):
            pieces = []
            off = 0
            for L in dia_len:
                idx = np.arange(off, off + L)
                src = np.repeat(idx, L)
                dst = np.tile(idx, L)
                m = src != dst
                pieces.append(np.stack([src[m], dst[m]], axis=0))
                off += L
            return np.concatenate(pieces, axis=1).astype(np.int32)

        def _graph_gcn(x, row, col, gw, gb, n_nodes):
            deg = jax.ops.segment_sum(jnp.ones(row.shape[0], x.dtype), col, num_segments=n_nodes)
            dis = jnp.maximum(deg, 1.0) ** (-0.5)
            norm = dis[row] * dis[col]
            x_i = x[col]
            x_j = x[row]
            alpha = jnp.tanh(x_i @ gw[:x.shape[1]] + x_j @ gw[x.shape[1]:] + gb)
            msg = norm[:, None] * alpha * x_j
            return jax.ops.segment_sum(msg, col, num_segments=n_nodes)
        row, col = (edge_index[0], edge_index[1])
        n_nodes = emotions_feat.shape[0]
        x1 = emotions_feat @ W1 + b1
        gnn_out = x1
        for kk in range(NUM_K):
            gnn_out = gnn_out + _graph_gcn(gnn_out, row, col, gate_w[kk], gate_b[kk], n_nodes)
        return jnp.concatenate([x1, gnn_out], axis=1)

    def _L1_gnn_ref(x, nnz_weight, bias, edge_index):
        import jax, jax.numpy as jnp
        import numpy as np
        INDIM = 1024
        OUTDIM = 1024
        NNZ = 8192
        N = 6250
        row, col = (edge_index[0], edge_index[1])
        W = jnp.zeros((OUTDIM, INDIM), dtype=nnz_weight.dtype).at[row, col].add(nnz_weight)
        return x @ W.T + bias

    def _L2_gnn_ref(x, edge_index, W, b):
        import jax, jax.numpy as jnp
        import numpy as np
        N_NODES = 1250
        N_EDGES = 20000
        DIM = 1024
        'GCNConv (add_self_loops=True, symmetric norm) -> Dropout(eval=identity) -> ReLU.'
        n = x.shape[0]
        loops = jnp.arange(n, dtype=edge_index.dtype)
        src = jnp.concatenate([edge_index[0], loops])
        dst = jnp.concatenate([edge_index[1], loops])
        deg = jax.ops.segment_sum(jnp.ones_like(dst, dtype=x.dtype), dst, num_segments=n)
        dinv = jnp.where(deg > 0, jax.lax.rsqrt(deg), jnp.zeros_like(deg))
        norm = dinv[src] * dinv[dst]
        h = x @ W
        msg = h[src] * norm[:, None]
        out = jax.ops.segment_sum(msg, dst, num_segments=n) + b
        return jax.nn.relu(out)

    def _L3_gnn_ref(x, W, a, src, dst):
        import jax, jax.numpy as jnp
        import numpy as np
        NEG_SLOPE = 0.1
        EPS = 1e-05
        N = x.shape[0]
        d = W.shape[1]
        h = x @ W
        a_l, a_r = (a[0, :d], a[0, d:])
        al = h @ a_l
        ar = h @ a_r
        e = jnp.exp(-jax.nn.leaky_relu(al[src] + ar[dst], negative_slope=NEG_SLOPE))
        rowsum = jax.ops.segment_sum(e, src, num_segments=N)
        h_prime = jax.ops.segment_sum(e[:, None] * h[dst], src, num_segments=N)
        h_prime = h_prime / (rowsum[:, None] + EPS)
        return jax.nn.elu(h_prime)
    edge_index = jnp.stack([src, dst])
    h = jnp.maximum(_layernorm(x, axis=-1), 0.0)
    x = x + _L0_gnn_ref(h, L0_gnn_qmask, edge_index, 0, L0_gnn_W1, L0_gnn_b1, L0_gnn_gate_w, L0_gnn_gate_b)
    h = jnp.maximum(_layernorm(x, axis=-1), 0.0)
    x = x + _L1_gnn_ref(h, edge_weight, L1_gnn_bias, edge_index)
    h = jnp.maximum(_layernorm(x, axis=-1), 0.0)
    x = x + _L2_gnn_ref(h, edge_index, L2_gnn_W, L2_gnn_b)
    h = jnp.maximum(_layernorm(x, axis=-1), 0.0)
    x = x + _L3_gnn_ref(h, L3_gnn_W, L3_gnn_a, src, dst)
    return x

_drawn_inputs = setup_inputs


def setup_inputs(seed=0):
    import zlib

    import numpy as np

    out = dict(_drawn_inputs(seed))
    spreads = {'L2_gnn_b': (0.0, 0.1)}
    factors = {'L0_gnn_b1': 3.548, 'L0_gnn_gate_b': 64.0, 'L1_gnn_bias': 3.03, 'L3_gnn_a': 15.022}
    for name, (base, spread) in spreads.items():
        noise = np.random.default_rng([zlib.crc32(name.encode()), seed]).standard_normal(out[name].shape)
        drawn = base * np.exp(spread * noise) if base else spread * noise
        out[name] = jnp.asarray(drawn.astype(out[name].dtype))
    for name, factor in factors.items():
        out[name] = (out[name] * factor).astype(out[name].dtype)
    return out
```

```python
from contextlib import ExitStack

import concourse.bass as bass
from concourse import mybir

ALU = mybir.AluOpType
ACT = mybir.ActivationFunctionType
AX_X = mybir.AxisListType.X
F32 = mybir.dt.float32
F32R = mybir.dt.float32r
BF16 = mybir.dt.bfloat16
F16 = mybir.dt.float16
I32 = mybir.dt.int32
I16 = mybir.dt.int16

P = 128
D = 1024
HID = 512
GATES = 4
N = 1250
E = 20000
T = -(-N // P)
NP = T * P
KT = D // P
WT_TILES = KT
WIN = 32
QW = P // WIN
WINDOWS = T * QW
CHUNKS = 5
CAP = CHUNKS * P
EP = 125
EC = E // EP
GENERAL_CHUNKS = E // (EP * CHUNKS)
HALF = NP // 2
HT = T // 2
BANK = 512
GRP = 2
GROUPS = T // GRP
GC = GRP * P
SLOTS = 5
TANH_LEAD = 3
EPS_LN = 1e-5
EPS_GAT = 1e-5
SLOPE = 0.1
KIB = 1024


def build_program(nc, x, src, dst, edge_weight, w1, b1, gate_w, gate_b, bias1, w2, b2, w3, att, out):
    ctx = ExitStack()
    base = -(-nc.sbuf_base // 64) * 64
    limit = nc.sbuf_usable_end
    R_Y = base
    R_W = R_Y + 80 * KIB
    R_C = R_W + 64 * KIB
    R_X = R_C + T * NP * 2
    R_S = R_X + 32 * KIB
    places = [R_S]

    def at(name, shape, dtype, offset):
        return nc.alloc_sbuf_tensor_at(name, shape, dtype, offset=offset)

    def small(name, shape, dtype):
        size = 4 if dtype in (F32, F32R, I32) else 2
        for n in shape[1:]:
            size *= n
        offset = places[0]
        places[0] = -(-(offset + size) // 32) * 32
        assert places[0] <= limit, name
        return at(name, shape, dtype, offset)

    def sem(name):
        return ctx.enter_context(nc.semaphore(name))

    def sems(name, n):
        return [sem(f"{name}{i}") for i in range(n)]

    ps = ctx.enter_context(nc.psum_tensor("ps", [P, 8 * BANK], F32))

    x1_dram = nc.dram_tensor("x_after_0", (NP, D), F32).ap()
    x2_dram = nc.dram_tensor("x_after_1", (NP, D), F32).ap()
    x3_dram = nc.dram_tensor("x_after_2", (NP, D), F32).ap()
    count_dram = nc.dram_tensor("count_rows", (NP, NP), I16).ap()
    wt_dram = nc.dram_tensor("weight_rows", (NP, D), F32).ap()

    xin = [at(f"xin{b}", [P, D], F32, R_X + b * 4 * KIB) for b in range(2)]
    xres = [at(f"xres{b}", [P, D], F32, R_X + (8 + 4 * b) * KIB) for b in range(2)]
    hT_hi = [at(f"hT_hi{b}", [P, KT, P], F32R, R_X + (16 + 8 * b) * KIB) for b in range(2)]
    hT_lo = [at(f"hT_lo{b}", [P, KT, P], F32R, R_X + (20 + 8 * b) * KIB) for b in range(2)]

    w1_raw = at("w1_raw", [P, KT, HID], F32, R_Y + 64 * KIB)
    w1_hi = at("w1_hi", [P, KT, HID], F32R, R_Y + 20 * KIB)
    w1_lo = at("w1_lo", [P, KT, HID], F32R, R_Y + 36 * KIB)
    wt_raw = at("wt_raw", [P, KT, D], F32, R_W + 32 * KIB)
    w2_raw = at("w2_raw", [P, KT, D], F32, R_Y + 48 * KIB)
    w3_raw = at("w3_raw", [P, KT, D], F32, R_W + 32 * KIB)
    w_hi = at("w_hi", [P, KT, D], F32R, R_W)
    w_lo = at("w_lo", [P, KT, D], F32R, R_W + 32 * KIB)

    g = at("g", [P, T, HID], F32, R_Y)
    g_hi = at("g_hi", [P, T, HID], F32R, R_Y + 20 * KIB)
    g_lo = at("g_lo", [P, T, HID], F32R, R_Y + 40 * KIB)
    gw = at("gw", [P, 2 * HID], F32, R_Y + 60 * KIB)
    gate_scratch = at("gate_scratch", [P, HID], F32, R_Y + 64 * KIB)
    diag = [at(f"diag{d}", [P, P], F32, R_Y + 66 * KIB + d * P * 4) for d in range(HT)]
    b1_all = at("b1_all", [P, HID], F32, R_Y + 60 * KIB)
    mask = [at(f"mask{k}", [P, HALF], F32, R_W + 5 * KIB * k) for k in range(SLOTS)]
    mask_lo = [at(f"mask_lo{k}", [P, HALF], F32R, R_W + 5 * KIB * k) for k in range(SLOTS)]
    mask_hi = [at(f"mask_hi{k}", [P, HALF], F32R, R_W + 5 * KIB * k + HALF * 4) for k in range(SLOTS)]

    y_all = at("y_all", [P, T, 2, D], F32R, R_Y)
    y_hi = [y_all[:, s, 0, :] for s in range(T)]
    y_lo = [y_all[:, s, 1, :] for s in range(T)]
    bias1_all = at("bias1_all", [P, D], F32, R_Y)
    b2_all = at("b2_all", [P, D], F32, R_X + 16 * KIB)
    cnt2 = [at(f"cnt2_{k}", [P, GC], F32R, R_X + 20 * KIB + k * GC * 4) for k in range(SLOTS)]
    gcn_work = at("gcn_work", [P, D], F32, R_X + 26 * KIB)
    att_all = at("att_all", [P, 2 * D], F32, R_X + 8 * KIB)
    att_e = [at(f"att_e{s}", [P, GC], F32, R_W + 2 * KIB * s) for s in range(T)]
    att_lo = [at(f"att_lo{s}", [P, GC], F32R, R_W + 2 * KIB * s) for s in range(T)]
    att_hi = [at(f"att_hi{s}", [P, GC], F32R, R_W + 2 * KIB * s + KIB) for s in range(T)]
    al_all = at("al_all", [P, NP], F32, R_W + 24 * KIB)
    elu_neg = [at(f"elu_neg{j}", [P, D], F32, R_X + (16 + 4 * j) * KIB) for j in range(GRP)]

    countT = at("countT", [P, T, NP], I16, R_C)
    count = at("count", [P, T, NP], I16, R_C)

    o = [R_W]

    def build(name, shape, dtype):
        size = 4 if dtype in (F32, I32) else 2
        for n in shape[1:]:
            size *= n
        offset = o[0]
        o[0] += -(-size // 32) * 32
        assert o[0] <= R_C, name
        return at(name, shape, dtype, offset)

    onehot = [[build(f"onehot{r}_{j}", [P, NP], BF16) for j in range(QW)] for r in range(2)]
    sel = [build(f"sel{b}", [P, 4, QW * CHUNKS, WIN], BF16) for b in range(2)]
    iota_f = build("iota_f", [P, NP], F32)
    iota_h = build("iota_h", [P, NP], F16)
    count_f = [build(f"count_f{b}", [P, NP], F32) for b in range(2)]
    count_row = [build(f"count_row{b}", [P, NP], I16) for b in range(2)]
    weight_row = [build(f"weight_row{b}", [P, D], F32) for b in range(2)]
    ends_raw = [build(f"ends_raw{b}", [P, 2, QW * CHUNKS], I32) for b in range(2)]
    ends = [build(f"ends{b}", [P, 2, QW * CHUNKS], F32) for b in range(2)]
    ew = [build(f"ew{b}", [P, QW * CHUNKS], F32) for b in range(2)]
    ew_rest = [build(f"ew_rest{b}", [P, 2, QW * CHUNKS], F32) for b in range(2)]
    ew_part = [build(f"ew_part{b}", [P, 3, QW * CHUNKS], BF16) for b in range(2)]
    dst_raw = at("dst_raw", [P, EC], I32, R_W + 16 * KIB)
    dst_f = at("dst_f", [P, EC], F32, R_W + 17 * KIB)
    below = at("below", [P, WINDOWS, EC], BF16, R_W)

    ident = small("ident", [P, P], F32)
    ones = small("ones", [P, P], F32)
    ones_r = small("ones_r", [P, 2], F32R)
    zeros = small("zeros", [P, P], BF16)
    stats = [small(f"stats{b}", [P, 2, 6], F32) for b in range(2)]
    mv = [small(f"mv{b}", [P, 2], F32) for b in range(2)]
    ln = [small(f"ln{b}", [P, 6], F32) for b in range(2)]
    deg = small("deg", [P, T], F32)
    norm = small("norm", [P, 2, T], F32)
    norm_root = small("norm_root", [P, 2, T], F32)
    norm_step = small("norm_step", [P, 2, T], F32)
    dis = small("dis", [P, 2, T], F32)
    below_n = small("below_n", [P, WINDOWS], F32)
    starts = small("starts", [P, WINDOWS], I32)
    captured = small("captured", [P, 1], F32)
    complete = small("complete", [P, 1], I32)
    gb = small("gb", [P, GATES], F32)
    u = small("u", [P, T], F32)
    v = small("v", [P, T], F32)
    al = small("al", [P, T], F32)
    ar = small("ar", [P, T], F32)
    al_col = [small(f"al_col{b}", [P, 2], F32) for b in range(2)]
    rden = small("rden", [P, GRP, 2], F32)
    gb_col = small("gb_col", [P, 1], F32)
    al_diag = [at(f"al_diag{b}", [P, P], F32, R_W + 32 * KIB + b * P * 4) for b in range(2)]

    consts_landed = sem("consts_landed")
    iota_done = sem("iota_done")
    consts_done = sem("consts_done")

    xin_landed = sems("xin_landed", 2)
    ln_chain = sem("ln_chain")
    var_ready = sem("var_ready")
    root_ready = sem("root_ready")
    scale_ready = sem("scale_ready")
    h_ready = sem("h_ready")
    h_transposed = sems("h_transposed", 2)
    hT_hi_ready = sem("hT_hi_ready")
    hT_lo_ready = sem("hT_lo_ready")
    product_ready = sems("product_ready", 2)
    product_read = sems("product_read", 2)
    w_landed = sems("w_landed", 4)
    w_hi_ready = sem("w_hi_ready")
    w_lo_ready = sem("w_lo_ready")
    res_landed = sems("res_landed", 2)
    res_added = sem("res_added")
    stored = sems("stored", 2)

    class Dense:

        def __init__(self, n):
            self.n = n

        def pairs(self, i):
            return HT * self.n + i

        def tiles(self, t):
            return T * self.n + t

    dense = [Dense(n) for n in range(4)]
    LN_STEPS = 7

    dst_landed = sem("dst_landed")
    below_chain = sem("below_chain")
    below_summed = sem("below_summed")
    starts_ready = sem("starts_ready")
    ends_landed = sems("ends_landed", 2)
    ends_ready = sem("ends_ready")
    sel_ready = sem("sel_ready")
    parts_chain = sem("parts_chain")
    wsel_ready = sem("wsel_ready")
    onehot_ready = sem("onehot_ready")
    onehot_used = sems("onehot_used", 2)
    counts_ready = sem("counts_ready")
    counts_copied = sem("counts_copied")
    weights_copied = sem("weights_copied")
    count_transposed = sems("count_transposed", 2)
    countT_ready = sem("countT_ready")
    count_row_ready = sem("count_row_ready")
    count_stored = sems("count_stored", 2)
    weights_stored = sems("weights_stored", 2)
    captured_ready = sem("captured_ready")
    captured_summed = sem("captured_summed")
    complete_ready = sem("complete_ready")
    gen_landed = sem("gen_landed")
    gen_chain = sem("gen_chain")
    gen_ready = sem("gen_ready")
    gen_used = sem("gen_used")
    gen_summed = sem("gen_summed")
    gen_copied = sem("gen_copied")
    gen_transposed = sem("gen_transposed")
    gen_countT_ready = sem("gen_countT_ready")
    gen_row_ready = sem("gen_row_ready")
    gen_stored = sem("gen_stored")
    built = sem("built")
    norm_chain = sem("norm_chain")
    norm_root_ready = sem("norm_root_ready")
    dis_ready = sem("dis_ready")
    gw_landed = sem("gw_landed")
    gate_chain = sem("gate_chain")
    gates_ready = sem("gates_ready")
    u_spread = sem("u_spread")
    g_hi_ready = sem("g_hi_ready")
    g_lo_ready = sem("g_lo_ready")
    tanh_ready = sem("tanh_ready")
    mask_ready = sem("mask_ready")
    mask_hi_ready = sem("mask_hi_ready")
    mask_lo_ready = sem("mask_lo_ready")
    mask_used = sems("mask_used", SLOTS)
    sum_ready = sem("sum_ready")
    sum_read = sem("sum_read")
    half_landed = sems("half_landed", 2)
    half_added = sem("half_added")
    half_stored = sems("half_stored", 2)
    y_hi_ready = sem("y_hi_ready")
    loops_added = sem("loops_added")
    cnt_ready = sem("cnt_ready")
    cnt_used = sems("cnt_used", SLOTS)
    agg_ready = sem("agg_ready")
    agg_read = sem("agg_read")
    agg_chain = sem("agg_chain")
    agg_landed = sems("agg_landed", 2)
    agg_stored = sems("agg_stored", 2)
    b2_landed = sem("b2_landed")
    bias1_landed = sem("bias1_landed")
    att_landed = sem("att_landed")
    count_landed = sem("count_landed")
    al_chain = sem("al_chain")
    al_ready = sem("al_ready")
    al_diag_ready = sem("al_diag_ready")
    al_diag_used = sem("al_diag_used")
    al_all_ready = sem("al_all_ready")
    logit_ready = sem("logit_ready")
    leaky_ready = sem("leaky_ready")
    exp_ready = sem("exp_ready")
    att_e_ready = sem("att_e_ready")
    att_hi_ready = sem("att_hi_ready")
    att_lo_ready = sem("att_lo_ready")
    att_used = sem("att_used")
    gat_ready = sem("gat_ready")
    gat_read = sem("gat_read")
    den_taken = sem("den_taken")
    elu_added = sem("elu_added")
    gat_pos_ready = sem("gat_pos_ready")
    gat_chain = sem("gat_chain")
    gat_neg_ready = sem("gat_neg_ready")
    gat_exp_ready = sem("gat_exp_ready")
    gat_landed = sems("gat_landed", 2)
    gat_added = sem("gat_added")
    gat_stored = sems("gat_stored", 2)
    al_copied = sem("al_copied")
    gb_chain = sem("gb_chain")

    block = ctx.enter_context(nc.Block())

    NHALF = [1, 2, 2, 2]
    W_RAW = [w1_raw, wt_raw, w2_raw, w3_raw]
    W_HI = [w1_hi, w_hi, w_hi, w_hi]
    W_LO = [w1_lo, w_lo, w_lo, w_lo]
    X_IN = [x, x1_dram, x2_dram, x3_dram]
    TRANSPOSED = ps[:, 0:2 * BANK]
    PRODUCT = [ps[:, (2 + 2 * b) * BANK:(4 + 2 * b) * BANK] for b in range(2)]
    SCRATCH = ps[:, 6 * BANK:8 * BANK]

    def rows(t):
        return bass.ds(t * P, P)

    def split_act(act, d):
        for k in range(KT):
            if k % 2 == 0:
                act.wait_ge(w_landed[k // 2], 16 * (d.n + 1))
            nc.scalar.activation(W_HI[d.n][:, k, :], W_RAW[d.n][:, k, :], ACT.Copy).then_inc(w_hi_ready, 1)

    def split_dve(dve, d):
        for k in range(KT):
            dve.wait_ge(w_hi_ready, KT * d.n + k + 1)
            nc.vector.tensor_tensor(W_LO[d.n][:, k, :], W_RAW[d.n][:, k, :], W_HI[d.n][:, k, :].bitcast(F32),
                                    ALU.subtract).then_inc(w_lo_ready, 1)

    def norm_dve(dve, d, i, b):
        t = 2 * i + b
        ve, root, r0, q, c, scale = (ln[b][:, j:j + 1] for j in range(6))
        dve.wait_ge(xin_landed[b], 16 * d.pairs(i + 1))
        for half in range(2):
            nc.vector.bn_stats(stats[b][:, half, :], xin[b][:, half * 512:(half + 1) * 512]).then_inc(ln_chain, 1)
        settled(dve, ln_chain, LN_STEPS * d.tiles(t) + 2)
        nc.vector.bn_aggr(mv[b][:, :], stats[b][:, :, :].rearrange("p a s -> p (a s)")).then_inc(ln_chain, 1)
        dve.wait_ge(ln_chain, LN_STEPS * d.tiles(t) + 3)
        nc.vector.tensor_scalar(ve, mv[b][:, 1:2], EPS_LN, None, ALU.add).then_inc(var_ready, 1)
        dve.wait_ge(root_ready, d.tiles(t + 1))
        nc.vector.reciprocal(r0, root).then_inc(ln_chain, 1)
        dve.wait_ge(ln_chain, LN_STEPS * d.tiles(t) + 4)
        nc.vector.scalar_tensor_tensor(q, r0, r0, ve, ALU.mult, ALU.mult).then_inc(ln_chain, 1)
        dve.wait_ge(ln_chain, LN_STEPS * d.tiles(t) + 5)
        nc.vector.tensor_scalar(c, q, -0.5, 1.5, ALU.mult, ALU.add).then_inc(ln_chain, 1)
        dve.wait_ge(ln_chain, LN_STEPS * d.tiles(t) + 6)
        nc.vector.tensor_tensor(scale, r0, c, ALU.mult).then_inc(ln_chain, 1)
        dve.wait_ge(ln_chain, LN_STEPS * d.tiles(t) + 7)
        nc.vector.tensor_scalar(q, mv[b][:, 0:1], scale, -1.0, ALU.mult, ALU.mult).then_inc(scale_ready, 1)

    def norm_act(act, d, i, b):
        t = 2 * i + b
        act.wait_ge(var_ready, d.tiles(t + 1))
        nc.scalar.activation(ln[b][:, 1:2], ln[b][:, 0:1], ACT.Sqrt).then_inc(root_ready, 1)
        act.wait_ge(scale_ready, d.tiles(t + 1))
        nc.scalar.activation(xin[b][:, :], xin[b][:, :], ACT.Relu, bias=ln[b][:, 3:4],
                             scale=ln[b][:, 5:6]).then_inc(h_ready, 1)

    def transposed_act(act, d, i, b):
        t = 2 * i + b
        act.wait_ge(h_transposed[b], d.pairs(i + 1))
        nc.scalar.activation(hT_hi[b][:, :, :].rearrange("p k m -> p (k m)"), TRANSPOSED,
                             ACT.Copy).then_inc(hT_hi_ready, 1)

    def transposed_dve(dve, d, i, b):
        t = 2 * i + b
        dve.wait_ge(hT_hi_ready, d.tiles(t + 1))
        nc.vector.tensor_tensor(hT_lo[b][:, :, :].rearrange("p k m -> p (k m)"), TRANSPOSED,
                                hT_hi[b][:, :, :].rearrange("p k m -> p (k m)").bitcast(F32),
                                ALU.subtract).then_inc(hT_lo_ready, 1)

    def transpose_pe(pe, d, i, b):
        t = 2 * i + b
        pe.wait_ge(h_ready, d.tiles(t + 1))
        pe.wait_ge(hT_lo_ready, d.tiles(t))
        for k in range(KT):
            last = nc.tensor.transpose(TRANSPOSED[:, k * P:(k + 1) * P], xin[b][:, k * P:(k + 1) * P], ident[:, :])
        last.then_inc(h_transposed[b], 1)

    def product_pe(pe, d, i, b, first, transpose_next):
        t = 2 * i + b
        hi, lo = W_HI[d.n], W_LO[d.n]
        pe.wait_ge(hT_lo_ready, d.tiles(t + 1))
        pe.wait_ge(product_read[b], d.pairs(i))
        for k in range(KT):
            if k == KT // 2 and transpose_next is not None:
                transpose_next()
            if first:
                pe.wait_ge(w_lo_ready, KT * d.n + k + 1)
            for left, rights in ((hT_hi[b], (hi, lo)), (hT_lo[b], (hi,))):
                for half in range(NHALF[d.n]):
                    for right in rights:
                        last = nc.tensor.matmul(PRODUCT[b][:, half * BANK:(half + 1) * BANK], left[:, k, :],
                                                right[:, k, half * BANK:(half + 1) * BANK],
                                                start=(k == 0 and left is hT_hi[b] and right is hi),
                                                stop=(k == KT - 1 and left is hT_lo[b]))
        last.then_inc(product_ready[b], 1)

    def dense_pe(pe, d):
        transpose_pe(pe, d, 0, 0)
        product_pe(pe, d, 0, 0, True, lambda: transpose_pe(pe, d, 0, 1))
        product_pe(pe, d, 0, 1, False, lambda: transpose_pe(pe, d, 1, 0))
        with pe.Fori(1, HT - 1) as i:
            product_pe(pe, d, i, 0, False, lambda: transpose_pe(pe, d, i, 1))
            product_pe(pe, d, i, 1, False, lambda: transpose_pe(pe, d, i + 1, 0))
        product_pe(pe, d, HT - 1, 0, False, lambda: transpose_pe(pe, d, HT - 1, 1))
        product_pe(pe, d, HT - 1, 1, False, None)

    def dense_dve(dve, d, finish):
        norm_dve(dve, d, 0, 0)
        split_dve(dve, d) if d.n != 3 else None
        transposed_dve(dve, d, 0, 0)
        norm_dve(dve, d, 0, 1)
        with dve.Fori(0, HT - 1) as i:
            transposed_dve(dve, d, i, 1)
            norm_dve(dve, d, i + 1, 0)
            finish(i, 0)
            transposed_dve(dve, d, i + 1, 0)
            norm_dve(dve, d, i + 1, 1)
            finish(i, 1)
        transposed_dve(dve, d, HT - 1, 1)
        finish(HT - 1, 0)
        finish(HT - 1, 1)

    def dense_act(act, d, finish):
        norm_act(act, d, 0, 0)
        split_act(act, d) if d.n != 3 else None
        transposed_act(act, d, 0, 0)
        norm_act(act, d, 0, 1)
        with act.Fori(0, HT - 1) as i:
            transposed_act(act, d, i, 1)
            norm_act(act, d, i + 1, 0)
            finish(i, 0)
            transposed_act(act, d, i + 1, 0)
            norm_act(act, d, i + 1, 1)
            finish(i, 1)
        transposed_act(act, d, HT - 1, 1)
        finish(HT - 1, 0)
        finish(HT - 1, 1)

    def load_weights(eng, d, dram):
        for q in range(4):
            eng.dma_start(W_RAW[d.n][:, 2 * q:2 * q + 2, :],
                          dram[2 * q * P:(2 * q + 2) * P, :].rearrange("(k p) n -> p k n", p=P)
                          ).then_inc(w_landed[q], 16)

    settles = sem("settles")

    def settled(eng, semaphore, value):
        eng.wait_ge(semaphore, value)
        eng.sem_inc(settles, 1)

    @block.sync
    def _(sp):
        sp.dma_start(dst_raw[0:EP, :], dst.rearrange("(p c) -> p c", c=EC)).then_inc(dst_landed, 16)
        d = dense[0]
        sp.dma_start(b1_all[:, :], b1.partition_broadcast(P)).then_inc(consts_landed, 16)
        sp.dma_start(gb[:, :], gate_b.rearrange("k a -> (k a)").partition_broadcast(P)).then_inc(consts_landed, 16)
        sp.dma_start(xin[0][:, :], x[0:P, :]).then_inc(xin_landed[0], 16)
        load_weights(sp, d, w1)
        sp.dma_start(xin[1][:, :], x[P:2 * P, :]).then_inc(xin_landed[1], 16)
        with sp.Fori(1, HT - 1) as i:
            for b in range(2):
                settled(sp, h_transposed[b], d.pairs(i))
                sp.dma_start(xin[b][:, :], x[rows(2 * i + b), :]).then_inc(xin_landed[b], 16)
        sp.wait_ge(h_transposed[0], d.pairs(HT - 1))
        sp.dma_start(xin[0][:, :], x[(T - 2) * P:(T - 1) * P, :]).then_inc(xin_landed[0], 16)
        sp.wait_ge(h_transposed[1], d.pairs(HT - 1))
        sp.dma_start(xin[1][0:N - (T - 1) * P, :], x[(T - 1) * P:N, :]).then_inc(xin_landed[1], 16)

        sp.wait_ge(starts_ready, 1)
        def load_edges(i, b):
            for j in range(QW):
                start = sp.value_load(starts[0:1, bass.ds(QW * (2 * i + b) + j, 1)], min_val=0, max_val=E - CAP)
                cols = slice(j * CHUNKS, (j + 1) * CHUNKS)
                for to, of in ((ends_raw[b][:, 0, cols], src), (ends_raw[b][:, 1, cols], dst), (ew[b][:, cols], edge_weight)):
                    sp.dma_start(to, of[bass.ds(start, CAP)].rearrange("(p c) -> p c", c=CHUNKS)).then_inc(ends_landed[b], 16)

        load_edges(0, 0)
        load_edges(0, 1)
        with sp.Fori(1, HT) as i:
            for b in range(2):
                settled(sp, ends_ready, 2 * i + b - 1)
                settled(sp, wsel_ready, 2 * i + b - 1)
                load_edges(i, b)

        sp.wait_ge(complete_ready, 1)
        whole = sp.value_load(complete[0:1, 0:1], min_val=0, max_val=1)
        with sp.If(whole == 0):
            sp.sem_inc(gen_stored, 1)
            with sp.Fori(0, T) as a:
                with sp.Fori(0, GENERAL_CHUNKS) as c:
                    settled(sp, gen_used, a * GENERAL_CHUNKS + c + 1)
                    for to, of in ((ends_raw[0][0:EP, 0, 0:CHUNKS], src), (ends_raw[0][0:EP, 1, 0:CHUNKS], dst),
                                   (ew[0][0:EP, 0:CHUNKS], edge_weight)):
                        sp.dma_start(to, of[bass.ds(c * (EP * CHUNKS), EP * CHUNKS)].rearrange("(p c) -> p c", c=CHUNKS)
                                     ).then_inc(gen_landed, 16)
                settled(sp, gen_row_ready, a + 1)
                sp.dma_start(count_dram[rows(a), :], count_row[0][:, :]).then_inc(gen_stored, 16)
                sp.dma_start(wt_dram[rows(a), :], weight_row[0][:, :]).then_inc(gen_stored, 16)
                settled(sp, gen_stored, 32 * (a + 1) + 1)
        for b in range(2):
            sp.wait_ge(weights_stored[b], 16 * WT_TILES // 2)
            sp.wait_ge(count_stored[b], 16 * HT)
        sp.wait_ge(built, 3)
        load_weights(sp, dense[1], wt_dram)
        sp.dma_start(gw[:, :], gate_w[0].rearrange("c a -> (c a)").partition_broadcast(P)).then_inc(gw_landed, 16)
        with sp.Fori(0, GATES - 1) as r:
            settled(sp, gates_ready, T * (r + 1))
            sp.dma_start(gw[:, :], gate_w[bass.ds(r + 1, 1)].rearrange("k c a -> (k c a)").partition_broadcast(P)
                         ).then_inc(gw_landed, 16)

        d = dense[1]
        sp.wait_ge(mask_used[SLOTS - 1], 4 * GATES)
        sp.wait_ge(sum_read, T * GATES)
        load_weights(sp, dense[2], w2)
        sp.wait_ge(half_added, T)
        sp.dma_start(bias1_all[:, :], bias1.partition_broadcast(P)).then_inc(bias1_landed, 16)
        with sp.Fori(0, HT) as i:
            for b in range(2):
                settled(sp, half_stored[b], 16 * (i + 1))
                settled(sp, h_transposed[b], d.pairs(i))
                sp.dma_start(xin[b][:, :], x1_dram[rows(2 * i + b), :]).then_inc(xin_landed[b], 16)
        d = dense[2]
        with sp.Fori(0, HT) as i:
            for b in range(2):
                settled(sp, stored[b], 16 * dense[1].pairs(i + 1))
                settled(sp, h_transposed[b], d.pairs(i))
                sp.dma_start(xin[b][:, :], x2_dram[rows(2 * i + b), :]).then_inc(xin_landed[b], 16)
        for b in range(2):
            sp.wait_ge(product_ready[b], d.pairs(HT))
        sp.dma_start(b2_all[:, :], b2.partition_broadcast(P)).then_inc(b2_landed, 16)
        load_weights(sp, dense[3], w3)
        d = dense[3]
        with sp.Fori(0, HT) as i:
            for b in range(2):
                settled(sp, agg_stored[b], 16 * (i + 1))
                settled(sp, h_transposed[b], d.pairs(i))
                sp.dma_start(xin[b][:, :], x3_dram[rows(2 * i + b), :]).then_inc(xin_landed[b], 16)
        sp.wait_ge(cnt_ready, T * GROUPS)
        sp.dma_start(count[:, :, :], count_dram.rearrange("(t p) s -> p t s", p=P)).then_inc(count_landed, 16)

    @block.gpsimd
    def _(pool):
        nc.gpsimd.iota(iota_f[:, :], [[1, NP]], base=0, channel_multiplier=0,
                       allow_small_or_imprecise_dtypes=True).then_inc(iota_done, 1)
        nc.gpsimd.memset(ones[:, :], 1.0).then_inc(consts_done, 1)
        nc.gpsimd.memset(zeros[:, :], 0.0).then_inc(consts_done, 1)
        pool.wait_ge(consts_done, 1)
        nc.gpsimd.affine_select(out=ident[:, :], in_=ones[:, :], pattern=[[-1, P]], compare_op=ALU.is_equal, fill=0.0,
                                base=0, channel_multiplier=1).then_inc(consts_done, 1)

        d = dense[0]

        def first_half(i, b, n):
            if not isinstance(i, int) or i > 0:
                settled(pool, stored[b], 16 * d.pairs(i))
            pool.dma_start(xres[b][0:n, 0:HID], x[bass.ds((2 * i + b) * P, n), 0:HID]).then_inc(res_landed[b], 16)
            settled(pool, res_landed[b], 16 * d.pairs(i + 1))
            settled(pool, product_read[b], d.pairs(i + 1))
            nc.gpsimd.tensor_tensor(xres[b][:, 0:HID], xres[b][:, 0:HID], g[:, bass.ds(2 * i + b, 1), :].rearrange("p a n -> p (a n)"),
                                    ALU.add).then_inc(res_added, 1)
            settled(pool, res_added, d.tiles(2 * i + b + 1))
            pool.dma_start(x1_dram[rows(2 * i + b), 0:HID], xres[b][:, 0:HID]).then_inc(stored[b], 16)

        first_half(0, 0, P)
        first_half(0, 1, P)
        with pool.Fori(1, HT - 1) as i:
            first_half(i, 0, P)
            first_half(i, 1, P)
        first_half(HT - 1, 0, P)
        first_half(HT - 1, 1, N - (T - 1) * P)

        PARTS = 5

        def weight_parts(i, b):
            a = 2 * i + b
            settled(pool, ends_landed[b], 16 * 3 * QW * (i + 1))
            settled(pool, sel_ready, a + 1)
            whole, rest, part = ew[b], ew_rest[b], ew_part[b]
            nc.gpsimd.tensor_copy(part[:, 0, :], whole[:, :]).then_inc(parts_chain, 1)
            settled(pool, parts_chain, PARTS * a + 1)
            nc.gpsimd.tensor_tensor(rest[:, 0, :], whole[:, :], part[:, 0, :], ALU.subtract).then_inc(parts_chain, 1)
            settled(pool, parts_chain, PARTS * a + 2)
            nc.gpsimd.tensor_copy(part[:, 1, :], rest[:, 0, :]).then_inc(parts_chain, 1)
            settled(pool, parts_chain, PARTS * a + 3)
            nc.gpsimd.tensor_tensor(rest[:, 1, :], rest[:, 0, :], part[:, 1, :], ALU.subtract).then_inc(parts_chain, 1)
            settled(pool, parts_chain, PARTS * a + 4)
            nc.gpsimd.tensor_copy(part[:, 2, :], rest[:, 1, :]).then_inc(parts_chain, 1)
            settled(pool, parts_chain, PARTS * a + 5)
            for k in range(3):
                last = nc.gpsimd.tensor_tensor(sel[b][:, 1 + k, :, :], sel[b][:, 0, :, :],
                                               part[:, k, :].unsqueeze(2).to_broadcast([P, QW * CHUNKS, WIN]), ALU.mult)
            last.then_inc(wsel_ready, 1)

        def store_rows(i, b, weights):
            a = 2 * i + b
            settled(pool, counts_copied, a + 1)
            if not isinstance(i, int) or i > 0:
                settled(pool, count_stored[b], 16 * i)
            nc.gpsimd.tensor_copy(count_row[b][:, :], count_f[b][:, :]).then_inc(count_row_ready, 1)
            settled(pool, count_row_ready, a + 1)
            pool.dma_start(count_dram[rows(a), :], count_row[b][:, :]).then_inc(count_stored[b], 16)
            if weights:
                settled(pool, weights_copied, a + 1)
                pool.dma_start(wt_dram[rows(a), :], weight_row[b][:, :]).then_inc(weights_stored[b], 16)

        weight_parts(0, 0)
        weight_parts(0, 1)
        store_rows(0, 0, True)
        weight_parts(1, 0)
        store_rows(0, 1, True)
        with pool.Fori(1, WT_TILES // 2) as i:
            weight_parts(i, 1)
            store_rows(i, 0, True)
            weight_parts(i + 1, 0)
            store_rows(i, 1, True)
        weight_parts(HT - 1, 1)
        store_rows(HT - 1, 0, False)
        store_rows(HT - 1, 1, False)

        pool.wait_ge(complete_ready, 1)
        whole = pool.value_load(complete[0:1, 0:1], min_val=0, max_val=1)
        with pool.If(whole == 0):
            for b in range(2):
                pool.wait_ge(count_stored[b], 16 * HT)
            with pool.Fori(0, T) as a:
                settled(pool, gen_copied, 2 * (a + 1) + 1)
                nc.gpsimd.tensor_copy(count_row[0][:, :], count_f[0][:, :]).then_inc(gen_row_ready, 1)
        pool.sem_inc(built, 1)

        def second_half(i, b, n):
            t = 2 * i + b
            if not isinstance(i, int) or i > 0:
                settled(pool, half_stored[b], 16 * i)
            pool.dma_start(xres[b][0:n, 0:HID], x[bass.ds(t * P, n), HID:D]).then_inc(half_landed[b], 16)
            settled(pool, half_landed[b], 16 * (i + 1))
            settled(pool, sum_read, T * (GATES - 1) + t + 1)
            nc.gpsimd.tensor_tensor(xres[b][:, 0:HID], xres[b][:, 0:HID], g[:, bass.ds(t, 1), :].rearrange("p a n -> p (a n)"),
                                    ALU.add).then_inc(half_added, 1)
            settled(pool, half_added, t + 1)
            pool.dma_start(x1_dram[rows(t), HID:D], xres[b][:, 0:HID]).then_inc(half_stored[b], 16)

        for b in range(2):
            pool.wait_ge(stored[b], 16 * d.pairs(HT))
        second_half(0, 0, P)
        second_half(0, 1, P)
        with pool.Fori(1, HT - 1) as i:
            second_half(i, 0, P)
            second_half(i, 1, P)
        second_half(HT - 1, 0, P)
        second_half(HT - 1, 1, N - (T - 1) * P)

        d = dense[1]

        def load1(i, b):
            pool.dma_start(xres[b][:, :], x1_dram[rows(2 * i + b), :]).then_inc(res_landed[b], 16)

        def store1(i, b):
            t = 2 * i + b
            settled(pool, product_read[b], d.pairs(i + 1))
            nc.gpsimd.tensor_tensor(xres[b][:, :], xres[b][:, :], bias1_all[:, :], ALU.add).then_inc(res_added, 1)
            settled(pool, res_added, d.tiles(t + 1))
            pool.dma_start(x2_dram[rows(t), :], xres[b][:, :]).then_inc(stored[b], 16)
            settled(pool, stored[b], 16 * d.pairs(i + 1))

        pool.wait_ge(bias1_landed, 16)
        for b in range(2):
            pool.wait_ge(half_stored[b], 16 * HT)
            load1(0, b)
        with pool.Fori(0, HT - 1) as i:
            for b in range(2):
                store1(i, b)
                load1(i + 1, b)
        store1(HT - 1, 0)
        store1(HT - 1, 1)

        def load2(i, b):
            pool.dma_start(xres[b][:, :], x2_dram[rows(2 * i + b), :]).then_inc(agg_landed[b], 16)

        def store2(i, b):
            settled(pool, agg_read, 2 * i + b + 1)
            pool.dma_start(x3_dram[rows(2 * i + b), :], xres[b][:, :]).then_inc(agg_stored[b], 16)
            settled(pool, agg_stored[b], 16 * (i + 1))

        load2(0, 0)
        load2(0, 1)
        with pool.Fori(0, HT - 1) as i:
            for b in range(2):
                store2(i, b)
                load2(i + 1, b)
        store2(HT - 1, 0)
        store2(HT - 1, 1)

        pool.dma_start(att_all[:, :], att.rearrange("a n -> (a n)").partition_broadcast(P)).then_inc(att_landed, 16)
        pool.wait_ge(al_ready, T)

        def load3(i, b):
            pool.dma_start(xres[b][:, :], x3_dram[rows(2 * i + b), :]).then_inc(gat_landed[b], 16)

        def store3(i, b, n):
            settled(pool, gat_added, 2 * i + b + 1)
            pool.dma_start(out[bass.ds((2 * i + b) * P, n), :], xres[b][0:n, :]).then_inc(gat_stored[b], 16)
            settled(pool, gat_stored[b], 16 * (i + 1))

        load3(0, 0)
        load3(0, 1)
        with pool.Fori(0, HT - 1) as i:
            for b in range(2):
                store3(i, b, P)
                load3(i + 1, b)
        store3(HT - 1, 0, P)
        store3(HT - 1, 1, N - (T - 1) * P)

    COUNTS = ps[:, 0:NP]
    WEIGHTS = ps[:, 3 * BANK:3 * BANK + D]
    COUNT_T = ps[:, 5 * BANK:5 * BANK + NP]
    BLOCKS = [(0, BANK), (BANK, 2 * BANK), (2 * BANK, NP)]
    SUMS = [ps[:, k * BANK:(k + 1) * BANK] for k in range(HT)]
    U_ALL = ps[:, HT * BANK:HT * BANK + HALF]
    AGG = [ps[:, 2 * j * BANK:(2 * j + 2) * BANK] for j in range(GRP)]
    DEN = [ps[:, (4 + j) * BANK:(4 + j) * BANK + 2] for j in range(GRP)]
    AL_ALL = ps[:, 5 * BANK:5 * BANK + NP]

    def use_of(m):
        return m % 2, m // 2

    @block.scalar
    def _(act):
        dense_act(act, dense[0], lambda i, b: None)

        def take_rows(i, b, weights):
            a = 2 * i + b
            ring, use = use_of(CHUNKS * b + CHUNKS - 1)
            act.wait_ge(count_transposed[b], i)
            act.wait_ge(count_row_ready, 2 * i)
            if weights:
                act.wait_ge(counts_ready, a + 1)
            else:
                act.wait_ge(onehot_used[ring], CHUNKS * i + use + 1)
            nc.scalar.activation(count_f[b][:, :], COUNTS, ACT.Copy,
                                 accum_out=deg[:, bass.ds(a, 1)]).then_inc(counts_copied, 1)
            if weights:
                act.wait_ge(onehot_used[ring], CHUNKS * i + use + 1)
                act.wait_ge(weights_stored[b], 16 * i)
                nc.scalar.activation(weight_row[b][:, :], WEIGHTS, ACT.Copy).then_inc(weights_copied, 1)
            act.wait_ge(count_transposed[b], i + 1)
            nc.scalar.activation(countT[:, :, bass.ds(a * P, P)], COUNT_T.rearrange("p (s n) -> p s n", n=P),
                                 ACT.Copy).then_inc(countT_ready, 1)

        take_rows(0, 0, True)
        take_rows(0, 1, True)
        with act.Fori(1, WT_TILES // 2) as i:
            take_rows(i, 0, True)
            take_rows(i, 1, True)
        take_rows(HT - 1, 0, False)
        take_rows(HT - 1, 1, False)

        act.wait_ge(complete_ready, 1)
        whole = act.value_load(complete[0:1, 0:1], min_val=0, max_val=1)
        with act.If(whole == 0):
            act.wait_ge(count_row_ready, T)
            for b in range(2):
                act.wait_ge(weights_stored[b], 16 * WT_TILES // 2)
            act.sem_inc(gen_copied, 1)
            act.sem_inc(gen_countT_ready, 1)
            with act.Fori(0, T) as a:
                act.wait_ge(gen_summed, a + 1)
                act.wait_ge(gen_stored, 32 * a + 1)
                nc.scalar.activation(count_f[0][:, :], COUNTS, ACT.Copy,
                                     accum_out=deg[:, bass.ds(a, 1)]).then_inc(gen_copied, 1)
                nc.scalar.activation(weight_row[0][:, :], WEIGHTS, ACT.Copy).then_inc(gen_copied, 1)
                act.wait_ge(gen_transposed, a + 1)
                nc.scalar.activation(countT[:, :, bass.ds(a * P, P)], COUNT_T.rearrange("p (s n) -> p s n", n=P),
                                     ACT.Copy).then_inc(gen_countT_ready, 1)
            act.wait_ge(gen_countT_ready, T + 1)
        act.sem_inc(built, 1)

        act.wait_ge(norm_chain, 2)
        nc.scalar.activation(norm_root[:, :, :], norm[:, :, :], ACT.Sqrt).then_inc(norm_root_ready, 1)

        def g_split(t, count):
            nc.scalar.activation(g_hi[:, t, :], g[:, t, :], ACT.Identity,
                                 scale=dis[:, 0, t:t + 1]).then_inc(g_hi_ready, 1)

        def tanh(q, r, h, s):
            k = s % SLOTS
            act.wait_ge(mask_used[k], 2 * q + s // SLOTS)
            if s == 0:
                act.wait_ge(u_spread, q + 1)
            if h == 0:
                act.wait_ge(gates_ready, T * r + s + 1)
            nc.scalar.activation(mask[k][:, :], U_ALL, ACT.Tanh, bias=v[:, s:s + 1]).then_inc(tanh_ready, 1)

        def mask_hi_of(q, s):
            k = s % SLOTS
            act.wait_ge(mask_ready, T * q + s + 1)
            nc.scalar.activation(mask_hi[k][:, :], mask[k][:, :], ACT.Copy).then_inc(mask_hi_ready, 1)

        def half_act(q, r, h, split, last=False):
            for s in range(T):
                if s < T - 1:
                    mask_hi_of(q, s + 1)
                elif not last:
                    mask_hi_of(q + 1, 0)
                if s < T - TANH_LEAD:
                    tanh(q, r, h, s + TANH_LEAD)
                elif not last:
                    tanh(q + 1, r + h, 1 - h, s + TANH_LEAD - T)
                if not split:
                    continue
                if h == 1 and s >= HT:
                    t = s - HT
                    act.wait_ge(sum_read, HT * q - HT + t + 1)
                    act.wait_ge(mask_used[t % SLOTS], 2 * q + 1)
                    g_split(t, None)
                if h == 0 and 1 <= s < 1 + HT:
                    act.wait_ge(sum_read, HT * q - HT + s)
                    g_split(s - 1 + HT, None)

        act.wait_ge(dis_ready, 1)
        for b in range(2):
            act.wait_ge(product_ready[b], dense[0].pairs(HT))
            act.wait_ge(product_read[b], dense[0].pairs(HT))
        for t in range(T):
            g_split(t, None)
        for s in range(TANH_LEAD):
            tanh(0, 0, 0, s)
        mask_hi_of(0, 0)
        half_act(0, 0, 0, False)
        with act.Fori(0, GATES - 1) as r:
            half_act(2 * r + 1, r, 1, True)
            half_act(2 * r + 2, r + 1, 0, True)
        half_act(2 * GATES - 1, GATES - 1, 1, False, last=True)

        act.wait_ge(mask_used[SLOTS - 1], 4 * GATES)
        dense_act(act, dense[1], lambda i, b: None)

        def y_act(d, i, b):
            t = 2 * i + b
            act.wait_ge(product_ready[b], d.pairs(i + 1))
            if d.n == 2:
                nc.scalar.activation(y_all[:, bass.ds(t, 1), 0, :].rearrange("p a n -> p (a n)"), PRODUCT[b], ACT.Identity,
                                     scale=dis[:, 1, bass.ds(t, 1)]).then_inc(y_hi_ready, 1)
            else:
                nc.scalar.activation(y_all[:, bass.ds(t, 1), 0, :].rearrange("p a n -> p (a n)"), PRODUCT[b],
                                     ACT.Copy).then_inc(y_hi_ready, 1)

        for b in range(2):
            act.wait_ge(product_ready[b], dense[1].pairs(HT))
        act.wait_ge(res_added, dense[1].tiles(T))
        dense_act(act, dense[2], lambda i, b: y_act(dense[2], i, b))

        def counts_act(grp):
            for s in range(T):
                act.wait_ge(cnt_used[s % SLOTS], 2 * grp + s // SLOTS)
                nc.scalar.activation(cnt2[s % SLOTS][:, :], countT[:, s, bass.ds(grp * GC, GC)],
                                     ACT.Copy).then_inc(cnt_ready, 1)

        for b in range(2):
            act.wait_ge(product_ready[b], dense[2].pairs(HT))
        act.wait_ge(loops_added, T)
        counts_act(0)
        counts_act(1)
        split_act(act, dense[3])
        with act.Fori(2, GROUPS) as grp:
            counts_act(grp)

        act.wait_ge(agg_read, T)
        dense_act(act, dense[3], lambda i, b: y_act(dense[3], i, b))
        act.wait_ge(al_diag_used, T)
        for b in range(2):
            act.wait_ge(product_ready[b], dense[3].pairs(HT))
        nc.scalar.activation(al_all[:, :], AL_ALL, ACT.Copy).then_inc(al_all_ready, 1)

        def exps(grp, s):
            act.wait_ge(leaky_ready, T * grp + s + 1)
            nc.scalar.activation(att_e[s][:, :], att_e[s][:, :], ACT.Exp, scale=-1.0).then_inc(exp_ready, 1)

        def att_hi_of(grp, s):
            act.wait_ge(att_e_ready, T * grp + s + 1)
            nc.scalar.activation(att_hi[s][:, :], att_e[s][:, :], ACT.Copy).then_inc(att_hi_ready, 1)

        def gat_take(grp, j):
            if j == 0:
                act.wait_ge(gat_ready, grp + 1)
            else:
                act.wait_ge(att_used, T * grp + T)
            nc.scalar.activation(rden[:, j, 0:1], DEN[j][:, 0:1], ACT.Copy).then_inc(den_taken, 1)
            nc.scalar.activation(xin[j][:, :], AGG[j], ACT.Copy).then_inc(gat_read, 1)

        def elu_act(grp, j):
            act.wait_ge(gat_neg_ready, GRP * grp + j + 1)
            nc.scalar.activation(elu_neg[j][:, :], elu_neg[j][:, :], ACT.Exp).then_inc(gat_exp_ready, 1)
            nc.scalar.activation(xin[j][:, :], xin[j][:, :], ACT.Relu, scale=rden[:, j, 1:2]).then_inc(gat_pos_ready, 1)

        def attention_act(grp, first, last):
            for s in range(T):
                if s < T - 1:
                    exps(grp, s + 1)
                elif not last:
                    exps(grp + 1, 0)
                att_hi_of(grp, s)
                if not first and s == 2:
                    gat_take(grp - 1, 0)
                    gat_take(grp - 1, 1)
                if not first and s in (5, 6):
                    elu_act(grp - 1, s - 5)

        exps(0, 0)
        attention_act(0, True, False)
        with act.Fori(1, GROUPS - 1) as grp:
            attention_act(grp, False, False)
        attention_act(GROUPS - 1, False, True)
        for j in range(GRP):
            gat_take(GROUPS - 1, j)
        for j in range(GRP):
            elu_act(GROUPS - 1, j)

    @block.vector
    def _(dve):
        dve.wait_ge(iota_done, 1)
        dve.wait_ge(dst_landed, 16)
        nc.vector.tensor_copy(dst_f[0:EP, :], dst_raw[0:EP, :]).then_inc(below_chain, 1)
        dve.wait_ge(below_chain, 1)
        nc.vector.tensor_tensor(below[0:EP, :, :], dst_f[0:EP, :].unsqueeze(1).to_broadcast([EP, WINDOWS, EC]),
                                iota_f[0:EP, :].rearrange("p (w i) -> p w i", i=WIN)[:, :, 0:1].to_broadcast([EP, WINDOWS, EC]),
                                ALU.is_lt).then_inc(below_chain, 1)
        dve.wait_ge(below_chain, 2)
        nc.vector.tensor_reduce(below_n[0:EP, :], below[0:EP, :, :], AX_X, ALU.add).then_inc(below_chain, 1)
        dve.wait_ge(below_summed, 1)
        nc.vector.tensor_scalar(starts[0:1, :], ps[0:1, 7 * BANK:7 * BANK + WINDOWS], float(E - CAP), None,
                                ALU.min).then_inc(starts_ready, 1)
        nc.vector.tensor_copy(iota_h[:, :], iota_f[:, :]).then_inc(below_chain, 1)
        dve.wait_ge(consts_done, 3)
        nc.vector.tensor_copy(ones_r[:, :], ones[:, 0:2]).then_inc(below_chain, 1)

        d0 = dense[0]

        def x1(i, b):
            dve.wait_ge(product_ready[b], d0.pairs(i + 1))
            nc.vector.tensor_tensor(g[:, bass.ds(2 * i + b, 1), :].rearrange("p a n -> p (a n)"), PRODUCT[b][:, 0:HID],
                                    b1_all[:, :], ALU.add).then_inc(product_read[b], 1)

        dve.wait_ge(consts_landed, 32)
        dense_dve(dve, d0, x1)

        def select(i, b):
            a = 2 * i + b
            ring, use = use_of(CHUNKS * b + CHUNKS - 1)
            dve.wait_ge(ends_landed[b], 16 * 3 * QW * (i + 1))
            if b == 0:
                dve.wait_ge(onehot_used[0], CHUNKS * i)
            else:
                dve.wait_ge(onehot_used[1], CHUNKS * i)
            nc.vector.tensor_copy(ends[b][:, :, :], ends_raw[b][:, :, :]).then_inc(ends_ready, 1)
            dve.wait_ge(ends_ready, a + 1)
            nc.vector.tensor_tensor(
                sel[b][:, 0, :, :].rearrange("p (j c) i -> p j c i", c=CHUNKS),
                ends[b][:, 1, :].rearrange("p (j c) -> p j c", c=CHUNKS).unsqueeze(3).to_broadcast([P, QW, CHUNKS, WIN]),
                iota_f[:, bass.ds(a * P, P)].rearrange("p (j i) -> p j i", i=WIN).unsqueeze(2).to_broadcast([P, QW, CHUNKS, WIN]),
                ALU.is_equal).then_inc(sel_ready, 1)
            for c in range(CHUNKS):
                r, n = use_of(CHUNKS * b + c)
                dve.wait_ge(onehot_used[r], CHUNKS * i + n)
                for j in range(QW):
                    last = nc.vector.tensor_scalar(onehot[r][j][:, :], iota_h[:, :], ends[b][:, 0, j * CHUNKS + c:j * CHUNKS + c + 1],
                                                   None, ALU.is_equal)
                last.then_inc(onehot_ready, 1)

        dve.wait_ge(below_chain, 5)
        select(0, 0)
        select(0, 1)
        with dve.Fori(1, HT) as i:
            select(i, 0)
            select(i, 1)

        dve.wait_ge(counts_copied, T)
        nc.vector.reduce_sum(captured[:, :], deg[:, :], AX_X).then_inc(captured_ready, 1)
        dve.wait_ge(captured_summed, 1)
        nc.vector.tensor_scalar(complete[:, :], ps[:, 0:1], float(E), None, ALU.is_equal).then_inc(complete_ready, 1)
        dve.wait_ge(complete_ready, 1)
        whole = dve.value_load(complete[0:1, 0:1], min_val=0, max_val=1)
        with dve.If(whole == 0):
            dsel = sel[0][:, :, :, :].rearrange("p k a i -> p k (a i)").rearrange("p k (c m) -> p k c m", m=P)
            STEPS = 8
            with dve.Fori(0, T) as a:
                with dve.Fori(0, GENERAL_CHUNKS) as c:
                    n = a * GENERAL_CHUNKS + c
                    dve.wait_ge(gen_landed, 48 * (n + 1))
                    dve.wait_ge(gen_used, n + 1)
                    nc.vector.tensor_copy(ends[0][0:EP, :, 0:CHUNKS], ends_raw[0][0:EP, :, 0:CHUNKS]).then_inc(gen_chain, 1)
                    nc.vector.tensor_copy(ew_part[0][0:EP, 0, 0:CHUNKS], ew[0][0:EP, 0:CHUNKS]).then_inc(gen_chain, 1)
                    dve.wait_ge(gen_chain, STEPS * n + 2)
                    nc.vector.tensor_tensor(ew_rest[0][0:EP, 0, 0:CHUNKS], ew[0][0:EP, 0:CHUNKS], ew_part[0][0:EP, 0, 0:CHUNKS],
                                            ALU.subtract).then_inc(gen_chain, 1)
                    dve.wait_ge(gen_chain, STEPS * n + 3)
                    nc.vector.tensor_copy(ew_part[0][0:EP, 1, 0:CHUNKS], ew_rest[0][0:EP, 0, 0:CHUNKS]).then_inc(gen_chain, 1)
                    dve.wait_ge(gen_chain, STEPS * n + 4)
                    nc.vector.tensor_tensor(ew_rest[0][0:EP, 1, 0:CHUNKS], ew_rest[0][0:EP, 0, 0:CHUNKS], ew_part[0][0:EP, 1, 0:CHUNKS],
                                            ALU.subtract).then_inc(gen_chain, 1)
                    dve.wait_ge(gen_chain, STEPS * n + 5)
                    nc.vector.tensor_copy(ew_part[0][0:EP, 2, 0:CHUNKS], ew_rest[0][0:EP, 1, 0:CHUNKS]).then_inc(gen_chain, 1)
                    nc.vector.tensor_tensor(
                        dsel[0:EP, 0], ends[0][0:EP, 1, 0:CHUNKS].unsqueeze(2).to_broadcast([EP, CHUNKS, P]),
                        iota_f[0:EP, bass.ds(a * P, P)].unsqueeze(1).to_broadcast([EP, CHUNKS, P]),
                        ALU.is_equal).then_inc(gen_chain, 1)
                    dve.wait_ge(gen_chain, STEPS * n + 7)
                    for k in range(3):
                        last = nc.vector.tensor_tensor(dsel[0:EP, 1 + k], dsel[0:EP, 0],
                                                       ew_part[0][0:EP, k, 0:CHUNKS].unsqueeze(2).to_broadcast([EP, CHUNKS, P]),
                                                       ALU.mult)
                    last.then_inc(gen_chain, 1)
                    for q in range(CHUNKS):
                        last = nc.vector.tensor_scalar(onehot[q // QW][q % QW][0:EP, :], iota_h[0:EP, :], ends[0][0:EP, 0, q:q + 1],
                                                       None, ALU.is_equal)
                    last.then_inc(gen_ready, 1)
            dve.wait_ge(gen_copied, 2 * T + 1)
            dve.wait_ge(gen_countT_ready, T + 1)

        dve.wait_ge(countT_ready, T)
        nc.vector.tensor_scalar(norm[:, 0, :], deg[:, :], 1.0, None, ALU.max).then_inc(norm_chain, 1)
        nc.vector.tensor_scalar(norm[:, 1, :], deg[:, :], 1.0, None, ALU.add).then_inc(norm_chain, 1)
        dve.wait_ge(norm_root_ready, 1)
        nc.vector.reciprocal(dis[:, :, :], norm_root[:, :, :]).then_inc(norm_chain, 1)
        dve.wait_ge(norm_chain, 3)
        nc.vector.tensor_tensor(norm_step[:, :, :], dis[:, :, :], dis[:, :, :], ALU.mult).then_inc(norm_chain, 1)
        dve.wait_ge(norm_chain, 4)
        nc.vector.tensor_tensor(norm_step[:, :, :], norm_step[:, :, :], norm[:, :, :], ALU.mult).then_inc(norm_chain, 1)
        dve.wait_ge(norm_chain, 5)
        nc.vector.tensor_scalar(norm_step[:, :, :], norm_step[:, :, :], -0.5, 1.5, ALU.mult, ALU.add).then_inc(norm_chain, 1)
        dve.wait_ge(norm_chain, 6)
        nc.vector.tensor_tensor(dis[:, :, :], dis[:, :, :], norm_step[:, :, :], ALU.mult).then_inc(dis_ready, 1)
        dve.wait_ge(dis_ready, 1)

        def gates(t, count, nxt):
            dve.wait_ge(gates_ready, count)
            nc.vector.tensor_tensor_reduce(gate_scratch[:, :], g[:, t, :], gw[:, 0:HID], 1.0, 0.0, ALU.mult, ALU.add,
                                           u[:, t:t + 1]).then_inc(gate_chain, 1)
            dve.wait_ge(gate_chain, 2 * count + 1)
            nc.vector.tensor_scalar(diag[t % HT][:, :], ident[:, :], u[:, t:t + 1], None, ALU.mult).then_inc(gate_chain, 1)
            nc.vector.tensor_tensor_reduce(gate_scratch[:, :], g[:, t, :], gw[:, HID:2 * HID], 1.0, gb_col[:, 0:1], ALU.mult, ALU.add,
                                           v[:, t:t + 1]).then_inc(gates_ready, 1)

        def g_rest(t, done):
            dve.wait_ge(g_hi_ready, done + 1)
            nc.vector.scalar_tensor_tensor(g_lo[:, t, :], g[:, t, :], dis[:, 0, t:t + 1], g_hi[:, t, :].bitcast(F32),
                                           ALU.mult, ALU.subtract).then_inc(g_lo_ready, 1)

        def mask_of(q, h, s):
            k = s % SLOTS
            dve.wait_ge(tanh_ready, T * q + s + 1)
            nc.vector.tensor_tensor(mask[k][:, :], mask[k][:, :], countT[:, s, h * HALF:(h + 1) * HALF], ALU.mult).then_inc(mask_ready, 1)

        def mask_rest(q, s):
            k = s % SLOTS
            dve.wait_ge(mask_hi_ready, T * q + s + 1)
            nc.vector.tensor_tensor(mask_lo[k][:, :], mask[k][:, :], mask_hi[k][:, :].bitcast(F32), ALU.subtract).then_inc(mask_lo_ready, 1)

        def take_sums(q, h):
            for dd in range(HT):
                t = HT * h + dd
                if dd < HT - 1:
                    dve.wait_ge(sum_ready, (HT - 1) * q + dd + 1)
                else:
                    dve.wait_ge(mask_used[SLOTS - 1], 2 * q + 2)
                nc.vector.scalar_tensor_tensor(g[:, t, :], SUMS[dd], dis[:, 0, t:t + 1], g[:, t, :],
                                               ALU.mult, ALU.add).then_inc(sum_read, 1)

        def half_dve(q, h, nxt, last=False):
            if nxt is not None:
                dve.wait_ge(gw_landed, 16 * (nxt + 1))
                if h == 1:
                    nc.vector.tensor_copy(gb_col[:, :], gb[:, bass.ds(nxt, 1)]).then_inc(gb_chain, 1)
            for s in range(T):
                if s < T - 2:
                    mask_of(q, h, s + 2)
                elif not last:
                    mask_of(q + 1, 1 - h, s + 2 - T)
                mask_rest(q, s)
                if s == 0 and not (isinstance(q, int) and q == 0):
                    take_sums(q - 1, 1 - h)
                if nxt is None:
                    continue
                if 1 <= s < 1 + HT:
                    t = s - 1 + (HT if h == 0 else 0)
                    if s == 1:
                        dve.wait_ge(sum_read, HT * q)
                        dve.wait_ge(gb_chain, nxt + 1)
                        dve.wait_ge(u_spread, q + 1)
                    gates(t, T * nxt + t, nxt)
                    if h == 0:
                        g_rest(t, T * nxt + t)
                if h == 1 and s >= HT:
                    g_rest(s - HT, T * nxt + s - HT)

        dve.wait_ge(gw_landed, 16)
        nc.vector.tensor_copy(gb_col[:, :], gb[:, 0:1]).then_inc(gb_chain, 1)
        dve.wait_ge(gb_chain, 1)
        for t in range(T):
            if t == HT:
                dve.wait_ge(u_spread, 1)
            gates(t, t, 0)
            g_rest(t, t)
        mask_of(0, 0, 0)
        mask_of(0, 0, 1)
        half_dve(0, 0, None)
        with dve.Fori(0, GATES - 1) as r:
            half_dve(2 * r + 1, 1, r + 1)
            half_dve(2 * r + 2, 0, r + 1)
        half_dve(2 * GATES - 1, 1, None, last=True)
        take_sums(2 * GATES - 1, 1)

        d1 = dense[1]

        def residual(i, b):
            dve.wait_ge(res_landed[b], 16 * d1.pairs(i + 1))
            dve.wait_ge(product_ready[b], d1.pairs(i + 1))
            nc.vector.tensor_tensor(xres[b][:, :], PRODUCT[b], xres[b][:, :], ALU.add).then_inc(product_read[b], 1)

        dense_dve(dve, d1, residual)

        d2 = dense[2]

        def y_rest(i, b):
            t = 2 * i + b
            dve.wait_ge(y_hi_ready, t + 1)
            nc.vector.scalar_tensor_tensor(y_all[:, bass.ds(t, 1), 1, :].rearrange("p a n -> p (a n)"), PRODUCT[b], dis[:, 1, bass.ds(t, 1)],
                                           y_all[:, bass.ds(t, 1), 0, :].rearrange("p a n -> p (a n)").bitcast(F32),
                                           ALU.mult, ALU.subtract).then_inc(product_read[b], 1)

        for b in range(2):
            dve.wait_ge(product_ready[b], d1.pairs(HT))
        for t in range(T):
            nc.vector.tensor_tensor(countT[:, t, t * P:(t + 1) * P], countT[:, t, t * P:(t + 1) * P], ident[:, :],
                                    ALU.add).then_inc(loops_added, 1)
        dense_dve(dve, d2, y_rest)

        def gcn_out(grp, j):
            t = GRP * grp + j
            if j == 0:
                dve.wait_ge(agg_ready, grp + 1)
            else:
                dve.wait_ge(cnt_used[SLOTS - 1], 2 * grp + 2)
            nc.vector.scalar_tensor_tensor(gcn_work[:, :], AGG[j], dis[:, 1, bass.ds(t, 1)], b2_all[:, :],
                                           ALU.mult, ALU.add).then_inc(agg_chain, 1)
            dve.wait_ge(agg_chain, t + 1)
            dve.wait_ge(agg_landed[j], 16 * (grp + 1))
            nc.vector.scalar_tensor_tensor(xres[j][:, :], gcn_work[:, :], 0.0, xres[j][:, :], ALU.max, ALU.add).then_inc(agg_read, 1)
            dve.wait_ge(agg_read, t + 1)

        dve.wait_ge(b2_landed, 16)
        with dve.Fori(0, 2) as grp:
            gcn_out(grp, 0)
            gcn_out(grp, 1)
        split_dve(dve, dense[3])
        with dve.Fori(2, GROUPS) as grp:
            gcn_out(grp, 0)
            gcn_out(grp, 1)

        d3 = dense[3]

        def scores(i, b):
            t = 2 * i + b
            dve.wait_ge(y_hi_ready, T + t + 1)
            nc.vector.tensor_tensor_reduce(SCRATCH, PRODUCT[b], att_all[:, 0:D], 1.0, 0.0, ALU.mult, ALU.add,
                                           al_col[b][:, 0:1]).then_inc(al_chain, 1)
            dve.wait_ge(al_chain, 2 * t + 1)
            nc.vector.tensor_tensor_reduce(SCRATCH, PRODUCT[b], att_all[:, D:2 * D], 1.0, 0.0, ALU.mult, ALU.add,
                                           al_col[b][:, 1:2]).then_inc(al_chain, 1)
            nc.vector.tensor_tensor(y_all[:, bass.ds(t, 1), 1, :].rearrange("p a n -> p (a n)"), PRODUCT[b],
                                    y_all[:, bass.ds(t, 1), 0, :].rearrange("p a n -> p (a n)").bitcast(F32),
                                    ALU.subtract).then_inc(product_read[b], 1)
            dve.wait_ge(al_chain, 2 * t + 2)
            nc.vector.tensor_copy(al[:, bass.ds(t, 1)], al_col[b][:, 0:1]).then_inc(al_copied, 1)
            nc.vector.tensor_copy(ar[:, bass.ds(t, 1)], al_col[b][:, 1:2]).then_inc(al_ready, 1)

        dve.wait_ge(att_landed, 16)
        dense_dve(dve, d3, scores)
        dve.wait_ge(al_copied, T)
        dve.wait_ge(al_ready, T)
        for b in range(2):
            dve.wait_ge(product_ready[b], d3.pairs(HT))
        for t in range(T):
            if t >= 2:
                dve.wait_ge(al_diag_used, t - 1)
            nc.vector.tensor_scalar(al_diag[t % 2][:, :], ident[:, :], al[:, t:t + 1], None, ALU.mult).then_inc(al_diag_ready, 1)

        def logits(grp, s):
            if not isinstance(grp, int) or grp > 0:
                dve.wait_ge(att_used, T * (grp - 1) + s + 1)
            nc.vector.tensor_scalar(att_e[s][:, :], al_all[:, bass.ds(grp * GC, GC)], ar[:, s:s + 1], None, ALU.add).then_inc(logit_ready, 1)
            dve.wait_ge(logit_ready, T * grp + s + 1)
            nc.vector.scalar_tensor_tensor(att_e[s][:, :], att_e[s][:, :], SLOPE, att_e[s][:, :], ALU.mult, ALU.max).then_inc(leaky_ready, 1)

        def att_of(grp, s):
            dve.wait_ge(exp_ready, T * grp + s + 1)
            nc.vector.tensor_tensor(att_e[s][:, :], att_e[s][:, :], count[:, s, bass.ds(grp * GC, GC)], ALU.mult).then_inc(att_e_ready, 1)

        def att_rest(grp, s):
            dve.wait_ge(att_hi_ready, T * grp + s + 1)
            nc.vector.tensor_tensor(att_lo[s][:, :], att_e[s][:, :], att_hi[s][:, :].bitcast(F32), ALU.subtract).then_inc(att_lo_ready, 1)

        GAT_STEPS = 2

        def elu_start(grp, j):
            t = GRP * grp + j
            dve.wait_ge(den_taken, t + 1)
            nc.vector.tensor_scalar(rden[:, j, 0:1], rden[:, j, 0:1], EPS_GAT, None, ALU.add).then_inc(gat_chain, 1)
            dve.wait_ge(gat_chain, GAT_STEPS * t + 1)
            nc.vector.reciprocal(rden[:, j, 1:2], rden[:, j, 0:1]).then_inc(gat_chain, 1)
            dve.wait_ge(gat_chain, GAT_STEPS * t + 2)
            dve.wait_ge(gat_read, t + 1)
            nc.vector.tensor_scalar(elu_neg[j][:, :], xin[j][:, :], rden[:, j, 1:2], 0.0, ALU.mult, ALU.min).then_inc(gat_neg_ready, 1)

        def elu_end(grp, j):
            t = GRP * grp + j
            dve.wait_ge(gat_landed[j], 16 * (grp + 1))
            dve.wait_ge(gat_exp_ready, t + 1)
            nc.vector.scalar_tensor_tensor(elu_neg[j][:, :], elu_neg[j][:, :], -1.0, xres[j][:, :], ALU.add, ALU.add).then_inc(elu_added, 1)
            dve.wait_ge(elu_added, t + 1)
            dve.wait_ge(gat_pos_ready, t + 1)
            nc.vector.tensor_tensor(xres[j][:, :], elu_neg[j][:, :], xin[j][:, :], ALU.add).then_inc(gat_added, 1)

        def attention_dve(grp, first, last):
            for s in range(T):
                if s < T - 2:
                    logits(grp, s + 2)
                elif not last:
                    logits(grp + 1, s + 2 - T)
                if s < T - 1:
                    att_of(grp, s + 1)
                elif not last:
                    att_of(grp + 1, 0)
                att_rest(grp, s)
                if not first and s == 4:
                    elu_start(grp - 1, 0)
                    elu_start(grp - 1, 1)
                if not first and s in (7, 8):
                    elu_end(grp - 1, s - 7)

        dve.wait_ge(count_landed, 16)
        dve.wait_ge(al_all_ready, 1)
        logits(0, 0)
        logits(0, 1)
        att_of(0, 0)
        attention_dve(0, True, False)
        with dve.Fori(1, GROUPS - 1) as grp:
            attention_dve(grp, False, False)
        attention_dve(GROUPS - 1, False, True)
        for j in range(GRP):
            elu_start(GROUPS - 1, j)
        for j in range(GRP):
            elu_end(GROUPS - 1, j)

    @block.tensor
    def _(pe):
        pe.wait_ge(consts_done, 3)
        pe.wait_ge(below_chain, 3)
        nc.tensor.matmul(ps[0:1, 7 * BANK:7 * BANK + WINDOWS], ones[0:EP, 0:1], below_n[0:EP, :],
                         start=True, stop=True).then_inc(below_summed, 1)
        dense_pe(pe, dense[0])
        for b in range(2):
            pe.wait_ge(product_read[b], dense[0].pairs(HT))

        def rows_pe(i, b, weights):
            a = 2 * i + b
            pe.wait_ge(wsel_ready, a + 1)
            pe.wait_ge(counts_copied, a)
            for c in range(CHUNKS):
                r, n = use_of(CHUNKS * b + c)
                pe.wait_ge(onehot_ready, CHUNKS * a + c + 1)
                for lo, hi in BLOCKS:
                    for j in range(QW):
                        last = nc.tensor.matmul(COUNTS[j * WIN:(j + 1) * WIN, lo:hi], sel[b][:, 0, j * CHUNKS + c, :],
                                                onehot[r][j][:, lo:hi], start=(c == 0), stop=(c == CHUNKS - 1))
                if weights:
                    if c == CHUNKS - 1:
                        last.then_inc(counts_ready, 1)
                    if c == 0:
                        pe.wait_ge(weights_copied, a)
                    for lo, hi in BLOCKS[:2]:
                        for k in range(3):
                            for j in range(QW):
                                last = nc.tensor.matmul(WEIGHTS[j * WIN:(j + 1) * WIN, lo:hi], sel[b][:, 1 + k, j * CHUNKS + c, :],
                                                        onehot[r][j][:, lo:hi], start=(c == 0 and k == 0),
                                                        stop=(c == CHUNKS - 1 and k == 2))
                last.then_inc(onehot_used[r], 1)
            pe.wait_ge(counts_copied, a + 1)
            pe.wait_ge(countT_ready, a)
            for s in range(T):
                last = nc.tensor.transpose(COUNT_T[:, s * P:(s + 1) * P], count_f[b][:, s * P:(s + 1) * P], ident[:, :])
            last.then_inc(count_transposed[b], 1)

        rows_pe(0, 0, True)
        rows_pe(0, 1, True)
        with pe.Fori(1, WT_TILES // 2) as i:
            rows_pe(i, 0, True)
            rows_pe(i, 1, True)
        rows_pe(HT - 1, 0, False)
        rows_pe(HT - 1, 1, False)
        pe.wait_ge(captured_ready, 1)
        nc.tensor.matmul(ps[:, 0:1], ones[:, :], captured[:, :], start=True, stop=True).then_inc(captured_summed, 1)

        pe.wait_ge(complete_ready, 1)
        whole = pe.value_load(complete[0:1, 0:1], min_val=0, max_val=1)
        with pe.If(whole == 0):
            pe.sem_inc(gen_used, 1)
            dsel = sel[0][:, :, :, :].rearrange("p k a i -> p k (a i)").rearrange("p k (c m) -> p k c m", m=P)
            with pe.Fori(0, T) as a:
                pe.wait_ge(gen_copied, 2 * a + 1)
                for part, blocks in ((COUNTS, BLOCKS), (WEIGHTS, BLOCKS[:2])):
                    for lo, hi in blocks:
                        nc.tensor.matmul(part[:, lo:hi], zeros[:, :], iota_h[:, lo:hi], start=True, stop=False, skip_group_check=True)
                with pe.Fori(0, GENERAL_CHUNKS) as c:
                    n = a * GENERAL_CHUNKS + c
                    pe.wait_ge(gen_ready, n + 1)
                    for q in range(CHUNKS):
                        right = onehot[q // QW][q % QW]
                        for lo, hi in BLOCKS:
                            last = nc.tensor.matmul(COUNTS[:, lo:hi], dsel[0:EP, 0, q, :], right[0:EP, lo:hi], start=False, stop=False, skip_group_check=True)
                        for lo, hi in BLOCKS[:2]:
                            for k in range(3):
                                last = nc.tensor.matmul(WEIGHTS[:, lo:hi], dsel[0:EP, 1 + k, q, :], right[0:EP, lo:hi], start=False, stop=False, skip_group_check=True)
                    last.then_inc(gen_used, 1)
                for part, blocks in ((COUNTS, BLOCKS), (WEIGHTS, BLOCKS[:2])):
                    for lo, hi in blocks:
                        last = nc.tensor.matmul(part[:, lo:hi], zeros[:, :], iota_h[:, lo:hi], start=False, stop=True, skip_group_check=True)
                last.then_inc(gen_summed, 1)
                pe.wait_ge(gen_copied, 2 * a + 2)
                pe.wait_ge(gen_countT_ready, a + 1)
                for s in range(T):
                    last = nc.tensor.transpose(COUNT_T[:, s * P:(s + 1) * P], count_f[0][:, s * P:(s + 1) * P], ident[:, :])
                last.then_inc(gen_transposed, 1)
            pe.wait_ge(gen_copied, 2 * T + 1)
            pe.wait_ge(gen_countT_ready, T + 1)
        pe.sem_inc(built, 1)

        def spread_u(q):
            pe.wait_ge(gate_chain, 2 * HT * q + 2 * HT)
            pe.wait_ge(tanh_ready, 2 * HT * q)
            for dd in range(HT):
                last = nc.tensor.matmul(U_ALL[:, dd * P:(dd + 1) * P], ones[:, :], diag[dd][:, :], start=True, stop=True)
            last.then_inc(u_spread, 1)

        def half_pe(q, r, h):
            for s in range(T):
                k = s % SLOTS
                if s == HT + 2 and not is_last(q):
                    spread_u(q + 1)
                if h == 0:
                    pe.wait_ge(g_lo_ready, T * r + s + 1)
                pe.wait_ge(mask_lo_ready, 2 * HT * q + s + 1)
                for dd in range(HT):
                    if s == 0:
                        pe.wait_ge(sum_read, HT * q - HT + dd + 1) if q_has_before(q) else None
                    cols = slice(dd * P, (dd + 1) * P)
                    nc.tensor.matmul(SUMS[dd], mask_hi[k][:, cols], g_hi[:, s, :], start=(s == 0), stop=False)
                    nc.tensor.matmul(SUMS[dd], mask_hi[k][:, cols], g_lo[:, s, :], start=False, stop=False)
                    last = nc.tensor.matmul(SUMS[dd], mask_lo[k][:, cols], g_hi[:, s, :], start=False, stop=(s == T - 1))
                    if s == T - 1 and dd < HT - 1:
                        last.then_inc(sum_ready, 1)
                last.then_inc(mask_used[k], 1)

        def q_has_before(q):
            return not (isinstance(q, int) and q == 0)

        def is_last(q):
            return isinstance(q, int) and q == 2 * GATES - 1

        pe.wait_ge(countT_ready, T)
        spread_u(0)
        half_pe(0, 0, 0)
        with pe.Fori(0, GATES - 1) as r:
            half_pe(2 * r + 1, r, 1)
            half_pe(2 * r + 2, r + 1, 0)
        half_pe(2 * GATES - 1, GATES - 1, 1)
        pe.wait_ge(sum_read, T * GATES)

        dense_pe(pe, dense[1])
        for b in range(2):
            pe.wait_ge(product_read[b], dense[1].pairs(HT))
        dense_pe(pe, dense[2])
        for b in range(2):
            pe.wait_ge(product_read[b], dense[2].pairs(HT))

        def gcn_pe(grp):
            for s in range(T):
                k = s % SLOTS
                pe.wait_ge(cnt_ready, T * grp + s + 1)
                for j in range(GRP):
                    if s == 0:
                        pe.wait_ge(agg_chain, GRP * grp - GRP + j + 1) if q_has_before(grp) else None
                    left = cnt2[k][:, j * P:(j + 1) * P]
                    for n in range(2):
                        out_n = AGG[j][:, n * BANK:(n + 1) * BANK]
                        nc.tensor.matmul(out_n, left, y_hi[s][:, n * BANK:(n + 1) * BANK], start=(s == 0), stop=False)
                        last = nc.tensor.matmul(out_n, left, y_lo[s][:, n * BANK:(n + 1) * BANK], start=False, stop=(s == T - 1))
                    if s == T - 1 and j == 0:
                        last.then_inc(agg_ready, 1)
                last.then_inc(cnt_used[k], 1)

        gcn_pe(0)
        with pe.Fori(1, GROUPS) as grp:
            gcn_pe(grp)
        pe.wait_ge(agg_chain, T)

        dense_pe(pe, dense[3])
        for b in range(2):
            pe.wait_ge(product_read[b], dense[3].pairs(HT))
        for t in range(T):
            pe.wait_ge(al_diag_ready, t + 1)
            nc.tensor.matmul(AL_ALL[:, t * P:(t + 1) * P], ones[:, :], al_diag[t % 2][:, :], start=True, stop=True).then_inc(al_diag_used, 1)

        def gat_pe(grp):
            for s in range(T):
                pe.wait_ge(att_lo_ready, T * grp + s + 1)
                for j in range(GRP):
                    if s == 0:
                        pe.wait_ge(gat_read, GRP * grp - GRP + j + 1) if q_has_before(grp) else None
                    hi, lo = att_hi[s][:, j * P:(j + 1) * P], att_lo[s][:, j * P:(j + 1) * P]
                    nc.tensor.matmul(DEN[j], hi, ones_r[:, :], start=(s == 0), stop=False)
                    for n in range(2):
                        cols = slice(n * BANK, (n + 1) * BANK)
                        nc.tensor.matmul(AGG[j][:, cols], hi, y_hi[s][:, cols], start=(s == 0), stop=False)
                        nc.tensor.matmul(AGG[j][:, cols], hi, y_lo[s][:, cols], start=False, stop=False)
                    nc.tensor.matmul(DEN[j], lo, ones_r[:, :], start=False, stop=(s == T - 1))
                    for n in range(2):
                        cols = slice(n * BANK, (n + 1) * BANK)
                        last = nc.tensor.matmul(AGG[j][:, cols], lo, y_hi[s][:, cols], start=False, stop=(s == T - 1))
                    if s == T - 1 and j == 0:
                        last.then_inc(gat_ready, 1)
                last.then_inc(att_used, 1)

        pe.wait_ge(al_all_ready, 1)
        gat_pe(0)
        with pe.Fori(1, GROUPS) as grp:
            gat_pe(grp)

    ctx.close()


_INS = ["x", "src", "dst", "edge_weight", "L0_gnn_W1", "L0_gnn_b1", "L0_gnn_gate_w", "L0_gnn_gate_b", "L1_gnn_bias",
        "L2_gnn_W", "L2_gnn_b", "L3_gnn_W", "L3_gnn_a"]


def kernel(**inputs):
    import numpy as np
    import concourse.bacc as bacc
    from concourse.bass_utils import run_bass_kernel_spmd

    nc = bacc.Bacc("TRN2", target_bir_lowering=False, num_devices=1)
    arrays, args = {}, []
    for name in _INS:
        a = np.ascontiguousarray(inputs[name])
        arrays[f"in_{name}"] = a
        args.append(nc.dram_tensor(f"in_{name}", a.shape, mybir.dt.from_np(a.dtype), kind="ExternalInput").ap())
    out = nc.dram_tensor("out_x", (N, D), F32, kind="ExternalOutput").ap()
    build_program(nc, *args, out)
    r = run_bass_kernel_spmd(nc, [arrays], core_ids=[0])
    return r.results[0]["out_x"]
```

```python
from contextlib import ExitStack

import concourse.bass as bass
from concourse import mybir

ALU = mybir.AluOpType
ACT = mybir.ActivationFunctionType
AX_X = mybir.AxisListType.X
F32 = mybir.dt.float32
F32R = mybir.dt.float32r
BF16 = mybir.dt.bfloat16
F16 = mybir.dt.float16
I32 = mybir.dt.int32
I16 = mybir.dt.int16

P = 128
D = 1024
HID = 512
GATES = 4
N = 1250
E = 20000
T = -(-N // P)
NP = T * P
KT = D // P
WT_TILES = KT
WIN = 32
QW = P // WIN
WINDOWS = T * QW
CHUNKS = 5
CAP = CHUNKS * P
EP = 125
EC = E // EP
GENERAL_CHUNKS = E // (EP * CHUNKS)
HALF = NP // 2
HT = T // 2
BANK = 512
GRP = 2
GROUPS = T // GRP
GC = GRP * P
SLOTS = 5
TANH_LEAD = 3
EPS_LN = 1e-5
EPS_GAT = 1e-5
SLOPE = 0.1
KIB = 1024


def build_program(nc, x, src, dst, edge_weight, w1, b1, gate_w, gate_b, bias1, w2, b2, w3, att, out):
    ctx = ExitStack()
    base = -(-nc.sbuf_base // 64) * 64
    limit = nc.sbuf_usable_end
    R_Y = base
    R_W = R_Y + 80 * KIB
    R_C = R_W + 64 * KIB
    R_X = R_C + T * NP * 2
    R_S = R_X + 32 * KIB
    places = [R_S]

    def at(name, shape, dtype, offset):
        return nc.alloc_sbuf_tensor_at(name, shape, dtype, offset=offset)

    def small(name, shape, dtype):
        size = 4 if dtype in (F32, F32R, I32) else 2
        for n in shape[1:]:
            size *= n
        offset = places[0]
        places[0] = -(-(offset + size) // 32) * 32
        assert places[0] <= limit, name
        return at(name, shape, dtype, offset)

    def sem(name):
        return ctx.enter_context(nc.semaphore(name))

    def sems(name, n):
        return [sem(f"{name}{i}") for i in range(n)]

    ps = ctx.enter_context(nc.psum_tensor("ps", [P, 8 * BANK], F32))

    x1_dram = nc.dram_tensor("x_after_0", (NP, D), F32).ap()
    x2_dram = nc.dram_tensor("x_after_1", (NP, D), F32).ap()
    x3_dram = nc.dram_tensor("x_after_2", (NP, D), F32).ap()
    count_dram = nc.dram_tensor("count_rows", (NP, NP), I16).ap()
    wt_dram = nc.dram_tensor("weight_rows", (NP, D), F32).ap()

    xin = [at(f"xin{b}", [P, D], F32, R_X + b * 4 * KIB) for b in range(2)]
    xres = [at(f"xres{b}", [P, D], F32, R_X + (8 + 4 * b) * KIB) for b in range(2)]
    hT_hi = [at(f"hT_hi{b}", [P, KT, P], F32R, R_X + (16 + 8 * b) * KIB) for b in range(2)]
    hT_lo = [at(f"hT_lo{b}", [P, KT, P], F32R, R_X + (20 + 8 * b) * KIB) for b in range(2)]

    w1_raw = at("w1_raw", [P, KT, HID], F32, R_Y + 64 * KIB)
    w1_hi = at("w1_hi", [P, KT, HID], F32R, R_Y + 20 * KIB)
    w1_lo = at("w1_lo", [P, KT, HID], F32R, R_Y + 36 * KIB)
    wt_raw = at("wt_raw", [P, KT, D], F32, R_W + 32 * KIB)
    wt_hi = at("wt_hi", [P, KT, D], F32R, R_W)
    wt_lo = at("wt_lo", [P, KT, D], F32R, R_W + 32 * KIB)
    w_raw = at("w_raw", [P, KT, D], F32, R_Y + 32 * KIB)
    w_hi = at("w_hi", [P, KT, D], F32R, R_Y)
    w_lo = at("w_lo", [P, KT, D], F32R, R_Y + 32 * KIB)

    g = at("g", [P, T, HID], F32, R_Y)
    g_hi = at("g_hi", [P, T, HID], F32R, R_Y + 20 * KIB)
    g_lo = at("g_lo", [P, T, HID], F32R, R_Y + 40 * KIB)
    gw = at("gw", [P, 2 * HID], F32, R_Y + 60 * KIB)
    gate_scratch = at("gate_scratch", [P, HID], F32, R_Y + 64 * KIB)
    diag = [at(f"diag{d}", [P, P], F32, R_Y + 66 * KIB + d * P * 4) for d in range(HT)]
    b1_all = at("b1_all", [P, HID], F32, R_Y + 60 * KIB)
    PIECE = HALF * 4
    piece = [R_X + 16 * KIB + n * PIECE for n in range(6)]
    piece += [R_Y + 66 * KIB + HT * P * 4 + n * PIECE for n in range(2 * SLOTS - 6)]
    assert piece[-1] + PIECE <= R_W
    mask = [at(f"mask{k}", [P, HALF], F32, piece[2 * k]) for k in range(SLOTS)]
    mask_lo = [at(f"mask_lo{k}", [P, HALF], F32R, piece[2 * k]) for k in range(SLOTS)]
    mask_hi = [at(f"mask_hi{k}", [P, HALF], F32R, piece[2 * k + 1]) for k in range(SLOTS)]

    y_all = at("y_all", [P, T, 2, D], F32R, R_Y + 64 * KIB)
    y_hi = [y_all[:, s, 0, :] for s in range(T)]
    y_lo = [y_all[:, s, 1, :] for s in range(T)]
    cnt2 = [at(f"cnt2_{k}", [P, GC], F32R, R_X + 24 * KIB + k * GC * 4) for k in range(SLOTS)]
    att_all = at("att_all", [P, 2 * D], F32, R_X + 8 * KIB)
    att_e = [at(f"att_e{s}", [P, GC], F32, R_Y + 2 * KIB * s) for s in range(T)]
    att_lo = [at(f"att_lo{s}", [P, GC], F32R, R_Y + 2 * KIB * s) for s in range(T)]
    att_hi = [at(f"att_hi{s}", [P, GC], F32R, R_Y + 2 * KIB * s + KIB) for s in range(T)]
    al_all = at("al_all", [P, NP], F32, R_Y + 24 * KIB)
    elu_neg = [at(f"elu_neg{j}", [P, D], F32, R_X + (16 + 4 * j) * KIB) for j in range(GRP)]

    countT = at("countT", [P, T, NP], I16, R_C)
    count = at("count", [P, T, NP], I16, R_C)

    o = [R_W]

    def build(name, shape, dtype):
        size = 4 if dtype in (F32, I32) else 2
        for n in shape[1:]:
            size *= n
        offset = o[0]
        o[0] += -(-size // 32) * 32
        assert o[0] <= R_C, name
        return at(name, shape, dtype, offset)

    onehot = [[build(f"onehot{r}_{j}", [P, NP], BF16) for j in range(QW)] for r in range(2)]
    sel = [build(f"sel{b}", [P, 4, QW * CHUNKS, WIN], BF16) for b in range(2)]
    iota_f = build("iota_f", [P, NP], F32)
    iota_h = build("iota_h", [P, NP], F16)
    count_f = [build(f"count_f{b}", [P, NP], F32) for b in range(2)]
    count_row = [build(f"count_row{b}", [P, NP], I16) for b in range(2)]
    weight_row = [build(f"weight_row{b}", [P, D], F32) for b in range(2)]
    ends_raw = [build(f"ends_raw{b}", [P, 2, QW * CHUNKS], I32) for b in range(2)]
    ends = [build(f"ends{b}", [P, 2, QW * CHUNKS], F32) for b in range(2)]
    ew = [build(f"ew{b}", [P, QW * CHUNKS], F32) for b in range(2)]
    ew_rest = [build(f"ew_rest{b}", [P, 2, QW * CHUNKS], F32) for b in range(2)]
    ew_part = [build(f"ew_part{b}", [P, 3, QW * CHUNKS], BF16) for b in range(2)]
    dst_raw = at("dst_raw", [P, EC], I32, R_W + 16 * KIB)
    dst_f = at("dst_f", [P, EC], F32, R_W + 17 * KIB)
    below = at("below", [P, WINDOWS, EC], BF16, R_W)

    ident = small("ident", [P, P], F32)
    ones = small("ones", [P, P], F32)
    ones_r = small("ones_r", [P, 2], F32R)
    zeros = small("zeros", [P, P], BF16)
    stats = [small(f"stats{b}", [P, 2, 6], F32) for b in range(2)]
    mv = [small(f"mv{b}", [P, 2], F32) for b in range(2)]
    ln = [small(f"ln{b}", [P, 6], F32) for b in range(2)]
    deg = small("deg", [P, T], F32)
    norm = small("norm", [P, 2, T], F32)
    norm_root = small("norm_root", [P, 2, T], F32)
    norm_step = small("norm_step", [P, 2, T], F32)
    dis = small("dis", [P, 2, T], F32)
    below_n = small("below_n", [P, WINDOWS], F32)
    starts = small("starts", [P, WINDOWS], I32)
    captured = small("captured", [P, 1], F32)
    complete = small("complete", [P, 1], I32)
    gb = small("gb", [P, GATES], F32)
    u = small("u", [P, T], F32)
    v = small("v", [P, T], F32)
    al = small("al", [P, T], F32)
    ar = small("ar", [P, T], F32)
    al_col = [small(f"al_col{b}", [P, 2], F32) for b in range(2)]
    rden = small("rden", [P, GRP, 2], F32)
    row_all = small("row_all", [P, D], F32)
    gb_col = small("gb_col", [P, 1], F32)
    al_diag = [at(f"al_diag{b}", [P, P], F32, R_Y + 32 * KIB + b * P * 4) for b in range(2)]

    consts_landed = sem("consts_landed")
    iota_done = sem("iota_done")
    consts_done = sem("consts_done")

    xin_landed = sems("xin_landed", 2)
    ln_chain = sem("ln_chain")
    var_ready = sem("var_ready")
    root_ready = sem("root_ready")
    scale_ready = sem("scale_ready")
    h_ready = sem("h_ready")
    h_transposed = sems("h_transposed", 2)
    hT_hi_ready = sem("hT_hi_ready")
    hT_lo_ready = sem("hT_lo_ready")
    product_ready = sems("product_ready", 2)
    product_read = sems("product_read", 2)
    w_landed = sems("w_landed", 4)
    w_hi_ready = sem("w_hi_ready")
    w_lo_ready = sem("w_lo_ready")
    res_landed = sems("res_landed", 2)
    res_added = sem("res_added")
    stored = sems("stored", 2)

    class Dense:

        def __init__(self, n):
            self.n = n

        def pairs(self, i):
            return HT * self.n + i

        def tiles(self, t):
            return T * self.n + t

    dense = [Dense(n) for n in range(4)]
    LN_STEPS = 7

    dst_landed = sem("dst_landed")
    below_chain = sem("below_chain")
    below_summed = sem("below_summed")
    starts_ready = sem("starts_ready")
    ends_landed = sems("ends_landed", 2)
    ends_ready = sem("ends_ready")
    sel_ready = sem("sel_ready")
    parts_chain = sem("parts_chain")
    wsel_ready = sem("wsel_ready")
    onehot_ready = sem("onehot_ready")
    onehot_used = sems("onehot_used", 2)
    counts_ready = sem("counts_ready")
    counts_copied = sem("counts_copied")
    weights_copied = sem("weights_copied")
    count_transposed = sems("count_transposed", 2)
    countT_ready = sem("countT_ready")
    count_row_ready = sem("count_row_ready")
    count_stored = sems("count_stored", 2)
    weights_stored = sems("weights_stored", 2)
    captured_ready = sem("captured_ready")
    captured_summed = sem("captured_summed")
    complete_ready = sem("complete_ready")
    gen_landed = sem("gen_landed")
    gen_chain = sem("gen_chain")
    gen_ready = sem("gen_ready")
    gen_used = sem("gen_used")
    gen_summed = sem("gen_summed")
    gen_copied = sem("gen_copied")
    gen_transposed = sem("gen_transposed")
    gen_countT_ready = sem("gen_countT_ready")
    gen_row_ready = sem("gen_row_ready")
    gen_stored = sem("gen_stored")
    built = sem("built")
    norm_chain = sem("norm_chain")
    norm_root_ready = sem("norm_root_ready")
    dis_ready = sem("dis_ready")
    gw_landed = sem("gw_landed")
    gate_chain = sem("gate_chain")
    gates_ready = sem("gates_ready")
    u_spread = sem("u_spread")
    g_hi_ready = sem("g_hi_ready")
    g_lo_ready = sem("g_lo_ready")
    tanh_ready = sem("tanh_ready")
    mask_ready = sem("mask_ready")
    mask_hi_ready = sem("mask_hi_ready")
    mask_lo_ready = sem("mask_lo_ready")
    mask_used = sems("mask_used", SLOTS)
    sum_ready = sem("sum_ready")
    sum_read = sem("sum_read")
    half_landed = sems("half_landed", 4)
    half_added = sem("half_added")
    half_stored = sems("half_stored", 2)
    y_hi_ready = sem("y_hi_ready")
    loops_added = sem("loops_added")
    cnt_ready = sem("cnt_ready")
    cnt_used = sems("cnt_used", SLOTS)
    agg_ready = sem("agg_ready")
    agg_read = sem("agg_read")
    agg_chain = sem("agg_chain")
    agg_landed = sems("agg_landed", 2)
    agg_stored = sems("agg_stored", 2)
    b2_landed = sem("b2_landed")
    bias1_landed = sem("bias1_landed")
    att_landed = sem("att_landed")
    count_landed = sem("count_landed")
    al_chain = sem("al_chain")
    al_ready = sem("al_ready")
    al_diag_ready = sem("al_diag_ready")
    al_diag_used = sem("al_diag_used")
    al_all_ready = sem("al_all_ready")
    logit_ready = sem("logit_ready")
    leaky_ready = sem("leaky_ready")
    exp_ready = sem("exp_ready")
    att_e_ready = sem("att_e_ready")
    att_hi_ready = sem("att_hi_ready")
    att_lo_ready = sem("att_lo_ready")
    att_used = sem("att_used")
    gat_ready = sem("gat_ready")
    gat_read = sem("gat_read")
    den_taken = sem("den_taken")
    elu_added = sem("elu_added")
    gat_pos_ready = sem("gat_pos_ready")
    gat_chain = sem("gat_chain")
    gat_neg_ready = sem("gat_neg_ready")
    gat_exp_ready = sem("gat_exp_ready")
    gat_landed = sems("gat_landed", 2)
    gat_added = sem("gat_added")
    gat_stored = sems("gat_stored", 2)
    al_copied = sem("al_copied")
    gb_chain = sem("gb_chain")

    block = ctx.enter_context(nc.Block())

    NHALF = [1, 2, 2, 2]
    W_RAW = [w1_raw, wt_raw, w_raw, w_raw]
    W_HI = [w1_hi, wt_hi, w_hi, w_hi]
    W_LO = [w1_lo, wt_lo, w_lo, w_lo]
    TRANSPOSED = ps[:, 6 * BANK:8 * BANK]
    PRODUCT = [ps[:, (2 + 2 * b) * BANK:(4 + 2 * b) * BANK] for b in range(2)]
    SCRATCH = ps[:, 0:2 * BANK]

    def rows(t):
        return bass.ds(t * P, P)

    def split_act(act, d, ks):
        for k in ks:
            if k % 2 == 0:
                act.wait_ge(w_landed[k // 2], 16 * (d.n + 1))
            nc.scalar.activation(W_HI[d.n][:, k, :], W_RAW[d.n][:, k, :], ACT.Copy).then_inc(w_hi_ready, 1)

    def split_dve(dve, d, ks):
        for k in ks:
            dve.wait_ge(w_hi_ready, KT * d.n + k + 1)
            nc.vector.tensor_tensor(W_LO[d.n][:, k, :], W_RAW[d.n][:, k, :], W_HI[d.n][:, k, :].bitcast(F32),
                                    ALU.subtract).then_inc(w_lo_ready, 1)

    def stats_dve(dve, d, i, b):
        t = 2 * i + b
        dve.wait_ge(xin_landed[b], 16 * d.pairs(i + 1))
        for half in range(2):
            nc.vector.bn_stats(stats[b][:, half, :], xin[b][:, half * 512:(half + 1) * 512]).then_inc(ln_chain, 1)
        settled(dve, ln_chain, LN_STEPS * d.tiles(t) + 2)
        nc.vector.bn_aggr(mv[b][:, :], stats[b][:, :, :].rearrange("p a s -> p (a s)")).then_inc(ln_chain, 1)
        dve.wait_ge(ln_chain, LN_STEPS * d.tiles(t) + 3)
        nc.vector.tensor_scalar(ln[b][:, 0:1], mv[b][:, 1:2], EPS_LN, None, ALU.add).then_inc(var_ready, 1)

    def scale_dve(dve, d, i, b):
        t = 2 * i + b
        ve, root, r0, q, c, scale = (ln[b][:, j:j + 1] for j in range(6))
        dve.wait_ge(root_ready, d.tiles(t + 1))
        nc.vector.reciprocal(r0, root).then_inc(ln_chain, 1)
        dve.wait_ge(ln_chain, LN_STEPS * d.tiles(t) + 4)
        nc.vector.scalar_tensor_tensor(q, r0, r0, ve, ALU.mult, ALU.mult).then_inc(ln_chain, 1)
        dve.wait_ge(ln_chain, LN_STEPS * d.tiles(t) + 5)
        nc.vector.tensor_scalar(c, q, -0.5, 1.5, ALU.mult, ALU.add).then_inc(ln_chain, 1)
        dve.wait_ge(ln_chain, LN_STEPS * d.tiles(t) + 6)
        nc.vector.tensor_tensor(scale, r0, c, ALU.mult).then_inc(ln_chain, 1)
        dve.wait_ge(ln_chain, LN_STEPS * d.tiles(t) + 7)
        nc.vector.tensor_scalar(q, mv[b][:, 0:1], scale, -1.0, ALU.mult, ALU.mult).then_inc(scale_ready, 1)

    def root_act(act, d, i, b):
        act.wait_ge(var_ready, d.tiles(2 * i + b + 1))
        nc.scalar.activation(ln[b][:, 1:2], ln[b][:, 0:1], ACT.Sqrt).then_inc(root_ready, 1)

    def h_act(act, d, i, b):
        act.wait_ge(scale_ready, d.tiles(2 * i + b + 1))
        nc.scalar.activation(xin[b][:, :], xin[b][:, :], ACT.Relu, bias=ln[b][:, 3:4],
                             scale=ln[b][:, 5:6]).then_inc(h_ready, 1)

    def transposed_act(act, d, i, b):
        t = 2 * i + b
        act.wait_ge(h_transposed[b], d.pairs(i + 1))
        nc.scalar.activation(hT_hi[b][:, :, :].rearrange("p k m -> p (k m)"), TRANSPOSED,
                             ACT.Copy).then_inc(hT_hi_ready, 1)

    def transposed_dve(dve, d, i, b):
        t = 2 * i + b
        dve.wait_ge(hT_hi_ready, d.tiles(t + 1))
        nc.vector.tensor_tensor(hT_lo[b][:, :, :].rearrange("p k m -> p (k m)"), TRANSPOSED,
                                hT_hi[b][:, :, :].rearrange("p k m -> p (k m)").bitcast(F32),
                                ALU.subtract).then_inc(hT_lo_ready, 1)

    def transpose_pe(pe, d, i, b):
        t = 2 * i + b
        pe.wait_ge(h_ready, d.tiles(t + 1))
        pe.wait_ge(hT_lo_ready, d.tiles(t))
        for k in range(KT):
            last = nc.tensor.transpose(TRANSPOSED[:, k * P:(k + 1) * P], xin[b][:, k * P:(k + 1) * P], ident[:, :])
        last.then_inc(h_transposed[b], 1)

    def product_pe(pe, d, i, b, first, transpose_next):
        t = 2 * i + b
        hi, lo = W_HI[d.n], W_LO[d.n]
        pe.wait_ge(hT_lo_ready, d.tiles(t + 1))
        pe.wait_ge(product_read[b], d.pairs(i))
        for k in range(KT):
            if k == KT // 2 and transpose_next is not None:
                transpose_next()
            if first:
                pe.wait_ge(w_lo_ready, KT * d.n + k + 1)
            for left, rights in ((hT_hi[b], (hi, lo)), (hT_lo[b], (hi,))):
                for half in range(NHALF[d.n]):
                    for right in rights:
                        last = nc.tensor.matmul(PRODUCT[b][:, half * BANK:(half + 1) * BANK], left[:, k, :],
                                                right[:, k, half * BANK:(half + 1) * BANK],
                                                start=(k == 0 and left is hT_hi[b] and right is hi),
                                                stop=(k == KT - 1 and left is hT_lo[b]))
        last.then_inc(product_ready[b], 1)

    def dense_pe(pe, d, nxt=None, free=None):
        if d.n == 0:
            transpose_pe(pe, d, 0, 0)
        if free is not None:
            free(0)
        product_pe(pe, d, 0, 0, True, lambda: transpose_pe(pe, d, 0, 1))
        if free is not None:
            free(1)
        product_pe(pe, d, 0, 1, False, lambda: transpose_pe(pe, d, 1, 0))
        with pe.Fori(1, HT - 1) as i:
            product_pe(pe, d, i, 0, False, lambda: transpose_pe(pe, d, i, 1))
            product_pe(pe, d, i, 1, False, lambda: transpose_pe(pe, d, i + 1, 0))
        product_pe(pe, d, HT - 1, 0, False, lambda: transpose_pe(pe, d, HT - 1, 1))
        product_pe(pe, d, HT - 1, 1, False, None if nxt is None else lambda: transpose_pe(pe, nxt, 0, 0))

    def dense_dve(dve, d, finish, nxt=None):
        if d.n == 0:
            stats_dve(dve, d, 0, 0)
            scale_dve(dve, d, 0, 0)
            split_dve(dve, d, range(KT))
            stats_dve(dve, d, 0, 1)
            transposed_dve(dve, d, 0, 0)
            scale_dve(dve, d, 0, 1)
        with dve.Fori(0, HT - 1) as i:
            for b in range(2):
                stats_dve(dve, d, i + 1, b)
                transposed_dve(dve, d, i + b, 1 - b)
                scale_dve(dve, d, i + 1, b)
                finish(i, b)
        if nxt is not None:
            stats_dve(dve, nxt, 0, 0)
        transposed_dve(dve, d, HT - 1, 1)
        if nxt is not None:
            scale_dve(dve, nxt, 0, 0)
        finish(HT - 1, 0)
        if nxt is not None:
            split_dve(dve, nxt, range(KT))
            stats_dve(dve, nxt, 0, 1)
            transposed_dve(dve, nxt, 0, 0)
            scale_dve(dve, nxt, 0, 1)
        finish(HT - 1, 1)

    def dense_act(act, d, finish, nxt=None):
        if d.n == 0:
            root_act(act, d, 0, 0)
            h_act(act, d, 0, 0)
            split_act(act, d, range(KT))
            root_act(act, d, 0, 1)
            transposed_act(act, d, 0, 0)
            h_act(act, d, 0, 1)
        with act.Fori(0, HT - 1) as i:
            for b in range(2):
                root_act(act, d, i + 1, b)
                transposed_act(act, d, i + b, 1 - b)
                h_act(act, d, i + 1, b)
                finish(i, b)
        if nxt is not None:
            root_act(act, nxt, 0, 0)
        transposed_act(act, d, HT - 1, 1)
        if nxt is not None:
            h_act(act, nxt, 0, 0)
        finish(HT - 1, 0)
        if nxt is not None:
            act.wait_ge(half_added, T)
            split_act(act, nxt, range(KT))
            root_act(act, nxt, 0, 1)
            transposed_act(act, nxt, 0, 0)
            h_act(act, nxt, 0, 1)
        finish(HT - 1, 1)

    def load_weights(eng, d, dram):
        for q in range(4):
            eng.dma_start(W_RAW[d.n][:, 2 * q:2 * q + 2, :],
                          dram[2 * q * P:(2 * q + 2) * P, :].rearrange("(k p) n -> p k n", p=P)
                          ).then_inc(w_landed[q], 16)

    settles = sem("settles")

    def settled(eng, semaphore, value):
        eng.wait_ge(semaphore, value)
        eng.sem_inc(settles, 1)

    @block.sync
    def _(sp):
        sp.dma_start(dst_raw[0:EP, :], dst.rearrange("(p c) -> p c", c=EC)).then_inc(dst_landed, 16)
        d = dense[0]
        sp.dma_start(b1_all[:, :], b1.partition_broadcast(P)).then_inc(consts_landed, 16)
        sp.dma_start(gb[:, :], gate_b.rearrange("k a -> (k a)").partition_broadcast(P)).then_inc(consts_landed, 16)
        sp.dma_start(xin[0][:, :], x[0:P, :]).then_inc(xin_landed[0], 16)
        load_weights(sp, d, w1)
        sp.dma_start(xin[1][:, :], x[P:2 * P, :]).then_inc(xin_landed[1], 16)
        with sp.Fori(1, HT - 1) as i:
            for b in range(2):
                settled(sp, h_transposed[b], d.pairs(i))
                sp.dma_start(xin[b][:, :], x[rows(2 * i + b), :]).then_inc(xin_landed[b], 16)
        sp.wait_ge(h_transposed[0], d.pairs(HT - 1))
        sp.dma_start(xin[0][:, :], x[(T - 2) * P:(T - 1) * P, :]).then_inc(xin_landed[0], 16)
        sp.wait_ge(h_transposed[1], d.pairs(HT - 1))
        sp.dma_start(xin[1][0:N - (T - 1) * P, :], x[(T - 1) * P:N, :]).then_inc(xin_landed[1], 16)

        def load_edges(i, b):
            for j in range(QW):
                start = sp.value_load(starts[0:1, bass.ds(QW * (2 * i + b) + j, 1)], min_val=0, max_val=E - CAP)
                cols = slice(j * CHUNKS, (j + 1) * CHUNKS)
                for to, of in ((ends_raw[b][:, 0, cols], src), (ends_raw[b][:, 1, cols], dst), (ew[b][:, cols], edge_weight)):
                    sp.dma_start(to, of[bass.ds(start, CAP)].rearrange("(p c) -> p c", c=CHUNKS)).then_inc(ends_landed[b], 16)

        sp.wait_ge(starts_ready, 1)
        load_edges(0, 0)
        load_edges(0, 1)
        for b in range(2):
            sp.wait_ge(product_read[b], d.pairs(HT))
        sp.dma_start(gw[:, :], gate_w[0].rearrange("c a -> (c a)").partition_broadcast(P)).then_inc(gw_landed, 16)
        with sp.Fori(1, HT) as i:
            for b in range(2):
                settled(sp, ends_ready, 2 * i + b - 1)
                settled(sp, wsel_ready, 2 * i + b - 1)
                load_edges(i, b)

        sp.wait_ge(complete_ready, 1)
        whole = sp.value_load(complete[0:1, 0:1], min_val=0, max_val=1)
        with sp.If(whole == 0):
            sp.sem_inc(gen_stored, 1)
            with sp.Fori(0, T) as a:
                with sp.Fori(0, GENERAL_CHUNKS) as c:
                    settled(sp, gen_used, a * GENERAL_CHUNKS + c + 1)
                    for to, of in ((ends_raw[0][0:EP, 0, 0:CHUNKS], src), (ends_raw[0][0:EP, 1, 0:CHUNKS], dst),
                                   (ew[0][0:EP, 0:CHUNKS], edge_weight)):
                        sp.dma_start(to, of[bass.ds(c * (EP * CHUNKS), EP * CHUNKS)].rearrange("(p c) -> p c", c=CHUNKS)
                                     ).then_inc(gen_landed, 16)
                settled(sp, gen_row_ready, a + 1)
                sp.dma_start(count_dram[rows(a), :], count_row[0][:, :]).then_inc(gen_stored, 16)
                sp.dma_start(wt_dram[rows(a), :], weight_row[0][:, :]).then_inc(gen_stored, 16)
                settled(sp, gen_stored, 32 * (a + 1) + 1)
        for b in range(2):
            sp.wait_ge(weights_stored[b], 16 * WT_TILES // 2)
            sp.wait_ge(count_stored[b], 16 * HT)
        sp.wait_ge(built, 3)
        load_weights(sp, dense[1], wt_dram)
        with sp.Fori(0, GATES - 1) as r:
            settled(sp, gates_ready, T * (r + 1))
            sp.dma_start(gw[:, :], gate_w[bass.ds(r + 1, 1)].rearrange("k c a -> (k c a)").partition_broadcast(P)
                         ).then_inc(gw_landed, 16)

        d = dense[1]

        def load_x1(i):
            for b in range(2):
                settled(sp, half_stored[b], 16 * (i + 1))
                if not isinstance(i, int) or i > 0:
                    settled(sp, h_transposed[b], d.pairs(i))
                sp.dma_start(xin[b][:, :], x1_dram[rows(2 * i + b), :]).then_inc(xin_landed[b], 16)

        for b in range(2):
            sp.wait_ge(h_transposed[b], d.pairs(0))
        load_x1(0)
        sp.dma_start(row_all[:, :], bias1.partition_broadcast(P)).then_inc(bias1_landed, 16)
        sp.wait_ge(mask_used[SLOTS - 1], 2 * 2 * GATES)
        for q in range(4):
            sp.dma_start(w_raw[:, 2 * q:2 * q + 2, :], w2[2 * q * P:(2 * q + 2) * P, :].rearrange("(k p) n -> p k n", p=P)
                         ).then_inc(w_landed[q], 16)
            load_x1(q + 1)
        d = dense[2]
        with sp.Fori(0, HT) as i:
            for b in range(2):
                settled(sp, stored[b], 16 * dense[1].pairs(i + 1))
                settled(sp, h_transposed[b], d.pairs(i))
                sp.dma_start(xin[b][:, :], x2_dram[rows(2 * i + b), :]).then_inc(xin_landed[b], 16)
        sp.wait_ge(res_added, dense[1].tiles(T))
        sp.dma_start(row_all[:, :], b2.partition_broadcast(P)).then_inc(b2_landed, 16)
        for b in range(2):
            sp.wait_ge(product_ready[b], d.pairs(HT))
        load_weights(sp, dense[3], w3)
        d = dense[3]
        with sp.Fori(0, HT) as i:
            for b in range(2):
                settled(sp, agg_stored[b], 16 * (i + 1))
                settled(sp, h_transposed[b], d.pairs(i))
                sp.dma_start(xin[b][:, :], x3_dram[rows(2 * i + b), :]).then_inc(xin_landed[b], 16)
        sp.wait_ge(cnt_ready, T * GROUPS)
        sp.dma_start(count[:, :, :], count_dram.rearrange("(t p) s -> p t s", p=P)).then_inc(count_landed, 16)

    @block.gpsimd
    def _(pool):
        nc.gpsimd.iota(iota_f[:, :], [[1, NP]], base=0, channel_multiplier=0,
                       allow_small_or_imprecise_dtypes=True).then_inc(iota_done, 1)
        nc.gpsimd.memset(ones[:, :], 1.0).then_inc(consts_done, 1)
        nc.gpsimd.memset(zeros[:, :], 0.0).then_inc(consts_done, 1)
        pool.wait_ge(consts_done, 1)
        nc.gpsimd.affine_select(out=ident[:, :], in_=ones[:, :], pattern=[[-1, P]], compare_op=ALU.is_equal, fill=0.0,
                                base=0, channel_multiplier=1).then_inc(consts_done, 1)

        d = dense[0]

        def first_half(i, b, n):
            if not isinstance(i, int) or i > 0:
                settled(pool, stored[b], 16 * d.pairs(i))
            pool.dma_start(xres[b][0:n, 0:HID], x[bass.ds((2 * i + b) * P, n), 0:HID]).then_inc(res_landed[b], 16)
            settled(pool, res_landed[b], 16 * d.pairs(i + 1))
            settled(pool, product_read[b], d.pairs(i + 1))
            nc.gpsimd.tensor_tensor(xres[b][:, 0:HID], xres[b][:, 0:HID], g[:, bass.ds(2 * i + b, 1), :].rearrange("p a n -> p (a n)"),
                                    ALU.add).then_inc(res_added, 1)
            settled(pool, res_added, d.tiles(2 * i + b + 1))
            pool.dma_start(x1_dram[rows(2 * i + b), 0:HID], xres[b][:, 0:HID]).then_inc(stored[b], 16)

        first_half(0, 0, P)
        first_half(0, 1, P)
        with pool.Fori(1, HT - 1) as i:
            first_half(i, 0, P)
            first_half(i, 1, P)
        first_half(HT - 1, 0, P)
        first_half(HT - 1, 1, N - (T - 1) * P)

        PARTS = 5

        def weight_parts(i, b):
            a = 2 * i + b
            settled(pool, ends_landed[b], 16 * 3 * QW * (i + 1))
            settled(pool, sel_ready, a + 1)
            whole, rest, part = ew[b], ew_rest[b], ew_part[b]
            nc.gpsimd.tensor_copy(part[:, 0, :], whole[:, :]).then_inc(parts_chain, 1)
            settled(pool, parts_chain, PARTS * a + 1)
            nc.gpsimd.tensor_tensor(rest[:, 0, :], whole[:, :], part[:, 0, :], ALU.subtract).then_inc(parts_chain, 1)
            settled(pool, parts_chain, PARTS * a + 2)
            nc.gpsimd.tensor_copy(part[:, 1, :], rest[:, 0, :]).then_inc(parts_chain, 1)
            settled(pool, parts_chain, PARTS * a + 3)
            nc.gpsimd.tensor_tensor(rest[:, 1, :], rest[:, 0, :], part[:, 1, :], ALU.subtract).then_inc(parts_chain, 1)
            settled(pool, parts_chain, PARTS * a + 4)
            nc.gpsimd.tensor_copy(part[:, 2, :], rest[:, 1, :]).then_inc(parts_chain, 1)
            settled(pool, parts_chain, PARTS * a + 5)
            for k in range(3):
                last = nc.gpsimd.tensor_tensor(sel[b][:, 1 + k, :, :], sel[b][:, 0, :, :],
                                               part[:, k, :].unsqueeze(2).to_broadcast([P, QW * CHUNKS, WIN]), ALU.mult)
            last.then_inc(wsel_ready, 1)

        def store_rows(i, b, weights):
            a = 2 * i + b
            settled(pool, counts_copied, a + 1)
            if not isinstance(i, int) or i > 0:
                settled(pool, count_stored[b], 16 * i)
            nc.gpsimd.tensor_copy(count_row[b][:, :], count_f[b][:, :]).then_inc(count_row_ready, 1)
            settled(pool, count_row_ready, a + 1)
            pool.dma_start(count_dram[rows(a), :], count_row[b][:, :]).then_inc(count_stored[b], 16)
            if weights:
                settled(pool, weights_copied, a + 1)
                pool.dma_start(wt_dram[rows(a), :], weight_row[b][:, :]).then_inc(weights_stored[b], 16)

        weight_parts(0, 0)
        weight_parts(0, 1)
        store_rows(0, 0, True)
        weight_parts(1, 0)
        store_rows(0, 1, True)
        with pool.Fori(1, WT_TILES // 2) as i:
            weight_parts(i, 1)
            store_rows(i, 0, True)
            weight_parts(i + 1, 0)
            store_rows(i, 1, True)
        weight_parts(HT - 1, 1)
        store_rows(HT - 1, 0, False)
        store_rows(HT - 1, 1, False)

        pool.wait_ge(complete_ready, 1)
        whole = pool.value_load(complete[0:1, 0:1], min_val=0, max_val=1)
        with pool.If(whole == 0):
            for b in range(2):
                pool.wait_ge(count_stored[b], 16 * HT)
            with pool.Fori(0, T) as a:
                settled(pool, gen_copied, 2 * (a + 1) + 1)
                nc.gpsimd.tensor_copy(count_row[0][:, :], count_f[0][:, :]).then_inc(gen_row_ready, 1)
        pool.sem_inc(built, 1)

        half = [xres[c % 2][:, c // 2 * HID:(c // 2 + 1) * HID] for c in range(4)]

        def load_half(t):
            n = min(P, N - t * P)
            pool.dma_start(half[t % 4][0:n, :], x[t * P:t * P + n, HID:D]).then_inc(half_landed[t % 4], 16)

        for b in range(2):
            pool.wait_ge(stored[b], 16 * d.pairs(HT))
        for t in range(4):
            load_half(t)
        for t in range(T):
            pool.wait_ge(half_landed[t % 4], 16 * (t // 4 + 1))
            pool.wait_ge(sum_read, T * (GATES - 1) + t + 1)
            nc.gpsimd.tensor_tensor(half[t % 4], half[t % 4], g[:, t, :], ALU.add).then_inc(half_added, 1)
            pool.wait_ge(half_added, t + 1)
            pool.dma_start(x1_dram[t * P:(t + 1) * P, HID:D], half[t % 4]).then_inc(half_stored[t % 2], 16)
            if 1 <= t < T - 3:
                pool.wait_ge(half_stored[(t - 1) % 2], 16 * ((t - 1) // 2 + 1))
                load_half(t + 3)

        d = dense[1]

        def load1(i, b):
            pool.dma_start(xres[b][:, :], x1_dram[rows(2 * i + b), :]).then_inc(res_landed[b], 16)

        def store1(i, b):
            t = 2 * i + b
            settled(pool, product_read[b], d.pairs(i + 1))
            nc.gpsimd.tensor_tensor(xres[b][:, :], xres[b][:, :], row_all[:, :], ALU.add).then_inc(res_added, 1)
            settled(pool, res_added, d.tiles(t + 1))
            pool.dma_start(x2_dram[rows(t), :], xres[b][:, :]).then_inc(stored[b], 16)
            settled(pool, stored[b], 16 * d.pairs(i + 1))

        pool.wait_ge(bias1_landed, 16)
        for b in range(2):
            pool.wait_ge(half_stored[b], 16 * HT)
            load1(0, b)
        with pool.Fori(0, HT - 1) as i:
            for b in range(2):
                store1(i, b)
                load1(i + 1, b)
        store1(HT - 1, 0)
        store1(HT - 1, 1)

        def load2(i, b):
            pool.dma_start(xres[b][:, :], x2_dram[rows(2 * i + b), :]).then_inc(agg_landed[b], 16)

        def store2(i, b):
            settled(pool, agg_read, 2 * GRP + 2 * i + b + 1)
            pool.dma_start(x3_dram[rows(2 * i + b), :], xres[b][:, :]).then_inc(agg_stored[b], 16)
            settled(pool, agg_stored[b], 16 * (i + 1))

        load2(0, 0)
        load2(0, 1)
        with pool.Fori(0, HT - 1) as i:
            for b in range(2):
                store2(i, b)
                load2(i + 1, b)
        store2(HT - 1, 0)
        store2(HT - 1, 1)

        pool.dma_start(att_all[:, :], att.rearrange("a n -> (a n)").partition_broadcast(P)).then_inc(att_landed, 16)
        pool.wait_ge(al_ready, T)

        def load3(i, b):
            pool.dma_start(xres[b][:, :], x3_dram[rows(2 * i + b), :]).then_inc(gat_landed[b], 16)

        def store3(i, b, n):
            settled(pool, gat_added, 2 * i + b + 1)
            pool.dma_start(out[bass.ds((2 * i + b) * P, n), :], xres[b][0:n, :]).then_inc(gat_stored[b], 16)
            settled(pool, gat_stored[b], 16 * (i + 1))

        load3(0, 0)
        load3(0, 1)
        with pool.Fori(0, HT - 1) as i:
            for b in range(2):
                store3(i, b, P)
                load3(i + 1, b)
        store3(HT - 1, 0, P)
        store3(HT - 1, 1, N - (T - 1) * P)

    COUNTS = ps[:, 0:NP]
    WEIGHTS = ps[:, 3 * BANK:3 * BANK + D]
    COUNT_T = ps[:, 5 * BANK:5 * BANK + NP]
    BLOCKS = [(0, BANK), (BANK, 2 * BANK), (2 * BANK, NP)]
    SUMS = [ps[:, k * BANK:(k + 1) * BANK] for k in range(HT)]
    U_ALL = ps[:, HT * BANK:HT * BANK + HALF]
    AGG2 = [[ps[:, (4 * c + 2 * j) * BANK:(4 * c + 2 * j + 2) * BANK] for j in range(GRP)] for c in range(2)]
    AGG = [ps[:, 2 * j * BANK:(2 * j + 2) * BANK] for j in range(GRP)]
    DEN = [ps[:, (4 + j) * BANK:(4 + j) * BANK + 2] for j in range(GRP)]
    AL_ALL = ps[:, 5 * BANK:5 * BANK + NP]

    def use_of(m):
        return m % 2, m // 2

    @block.scalar
    def _(act):
        dense_act(act, dense[0], lambda i, b: None)

        def take_rows(i, b, weights):
            a = 2 * i + b
            ring, use = use_of(CHUNKS * b + CHUNKS - 1)
            act.wait_ge(count_transposed[b], i)
            act.wait_ge(count_row_ready, 2 * i)
            if weights:
                act.wait_ge(counts_ready, a + 1)
            else:
                act.wait_ge(onehot_used[ring], CHUNKS * i + use + 1)
            nc.scalar.activation(count_f[b][:, :], COUNTS, ACT.Copy,
                                 accum_out=deg[:, bass.ds(a, 1)]).then_inc(counts_copied, 1)
            if weights:
                act.wait_ge(onehot_used[ring], CHUNKS * i + use + 1)
                act.wait_ge(weights_stored[b], 16 * i)
                nc.scalar.activation(weight_row[b][:, :], WEIGHTS, ACT.Copy).then_inc(weights_copied, 1)
            act.wait_ge(count_transposed[b], i + 1)
            nc.scalar.activation(countT[:, :, bass.ds(a * P, P)], COUNT_T.rearrange("p (s n) -> p s n", n=P),
                                 ACT.Copy).then_inc(countT_ready, 1)

        take_rows(0, 0, True)
        take_rows(0, 1, True)
        with act.Fori(1, WT_TILES // 2) as i:
            take_rows(i, 0, True)
            take_rows(i, 1, True)
        take_rows(HT - 1, 0, False)
        take_rows(HT - 1, 1, False)

        act.wait_ge(complete_ready, 1)
        whole = act.value_load(complete[0:1, 0:1], min_val=0, max_val=1)
        with act.If(whole == 0):
            act.wait_ge(count_row_ready, T)
            for b in range(2):
                act.wait_ge(weights_stored[b], 16 * WT_TILES // 2)
            act.sem_inc(gen_copied, 1)
            act.sem_inc(gen_countT_ready, 1)
            with act.Fori(0, T) as a:
                act.wait_ge(gen_summed, a + 1)
                act.wait_ge(gen_stored, 32 * a + 1)
                nc.scalar.activation(count_f[0][:, :], COUNTS, ACT.Copy,
                                     accum_out=deg[:, bass.ds(a, 1)]).then_inc(gen_copied, 1)
                nc.scalar.activation(weight_row[0][:, :], WEIGHTS, ACT.Copy).then_inc(gen_copied, 1)
                act.wait_ge(gen_transposed, a + 1)
                nc.scalar.activation(countT[:, :, bass.ds(a * P, P)], COUNT_T.rearrange("p (s n) -> p s n", n=P),
                                     ACT.Copy).then_inc(gen_countT_ready, 1)
            act.wait_ge(gen_countT_ready, T + 1)
        act.sem_inc(built, 1)

        act.wait_ge(norm_chain, 2)
        nc.scalar.activation(norm_root[:, :, :], norm[:, :, :], ACT.Sqrt).then_inc(norm_root_ready, 1)

        def g_split(t):
            nc.scalar.activation(g_hi[:, t, :], g[:, t, :], ACT.Identity,
                                 scale=dis[:, 0, t:t + 1]).then_inc(g_hi_ready, 1)

        def tanh(q, r, h, s):
            k = s % SLOTS
            act.wait_ge(mask_used[k], 2 * q + s // SLOTS)
            if s == 0:
                act.wait_ge(u_spread, q + 1)
            if h == 0:
                act.wait_ge(gates_ready, T * r + s + 1)
            nc.scalar.activation(mask[k][:, :], U_ALL, ACT.Tanh, bias=v[:, s:s + 1]).then_inc(tanh_ready, 1)

        def mask_hi_of(q, s):
            k = s % SLOTS
            act.wait_ge(mask_ready, T * q + s + 1)
            nc.scalar.activation(mask_hi[k][:, :], mask[k][:, :], ACT.Copy).then_inc(mask_hi_ready, 1)

        def half_act(q, r, h, split, last=False):
            for s in range(T):
                if s < T - 1:
                    mask_hi_of(q, s + 1)
                elif not last:
                    mask_hi_of(q + 1, 0)
                if s < T - TANH_LEAD:
                    tanh(q, r, h, s + TANH_LEAD)
                elif not last:
                    tanh(q + 1, r + h, 1 - h, s + TANH_LEAD - T)
                if isinstance(q, int) and q == 0 and s + 2 < T:
                    g_split(s + 2)
                if last:
                    if s >= T - KT:
                        split_act(act, dense[1], [s - (T - KT)])
                    if s in (HT, HT + 2):
                        root_act(act, dense[1], 0, (s - HT) // 2)
                    if s in (HT + 1, HT + 3):
                        h_act(act, dense[1], 0, (s - HT) // 2)
                if not split:
                    continue
                if h == 1 and s >= HT:
                    t = s - HT
                    act.wait_ge(sum_read, HT * q - HT + t + 1)
                    act.wait_ge(mask_used[t % SLOTS], 2 * q + 1)
                    g_split(t)
                if h == 0 and 1 <= s < 1 + HT:
                    act.wait_ge(sum_read, HT * q - HT + s)
                    g_split(s - 1 + HT)

        act.wait_ge(dis_ready, 1)
        for b in range(2):
            act.wait_ge(product_ready[b], dense[0].pairs(HT))
            act.wait_ge(product_read[b], dense[0].pairs(HT))
        g_split(0)
        g_split(1)
        for s in range(TANH_LEAD):
            tanh(0, 0, 0, s)
        mask_hi_of(0, 0)
        half_act(0, 0, 0, False)
        with act.Fori(0, GATES - 1) as r:
            half_act(2 * r + 1, r, 1, True)
            half_act(2 * r + 2, r + 1, 0, True)
        half_act(2 * GATES - 1, GATES - 1, 1, False, last=True)

        transposed_act(act, dense[1], 0, 0)

        dense_act(act, dense[1], lambda i, b: None, dense[2])

        def y_act(d, i, b):
            t = 2 * i + b
            act.wait_ge(product_ready[b], d.pairs(i + 1))
            if d.n == 2:
                nc.scalar.activation(y_all[:, bass.ds(t, 1), 0, :].rearrange("p a n -> p (a n)"), PRODUCT[b], ACT.Identity,
                                     scale=dis[:, 1, bass.ds(t, 1)]).then_inc(y_hi_ready, 1)
            else:
                nc.scalar.activation(y_all[:, bass.ds(t, 1), 0, :].rearrange("p a n -> p (a n)"), PRODUCT[b],
                                     ACT.Copy).then_inc(y_hi_ready, 1)

        dense_act(act, dense[2], lambda i, b: y_act(dense[2], i, b))

        def counts_act(grp, s):
            act.wait_ge(cnt_used[s % SLOTS], 2 * grp + s // SLOTS)
            nc.scalar.activation(cnt2[s % SLOTS][:, :], countT[:, s, bass.ds(grp * GC, GC)],
                                 ACT.Copy).then_inc(cnt_ready, 1)

        for b in range(2):
            act.wait_ge(product_ready[b], dense[2].pairs(HT))
        act.wait_ge(loops_added, T)
        for grp in range(2):
            for s in range(T):
                counts_act(grp, s)
        split_act(act, dense[3], range(KT))
        with act.Fori(2, GROUPS - 1) as grp:
            for s in range(T):
                counts_act(grp, s)
        for s in range(T):
            counts_act(GROUPS - 1, s)
            if s == SLOTS - 1:
                for b in range(2):
                    root_act(act, dense[3], 0, b)
                    h_act(act, dense[3], 0, b)
        transposed_act(act, dense[3], 0, 0)

        dense_act(act, dense[3], lambda i, b: y_act(dense[3], i, b))
        act.wait_ge(al_diag_used, T)
        for b in range(2):
            act.wait_ge(product_ready[b], dense[3].pairs(HT))
        nc.scalar.activation(al_all[:, :], AL_ALL, ACT.Copy).then_inc(al_all_ready, 1)

        def exps(grp, s):
            act.wait_ge(leaky_ready, T * grp + s + 1)
            nc.scalar.activation(att_e[s][:, :], att_e[s][:, :], ACT.Exp, scale=-1.0).then_inc(exp_ready, 1)

        def att_hi_of(grp, s):
            act.wait_ge(att_e_ready, T * grp + s + 1)
            nc.scalar.activation(att_hi[s][:, :], att_e[s][:, :], ACT.Copy).then_inc(att_hi_ready, 1)

        def gat_take(grp, j):
            if j == 0:
                act.wait_ge(gat_ready, grp + 1)
            else:
                act.wait_ge(att_used, T * grp + T)
            nc.scalar.activation(rden[:, j, 0:1], DEN[j][:, 0:1], ACT.Copy).then_inc(den_taken, 1)
            nc.scalar.activation(xin[j][:, :], AGG[j], ACT.Copy).then_inc(gat_read, 1)

        def elu_act(grp, j):
            act.wait_ge(gat_neg_ready, GRP * grp + j + 1)
            nc.scalar.activation(elu_neg[j][:, :], elu_neg[j][:, :], ACT.Exp).then_inc(gat_exp_ready, 1)
            nc.scalar.activation(xin[j][:, :], xin[j][:, :], ACT.Relu, scale=rden[:, j, 1:2]).then_inc(gat_pos_ready, 1)

        def attention_act(grp, first, last):
            for s in range(T):
                if s < T - 1:
                    exps(grp, s + 1)
                elif not last:
                    exps(grp + 1, 0)
                att_hi_of(grp, s)
                if not first and s == 2:
                    gat_take(grp - 1, 0)
                    gat_take(grp - 1, 1)
                if not first and s in (5, 6):
                    elu_act(grp - 1, s - 5)

        exps(0, 0)
        attention_act(0, True, False)
        with act.Fori(1, GROUPS - 1) as grp:
            attention_act(grp, False, False)
        attention_act(GROUPS - 1, False, True)
        for j in range(GRP):
            gat_take(GROUPS - 1, j)
        for j in range(GRP):
            elu_act(GROUPS - 1, j)

    @block.vector
    def _(dve):
        dve.wait_ge(iota_done, 1)
        dve.wait_ge(dst_landed, 16)
        nc.vector.tensor_copy(dst_f[0:EP, :], dst_raw[0:EP, :]).then_inc(below_chain, 1)
        dve.wait_ge(below_chain, 1)
        nc.vector.tensor_tensor(below[0:EP, :, :], dst_f[0:EP, :].unsqueeze(1).to_broadcast([EP, WINDOWS, EC]),
                                iota_f[0:EP, :].rearrange("p (w i) -> p w i", i=WIN)[:, :, 0:1].to_broadcast([EP, WINDOWS, EC]),
                                ALU.is_lt).then_inc(below_chain, 1)
        dve.wait_ge(below_chain, 2)
        nc.vector.tensor_reduce(below_n[0:EP, :], below[0:EP, :, :], AX_X, ALU.add).then_inc(below_chain, 1)
        dve.wait_ge(below_summed, 1)
        nc.vector.tensor_scalar(starts[0:1, :], ps[0:1, 7 * BANK:7 * BANK + WINDOWS], float(E - CAP), None,
                                ALU.min).then_inc(starts_ready, 1)
        nc.vector.tensor_copy(iota_h[:, :], iota_f[:, :]).then_inc(below_chain, 1)
        dve.wait_ge(consts_done, 3)
        nc.vector.tensor_copy(ones_r[:, :], ones[:, 0:2]).then_inc(below_chain, 1)

        d0 = dense[0]

        def x1(i, b):
            dve.wait_ge(product_ready[b], d0.pairs(i + 1))
            nc.vector.tensor_tensor(g[:, bass.ds(2 * i + b, 1), :].rearrange("p a n -> p (a n)"), PRODUCT[b][:, 0:HID],
                                    b1_all[:, :], ALU.add).then_inc(product_read[b], 1)

        dve.wait_ge(consts_landed, 32)
        dense_dve(dve, d0, x1)

        def select(i, b):
            a = 2 * i + b
            dve.wait_ge(ends_landed[b], 16 * 3 * QW * (i + 1))
            nc.vector.tensor_copy(ends[b][:, :, :], ends_raw[b][:, :, :]).then_inc(ends_ready, 1)
            dve.wait_ge(ends_ready, a + 1)
            nc.vector.tensor_tensor(
                sel[b][:, 0, :, :].rearrange("p (j c) i -> p j c i", c=CHUNKS),
                ends[b][:, 1, :].rearrange("p (j c) -> p j c", c=CHUNKS).unsqueeze(3).to_broadcast([P, QW, CHUNKS, WIN]),
                iota_f[:, bass.ds(a * P, P)].rearrange("p (j i) -> p j i", i=WIN).unsqueeze(2).to_broadcast([P, QW, CHUNKS, WIN]),
                ALU.is_equal).then_inc(sel_ready, 1)

        def onehots(i, b, nxt):
            for c in range(CHUNKS):
                r, n = use_of(CHUNKS * b + c)
                dve.wait_ge(onehot_used[r], CHUNKS * i + n)
                for j in range(QW):
                    last = nc.vector.tensor_scalar(onehot[r][j][:, :], iota_h[:, :], ends[b][:, 0, j * CHUNKS + c:j * CHUNKS + c + 1],
                                                   None, ALU.is_equal)
                last.then_inc(onehot_ready, 1)
                if c == 2 and nxt is not None:
                    select(*nxt)

        dve.wait_ge(below_chain, 5)
        select(0, 0)
        onehots(0, 0, (0, 1))
        onehots(0, 1, (1, 0))
        with dve.Fori(1, HT - 1) as i:
            onehots(i, 0, (i, 1))
            onehots(i, 1, (i + 1, 0))
        onehots(HT - 1, 0, (HT - 1, 1))
        onehots(HT - 1, 1, None)

        def gates(t, count):
            if not isinstance(count, int) or count > 0:
                dve.wait_ge(gates_ready, count)
            nc.vector.tensor_tensor_reduce(gate_scratch[:, :], g[:, t, :], gw[:, 0:HID], 1.0, 0.0, ALU.mult, ALU.add,
                                           u[:, t:t + 1]).then_inc(gate_chain, 1)
            dve.wait_ge(gate_chain, 2 * count + 1)
            nc.vector.tensor_scalar(diag[t % HT][:, :], ident[:, :], u[:, t:t + 1], None, ALU.mult).then_inc(gate_chain, 1)
            nc.vector.tensor_tensor_reduce(gate_scratch[:, :], g[:, t, :], gw[:, HID:2 * HID], 1.0, gb_col[:, 0:1], ALU.mult, ALU.add,
                                           v[:, t:t + 1]).then_inc(gates_ready, 1)

        def g_rest(t, done):
            dve.wait_ge(g_hi_ready, done + 1)
            nc.vector.scalar_tensor_tensor(g_lo[:, t, :], g[:, t, :], dis[:, 0, t:t + 1], g_hi[:, t, :].bitcast(F32),
                                           ALU.mult, ALU.subtract).then_inc(g_lo_ready, 1)

        dve.wait_ge(gw_landed, 16)
        nc.vector.tensor_copy(gb_col[:, :], gb[:, 0:1]).then_inc(gb_chain, 1)
        dve.wait_ge(gb_chain, 1)
        for t in range(HT):
            gates(t, t)

        dve.wait_ge(counts_copied, T)
        nc.vector.reduce_sum(captured[:, :], deg[:, :], AX_X).then_inc(captured_ready, 1)
        dve.wait_ge(captured_summed, 1)
        nc.vector.tensor_scalar(complete[:, :], ps[:, 0:1], float(E), None, ALU.is_equal).then_inc(complete_ready, 1)
        dve.wait_ge(complete_ready, 1)
        whole = dve.value_load(complete[0:1, 0:1], min_val=0, max_val=1)
        with dve.If(whole == 0):
            dsel = sel[0][:, :, :, :].rearrange("p k a i -> p k (a i)").rearrange("p k (c m) -> p k c m", m=P)
            STEPS = 8
            with dve.Fori(0, T) as a:
                with dve.Fori(0, GENERAL_CHUNKS) as c:
                    n = a * GENERAL_CHUNKS + c
                    dve.wait_ge(gen_landed, 48 * (n + 1))
                    dve.wait_ge(gen_used, n + 1)
                    nc.vector.tensor_copy(ends[0][0:EP, :, 0:CHUNKS], ends_raw[0][0:EP, :, 0:CHUNKS]).then_inc(gen_chain, 1)
                    nc.vector.tensor_copy(ew_part[0][0:EP, 0, 0:CHUNKS], ew[0][0:EP, 0:CHUNKS]).then_inc(gen_chain, 1)
                    dve.wait_ge(gen_chain, STEPS * n + 2)
                    nc.vector.tensor_tensor(ew_rest[0][0:EP, 0, 0:CHUNKS], ew[0][0:EP, 0:CHUNKS], ew_part[0][0:EP, 0, 0:CHUNKS],
                                            ALU.subtract).then_inc(gen_chain, 1)
                    dve.wait_ge(gen_chain, STEPS * n + 3)
                    nc.vector.tensor_copy(ew_part[0][0:EP, 1, 0:CHUNKS], ew_rest[0][0:EP, 0, 0:CHUNKS]).then_inc(gen_chain, 1)
                    dve.wait_ge(gen_chain, STEPS * n + 4)
                    nc.vector.tensor_tensor(ew_rest[0][0:EP, 1, 0:CHUNKS], ew_rest[0][0:EP, 0, 0:CHUNKS], ew_part[0][0:EP, 1, 0:CHUNKS],
                                            ALU.subtract).then_inc(gen_chain, 1)
                    dve.wait_ge(gen_chain, STEPS * n + 5)
                    nc.vector.tensor_copy(ew_part[0][0:EP, 2, 0:CHUNKS], ew_rest[0][0:EP, 1, 0:CHUNKS]).then_inc(gen_chain, 1)
                    nc.vector.tensor_tensor(
                        dsel[0:EP, 0], ends[0][0:EP, 1, 0:CHUNKS].unsqueeze(2).to_broadcast([EP, CHUNKS, P]),
                        iota_f[0:EP, bass.ds(a * P, P)].unsqueeze(1).to_broadcast([EP, CHUNKS, P]),
                        ALU.is_equal).then_inc(gen_chain, 1)
                    dve.wait_ge(gen_chain, STEPS * n + 7)
                    for k in range(3):
                        last = nc.vector.tensor_tensor(dsel[0:EP, 1 + k], dsel[0:EP, 0],
                                                       ew_part[0][0:EP, k, 0:CHUNKS].unsqueeze(2).to_broadcast([EP, CHUNKS, P]),
                                                       ALU.mult)
                    last.then_inc(gen_chain, 1)
                    for q in range(CHUNKS):
                        last = nc.vector.tensor_scalar(onehot[q // QW][q % QW][0:EP, :], iota_h[0:EP, :], ends[0][0:EP, 0, q:q + 1],
                                                       None, ALU.is_equal)
                    last.then_inc(gen_ready, 1)
            dve.wait_ge(gen_copied, 2 * T + 1)
            dve.wait_ge(gen_countT_ready, T + 1)

        dve.wait_ge(countT_ready, T)
        nc.vector.tensor_scalar(norm[:, 0, :], deg[:, :], 1.0, None, ALU.max).then_inc(norm_chain, 1)
        nc.vector.tensor_scalar(norm[:, 1, :], deg[:, :], 1.0, None, ALU.add).then_inc(norm_chain, 1)
        dve.wait_ge(norm_root_ready, 1)
        nc.vector.reciprocal(dis[:, :, :], norm_root[:, :, :]).then_inc(norm_chain, 1)
        dve.wait_ge(norm_chain, 3)
        nc.vector.tensor_tensor(norm_step[:, :, :], dis[:, :, :], dis[:, :, :], ALU.mult).then_inc(norm_chain, 1)
        dve.wait_ge(norm_chain, 4)
        nc.vector.tensor_tensor(norm_step[:, :, :], norm_step[:, :, :], norm[:, :, :], ALU.mult).then_inc(norm_chain, 1)
        dve.wait_ge(norm_chain, 5)
        nc.vector.tensor_scalar(norm_step[:, :, :], norm_step[:, :, :], -0.5, 1.5, ALU.mult, ALU.add).then_inc(norm_chain, 1)
        dve.wait_ge(norm_chain, 6)
        nc.vector.tensor_tensor(dis[:, :, :], dis[:, :, :], norm_step[:, :, :], ALU.mult).then_inc(dis_ready, 1)
        dve.wait_ge(dis_ready, 1)

        def mask_of(q, h, s):
            k = s % SLOTS
            dve.wait_ge(tanh_ready, T * q + s + 1)
            nc.vector.tensor_tensor(mask[k][:, :], mask[k][:, :], countT[:, s, h * HALF:(h + 1) * HALF], ALU.mult).then_inc(mask_ready, 1)

        def mask_rest(q, s):
            k = s % SLOTS
            dve.wait_ge(mask_hi_ready, T * q + s + 1)
            nc.vector.tensor_tensor(mask_lo[k][:, :], mask[k][:, :], mask_hi[k][:, :].bitcast(F32), ALU.subtract).then_inc(mask_lo_ready, 1)

        def take_sums(q, h):
            for dd in range(HT):
                t = HT * h + dd
                if dd < HT - 1:
                    dve.wait_ge(sum_ready, (HT - 1) * q + dd + 1)
                else:
                    dve.wait_ge(mask_used[SLOTS - 1], 2 * q + 2)
                nc.vector.scalar_tensor_tensor(g[:, t, :], SUMS[dd], dis[:, 0, t:t + 1], g[:, t, :],
                                               ALU.mult, ALU.add).then_inc(sum_read, 1)

        def half_dve(q, h, nxt, last=False):
            if nxt is not None:
                dve.wait_ge(gw_landed, 16 * (nxt + 1))
                if h == 1:
                    nc.vector.tensor_copy(gb_col[:, :], gb[:, bass.ds(nxt, 1)]).then_inc(gb_chain, 1)
            for s in range(T):
                if s < T - 2:
                    mask_of(q, h, s + 2)
                elif not last:
                    mask_of(q + 1, 1 - h, s + 2 - T)
                mask_rest(q, s)
                if last:
                    if s >= T - KT:
                        split_dve(dve, dense[1], [s - (T - KT)])
                    if s in (HT, HT + 2):
                        stats_dve(dve, dense[1], 0, (s - HT) // 2)
                    if s in (HT + 1, HT + 3):
                        scale_dve(dve, dense[1], 0, (s - HT) // 2)
                if s == 0 and not (isinstance(q, int) and q == 0):
                    take_sums(q - 1, 1 - h)
                if isinstance(q, int) and q == 0:
                    if s < HT:
                        if s == 0:
                            dve.wait_ge(u_spread, 1)
                        gates(s + HT, s + HT)
                    if s + 2 < T:
                        g_rest(s + 2, s + 2)
                if nxt is None:
                    continue
                if 1 <= s < 1 + HT:
                    t = s - 1 + (HT if h == 0 else 0)
                    if s == 1:
                        dve.wait_ge(sum_read, HT * q)
                        dve.wait_ge(gb_chain, nxt + 1)
                        dve.wait_ge(u_spread, q + 1)
                    gates(t, T * nxt + t)
                    if h == 0:
                        g_rest(t, T * nxt + t)
                if h == 1 and s >= HT:
                    g_rest(s - HT, T * nxt + s - HT)

        g_rest(0, 0)
        g_rest(1, 1)
        mask_of(0, 0, 0)
        mask_of(0, 0, 1)
        half_dve(0, 0, None)
        with dve.Fori(0, GATES - 1) as r:
            half_dve(2 * r + 1, 1, r + 1)
            half_dve(2 * r + 2, 0, r + 1)
        half_dve(2 * GATES - 1, 1, None, last=True)
        transposed_dve(dve, dense[1], 0, 0)
        take_sums(2 * GATES - 1, 1)

        d1 = dense[1]

        def residual(i, b):
            dve.wait_ge(res_landed[b], 16 * d1.pairs(i + 1))
            dve.wait_ge(product_ready[b], d1.pairs(i + 1))
            nc.vector.tensor_tensor(xres[b][:, :], PRODUCT[b], xres[b][:, :], ALU.add).then_inc(product_read[b], 1)

        for t in range(T):
            nc.vector.tensor_tensor(countT[:, t, t * P:(t + 1) * P], countT[:, t, t * P:(t + 1) * P], ident[:, :],
                                    ALU.add).then_inc(loops_added, 1)
        dense_dve(dve, d1, residual, dense[2])

        d2 = dense[2]

        def y_rest(i, b):
            t = 2 * i + b
            dve.wait_ge(y_hi_ready, t + 1)
            nc.vector.scalar_tensor_tensor(y_all[:, bass.ds(t, 1), 1, :].rearrange("p a n -> p (a n)"), PRODUCT[b], dis[:, 1, bass.ds(t, 1)],
                                           y_all[:, bass.ds(t, 1), 0, :].rearrange("p a n -> p (a n)").bitcast(F32),
                                           ALU.mult, ALU.subtract).then_inc(product_read[b], 1)

        dense_dve(dve, d2, y_rest)

        def gcn_out(grp, j):
            t = GRP * grp + j
            sums = AGG2[grp % 2][j]
            if j == 0:
                dve.wait_ge(agg_ready, grp + 1)
            else:
                dve.wait_ge(cnt_used[SLOTS - 1], 2 * grp + 2)
            nc.vector.scalar_tensor_tensor(sums, sums, dis[:, 1, t:t + 1], row_all[:, :], ALU.mult, ALU.add).then_inc(agg_chain, 1)
            dve.wait_ge(agg_chain, t + 1)
            dve.wait_ge(agg_landed[j], 16 * (grp + 1))
            nc.vector.scalar_tensor_tensor(xres[j][:, :], sums, 0.0, xres[j][:, :], ALU.max, ALU.add).then_inc(agg_read, 1)

        dve.wait_ge(b2_landed, 16)
        dve.sem_inc(agg_read, 2 * GRP)
        for grp in range(GROUPS):
            if grp == 2:
                split_dve(dve, dense[3], range(KT))
            if grp == GROUPS - 1:
                for b in range(2):
                    stats_dve(dve, dense[3], 0, b)
                    scale_dve(dve, dense[3], 0, b)
                transposed_dve(dve, dense[3], 0, 0)
            for j in range(GRP):
                gcn_out(grp, j)

        d3 = dense[3]

        def scores(i, b):
            t = 2 * i + b
            dve.wait_ge(y_hi_ready, T + t + 1)
            nc.vector.tensor_tensor_reduce(SCRATCH, PRODUCT[b], att_all[:, 0:D], 1.0, 0.0, ALU.mult, ALU.add,
                                           al_col[b][:, 0:1]).then_inc(al_chain, 1)
            dve.wait_ge(al_chain, 2 * t + 1)
            nc.vector.tensor_tensor_reduce(SCRATCH, PRODUCT[b], att_all[:, D:2 * D], 1.0, 0.0, ALU.mult, ALU.add,
                                           al_col[b][:, 1:2]).then_inc(al_chain, 1)
            nc.vector.tensor_tensor(y_all[:, bass.ds(t, 1), 1, :].rearrange("p a n -> p (a n)"), PRODUCT[b],
                                    y_all[:, bass.ds(t, 1), 0, :].rearrange("p a n -> p (a n)").bitcast(F32),
                                    ALU.subtract).then_inc(product_read[b], 1)
            dve.wait_ge(al_chain, 2 * t + 2)
            nc.vector.tensor_copy(al[:, bass.ds(t, 1)], al_col[b][:, 0:1]).then_inc(al_copied, 1)
            nc.vector.tensor_copy(ar[:, bass.ds(t, 1)], al_col[b][:, 1:2]).then_inc(al_ready, 1)

        dve.wait_ge(att_landed, 16)
        dense_dve(dve, d3, scores)
        dve.wait_ge(al_copied, T)
        dve.wait_ge(al_ready, T)
        for b in range(2):
            dve.wait_ge(product_ready[b], d3.pairs(HT))
        for t in range(T):
            if t >= 2:
                dve.wait_ge(al_diag_used, t - 1)
            nc.vector.tensor_scalar(al_diag[t % 2][:, :], ident[:, :], al[:, t:t + 1], None, ALU.mult).then_inc(al_diag_ready, 1)

        def logits(grp, s):
            if not isinstance(grp, int) or grp > 0:
                dve.wait_ge(att_used, T * (grp - 1) + s + 1)
            nc.vector.tensor_scalar(att_e[s][:, :], al_all[:, bass.ds(grp * GC, GC)], ar[:, s:s + 1], None, ALU.add).then_inc(logit_ready, 1)
            dve.wait_ge(logit_ready, T * grp + s + 1)
            nc.vector.scalar_tensor_tensor(att_e[s][:, :], att_e[s][:, :], SLOPE, att_e[s][:, :], ALU.mult, ALU.max).then_inc(leaky_ready, 1)

        def att_of(grp, s):
            dve.wait_ge(exp_ready, T * grp + s + 1)
            nc.vector.tensor_tensor(att_e[s][:, :], att_e[s][:, :], count[:, s, bass.ds(grp * GC, GC)], ALU.mult).then_inc(att_e_ready, 1)

        def att_rest(grp, s):
            dve.wait_ge(att_hi_ready, T * grp + s + 1)
            nc.vector.tensor_tensor(att_lo[s][:, :], att_e[s][:, :], att_hi[s][:, :].bitcast(F32), ALU.subtract).then_inc(att_lo_ready, 1)

        GAT_STEPS = 2

        def elu_start(grp, j):
            t = GRP * grp + j
            dve.wait_ge(den_taken, t + 1)
            nc.vector.tensor_scalar(rden[:, j, 0:1], rden[:, j, 0:1], EPS_GAT, None, ALU.add).then_inc(gat_chain, 1)
            dve.wait_ge(gat_chain, GAT_STEPS * t + 1)
            nc.vector.reciprocal(rden[:, j, 1:2], rden[:, j, 0:1]).then_inc(gat_chain, 1)
            dve.wait_ge(gat_chain, GAT_STEPS * t + 2)
            dve.wait_ge(gat_read, t + 1)
            nc.vector.tensor_scalar(elu_neg[j][:, :], xin[j][:, :], rden[:, j, 1:2], 0.0, ALU.mult, ALU.min).then_inc(gat_neg_ready, 1)

        def elu_end(grp, j):
            t = GRP * grp + j
            dve.wait_ge(gat_landed[j], 16 * (grp + 1))
            dve.wait_ge(gat_exp_ready, t + 1)
            nc.vector.scalar_tensor_tensor(elu_neg[j][:, :], elu_neg[j][:, :], -1.0, xres[j][:, :], ALU.add, ALU.add).then_inc(elu_added, 1)
            dve.wait_ge(elu_added, t + 1)
            dve.wait_ge(gat_pos_ready, t + 1)
            nc.vector.tensor_tensor(xres[j][:, :], elu_neg[j][:, :], xin[j][:, :], ALU.add).then_inc(gat_added, 1)

        def attention_dve(grp, first, last):
            for s in range(T):
                if s < T - 2:
                    logits(grp, s + 2)
                elif not last:
                    logits(grp + 1, s + 2 - T)
                if s < T - 1:
                    att_of(grp, s + 1)
                elif not last:
                    att_of(grp + 1, 0)
                att_rest(grp, s)
                if not first and s == 4:
                    elu_start(grp - 1, 0)
                    elu_start(grp - 1, 1)
                if not first and s in (7, 8):
                    elu_end(grp - 1, s - 7)

        dve.wait_ge(count_landed, 16)
        dve.wait_ge(al_all_ready, 1)
        logits(0, 0)
        logits(0, 1)
        att_of(0, 0)
        attention_dve(0, True, False)
        with dve.Fori(1, GROUPS - 1) as grp:
            attention_dve(grp, False, False)
        attention_dve(GROUPS - 1, False, True)
        for j in range(GRP):
            elu_start(GROUPS - 1, j)
        for j in range(GRP):
            elu_end(GROUPS - 1, j)

    @block.tensor
    def _(pe):
        pe.wait_ge(consts_done, 3)
        pe.wait_ge(below_chain, 3)
        nc.tensor.matmul(ps[0:1, 7 * BANK:7 * BANK + WINDOWS], ones[0:EP, 0:1], below_n[0:EP, :],
                         start=True, stop=True).then_inc(below_summed, 1)
        dense_pe(pe, dense[0])
        for b in range(2):
            pe.wait_ge(product_read[b], dense[0].pairs(HT))

        def rows_pe(i, b, weights):
            a = 2 * i + b
            pe.wait_ge(wsel_ready, a + 1)
            pe.wait_ge(counts_copied, a)
            for c in range(CHUNKS):
                r, n = use_of(CHUNKS * b + c)
                pe.wait_ge(onehot_ready, CHUNKS * a + c + 1)
                for lo, hi in BLOCKS:
                    for j in range(QW):
                        last = nc.tensor.matmul(COUNTS[j * WIN:(j + 1) * WIN, lo:hi], sel[b][:, 0, j * CHUNKS + c, :],
                                                onehot[r][j][:, lo:hi], start=(c == 0), stop=(c == CHUNKS - 1))
                if weights:
                    if c == CHUNKS - 1:
                        last.then_inc(counts_ready, 1)
                    if c == 0:
                        pe.wait_ge(weights_copied, a)
                    for lo, hi in BLOCKS[:2]:
                        for k in range(3):
                            for j in range(QW):
                                last = nc.tensor.matmul(WEIGHTS[j * WIN:(j + 1) * WIN, lo:hi], sel[b][:, 1 + k, j * CHUNKS + c, :],
                                                        onehot[r][j][:, lo:hi], start=(c == 0 and k == 0),
                                                        stop=(c == CHUNKS - 1 and k == 2))
                last.then_inc(onehot_used[r], 1)
            pe.wait_ge(counts_copied, a + 1)
            pe.wait_ge(countT_ready, a)
            for s in range(T):
                last = nc.tensor.transpose(COUNT_T[:, s * P:(s + 1) * P], count_f[b][:, s * P:(s + 1) * P], ident[:, :])
            last.then_inc(count_transposed[b], 1)

        rows_pe(0, 0, True)
        rows_pe(0, 1, True)
        with pe.Fori(1, WT_TILES // 2) as i:
            rows_pe(i, 0, True)
            rows_pe(i, 1, True)
        rows_pe(HT - 1, 0, False)
        rows_pe(HT - 1, 1, False)
        pe.wait_ge(captured_ready, 1)
        nc.tensor.matmul(ps[:, 0:1], ones[:, :], captured[:, :], start=True, stop=True).then_inc(captured_summed, 1)

        pe.wait_ge(complete_ready, 1)
        whole = pe.value_load(complete[0:1, 0:1], min_val=0, max_val=1)
        with pe.If(whole == 0):
            pe.sem_inc(gen_used, 1)
            dsel = sel[0][:, :, :, :].rearrange("p k a i -> p k (a i)").rearrange("p k (c m) -> p k c m", m=P)
            with pe.Fori(0, T) as a:
                pe.wait_ge(gen_copied, 2 * a + 1)
                for part, blocks in ((COUNTS, BLOCKS), (WEIGHTS, BLOCKS[:2])):
                    for lo, hi in blocks:
                        nc.tensor.matmul(part[:, lo:hi], zeros[:, :], iota_h[:, lo:hi], start=True, stop=False, skip_group_check=True)
                with pe.Fori(0, GENERAL_CHUNKS) as c:
                    n = a * GENERAL_CHUNKS + c
                    pe.wait_ge(gen_ready, n + 1)
                    for q in range(CHUNKS):
                        right = onehot[q // QW][q % QW]
                        for lo, hi in BLOCKS:
                            last = nc.tensor.matmul(COUNTS[:, lo:hi], dsel[0:EP, 0, q, :], right[0:EP, lo:hi], start=False, stop=False, skip_group_check=True)
                        for lo, hi in BLOCKS[:2]:
                            for k in range(3):
                                last = nc.tensor.matmul(WEIGHTS[:, lo:hi], dsel[0:EP, 1 + k, q, :], right[0:EP, lo:hi], start=False, stop=False, skip_group_check=True)
                    last.then_inc(gen_used, 1)
                for part, blocks in ((COUNTS, BLOCKS), (WEIGHTS, BLOCKS[:2])):
                    for lo, hi in blocks:
                        last = nc.tensor.matmul(part[:, lo:hi], zeros[:, :], iota_h[:, lo:hi], start=False, stop=True, skip_group_check=True)
                last.then_inc(gen_summed, 1)
                pe.wait_ge(gen_copied, 2 * a + 2)
                pe.wait_ge(gen_countT_ready, a + 1)
                for s in range(T):
                    last = nc.tensor.transpose(COUNT_T[:, s * P:(s + 1) * P], count_f[0][:, s * P:(s + 1) * P], ident[:, :])
                last.then_inc(gen_transposed, 1)
            pe.wait_ge(gen_copied, 2 * T + 1)
            pe.wait_ge(gen_countT_ready, T + 1)
        pe.sem_inc(built, 1)

        def spread_u(q):
            pe.wait_ge(gate_chain, 2 * HT * q + 2 * HT)
            pe.wait_ge(tanh_ready, 2 * HT * q)
            for dd in range(HT):
                last = nc.tensor.matmul(U_ALL[:, dd * P:(dd + 1) * P], ones[:, :], diag[dd][:, :], start=True, stop=True)
            last.then_inc(u_spread, 1)

        def half_pe(q, r, h):
            for s in range(T):
                k = s % SLOTS
                if s == HT + 2 and not is_last(q):
                    spread_u(q + 1)
                if s == T - 1 and is_last(q):
                    pe.wait_ge(tanh_ready, 2 * GATES * T)
                    transpose_pe(pe, dense[1], 0, 0)
                if h == 0:
                    pe.wait_ge(g_lo_ready, T * r + s + 1)
                pe.wait_ge(mask_lo_ready, 2 * HT * q + s + 1)
                for dd in range(HT):
                    if s == 0:
                        pe.wait_ge(sum_read, HT * q - HT + dd + 1) if q_has_before(q) else None
                    cols = slice(dd * P, (dd + 1) * P)
                    nc.tensor.matmul(SUMS[dd], mask_hi[k][:, cols], g_hi[:, s, :], start=(s == 0), stop=False)
                    nc.tensor.matmul(SUMS[dd], mask_hi[k][:, cols], g_lo[:, s, :], start=False, stop=False)
                    last = nc.tensor.matmul(SUMS[dd], mask_lo[k][:, cols], g_hi[:, s, :], start=False, stop=(s == T - 1))
                    if s == T - 1 and dd < HT - 1:
                        last.then_inc(sum_ready, 1)
                last.then_inc(mask_used[k], 1)

        def q_has_before(q):
            return not (isinstance(q, int) and q == 0)

        def is_last(q):
            return isinstance(q, int) and q == 2 * GATES - 1

        pe.wait_ge(countT_ready, T)
        spread_u(0)
        half_pe(0, 0, 0)
        with pe.Fori(0, GATES - 1) as r:
            half_pe(2 * r + 1, r, 1)
            half_pe(2 * r + 2, r + 1, 0)
        half_pe(2 * GATES - 1, GATES - 1, 1)

        dense_pe(pe, dense[1], dense[2], lambda b: pe.wait_ge(sum_read, T * GATES - 1 + b))
        dense_pe(pe, dense[2])

        def gcn_pe(grp, sums):
            for s in range(T):
                k = s % SLOTS
                if s == SLOTS and isinstance(grp, int):
                    transpose_pe(pe, dense[3], 0, 0)
                pe.wait_ge(product_read[s % 2], dense[2].pairs(s // 2 + 1))
                pe.wait_ge(cnt_ready, T * grp + s + 1)
                for j in range(GRP):
                    if s == 0:
                        pe.wait_ge(agg_read, GRP * grp + j + 1)
                        pe.wait_ge(product_read[0], dense[2].pairs(HT))
                    left = cnt2[k][:, j * P:(j + 1) * P]
                    for n in range(2):
                        out_n = sums[j][:, n * BANK:(n + 1) * BANK]
                        nc.tensor.matmul(out_n, left, y_hi[s][:, n * BANK:(n + 1) * BANK], start=(s == 0), stop=False)
                        last = nc.tensor.matmul(out_n, left, y_lo[s][:, n * BANK:(n + 1) * BANK], start=False, stop=(s == T - 1))
                    if s == T - 1 and j == 0:
                        last.then_inc(agg_ready, 1)
                last.then_inc(cnt_used[k], 1)

        with pe.Fori(0, GROUPS // 2) as i:
            gcn_pe(2 * i, AGG2[0])
            gcn_pe(2 * i + 1, AGG2[1])
        gcn_pe(GROUPS - 1, AGG2[0])

        dense_pe(pe, dense[3], free=lambda b: pe.wait_ge(agg_read, 2 * GRP + T))
        for b in range(2):
            pe.wait_ge(product_read[b], dense[3].pairs(HT))
        for t in range(T):
            pe.wait_ge(al_diag_ready, t + 1)
            nc.tensor.matmul(AL_ALL[:, t * P:(t + 1) * P], ones[:, :], al_diag[t % 2][:, :], start=True, stop=True).then_inc(al_diag_used, 1)

        def gat_pe(grp):
            for s in range(T):
                pe.wait_ge(att_lo_ready, T * grp + s + 1)
                for j in range(GRP):
                    if s == 0:
                        pe.wait_ge(gat_read, GRP * grp - GRP + j + 1) if q_has_before(grp) else None
                    hi, lo = att_hi[s][:, j * P:(j + 1) * P], att_lo[s][:, j * P:(j + 1) * P]
                    nc.tensor.matmul(DEN[j], hi, ones_r[:, :], start=(s == 0), stop=False)
                    for n in range(2):
                        cols = slice(n * BANK, (n + 1) * BANK)
                        nc.tensor.matmul(AGG[j][:, cols], hi, y_hi[s][:, cols], start=(s == 0), stop=False)
                        nc.tensor.matmul(AGG[j][:, cols], hi, y_lo[s][:, cols], start=False, stop=False)
                    nc.tensor.matmul(DEN[j], lo, ones_r[:, :], start=False, stop=(s == T - 1))
                    for n in range(2):
                        cols = slice(n * BANK, (n + 1) * BANK)
                        last = nc.tensor.matmul(AGG[j][:, cols], lo, y_hi[s][:, cols], start=False, stop=(s == T - 1))
                    if s == T - 1 and j == 0:
                        last.then_inc(gat_ready, 1)
                last.then_inc(att_used, 1)

        pe.wait_ge(al_all_ready, 1)
        gat_pe(0)
        with pe.Fori(1, GROUPS) as grp:
            gat_pe(grp)

    ctx.close()


_INS = ["x", "src", "dst", "edge_weight", "L0_gnn_W1", "L0_gnn_b1", "L0_gnn_gate_w", "L0_gnn_gate_b", "L1_gnn_bias",
        "L2_gnn_W", "L2_gnn_b", "L3_gnn_W", "L3_gnn_a"]


def kernel(**inputs):
    import numpy as np
    import concourse.bacc as bacc
    from concourse.bass_utils import run_bass_kernel_spmd

    nc = bacc.Bacc("TRN2", target_bir_lowering=False, num_devices=1)
    arrays, args = {}, []
    for name in _INS:
        a = np.ascontiguousarray(inputs[name])
        arrays[f"in_{name}"] = a
        args.append(nc.dram_tensor(f"in_{name}", a.shape, mybir.dt.from_np(a.dtype), kind="ExternalInput").ap())
    out = nc.dram_tensor("out_x", (N, D), F32, kind="ExternalOutput").ap()
    build_program(nc, *args, out)
    r = run_bass_kernel_spmd(nc, [arrays], core_ids=[0])
    return r.results[0]["out_x"]
```

```python
from contextlib import ExitStack

import concourse.bass as bass
from concourse import mybir

ALU = mybir.AluOpType
ACT = mybir.ActivationFunctionType
AX_X = mybir.AxisListType.X
F32 = mybir.dt.float32
F32R = mybir.dt.float32r
BF16 = mybir.dt.bfloat16
F16 = mybir.dt.float16
I32 = mybir.dt.int32
I16 = mybir.dt.int16

P = 128
D = 1024
HID = 512
GATES = 4
N = 1250
E = 20000
T = -(-N // P)
NP = T * P
KT = D // P
WT_TILES = KT
WIN = 32
QW = P // WIN
WINDOWS = T * QW
CHUNKS = 5
CAP = CHUNKS * P
EP = 125
EC = E // EP
GENERAL_CHUNKS = E // (EP * CHUNKS)
HALF = NP // 2
HT = T // 2
BANK = 512
GRP = 2
GROUPS = T // GRP
GC = GRP * P
SLOTS = 5
TANH_LEAD = 3
EPS_LN = 1e-5
EPS_GAT = 1e-5
SLOPE = 0.1
KIB = 1024


def build_program(nc, x, src, dst, edge_weight, w1, b1, gate_w, gate_b, bias1, w2, b2, w3, att, out):
    ctx = ExitStack()
    base = -(-nc.sbuf_base // 64) * 64
    limit = nc.sbuf_usable_end
    R_Y = base
    R_W = R_Y + 80 * KIB
    R_C = R_W + 64 * KIB
    R_X = R_C + T * NP * 2
    R_S = R_X + 32 * KIB
    places = [R_S]

    def at(name, shape, dtype, offset):
        return nc.alloc_sbuf_tensor_at(name, shape, dtype, offset=offset)

    def small(name, shape, dtype):
        size = 4 if dtype in (F32, F32R, I32) else 2
        for n in shape[1:]:
            size *= n
        offset = places[0]
        places[0] = -(-(offset + size) // 32) * 32
        assert places[0] <= limit, name
        return at(name, shape, dtype, offset)

    def sem(name):
        return ctx.enter_context(nc.semaphore(name))

    def sems(name, n):
        return [sem(f"{name}{i}") for i in range(n)]

    ps = ctx.enter_context(nc.psum_tensor("ps", [P, 8 * BANK], F32))

    x1_dram = nc.dram_tensor("x_after_0", (NP, D), F32).ap()
    x2_dram = nc.dram_tensor("x_after_1", (NP, D), F32).ap()
    x3_dram = nc.dram_tensor("x_after_2", (NP, D), F32).ap()
    count_dram = nc.dram_tensor("count_rows", (NP, NP), I16).ap()
    wt_dram = nc.dram_tensor("weight_rows", (NP, D), F32).ap()

    xin = [at(f"xin{b}", [P, D], F32, R_X + b * 4 * KIB) for b in range(2)]
    xres = [at(f"xres{b}", [P, D], F32, R_X + (8 + 4 * b) * KIB) for b in range(2)]
    hT_hi = [at(f"hT_hi{b}", [P, KT, P], F32R, R_X + (16 + 8 * b) * KIB) for b in range(2)]
    hT_lo = [at(f"hT_lo{b}", [P, KT, P], F32R, R_X + (20 + 8 * b) * KIB) for b in range(2)]

    w1_raw = at("w1_raw", [P, KT, HID], F32, R_Y + 64 * KIB)
    w1_hi = at("w1_hi", [P, KT, HID], F32R, R_Y + 20 * KIB)
    w1_lo = at("w1_lo", [P, KT, HID], F32R, R_Y + 36 * KIB)
    wt_raw = at("wt_raw", [P, KT, D], F32, R_W + 32 * KIB)
    wt_hi = at("wt_hi", [P, KT, D], F32R, R_W)
    wt_lo = at("wt_lo", [P, KT, D], F32R, R_W + 32 * KIB)
    w_raw = at("w_raw", [P, KT, D], F32, R_Y + 32 * KIB)
    w_hi = at("w_hi", [P, KT, D], F32R, R_Y)
    w_lo = at("w_lo", [P, KT, D], F32R, R_Y + 32 * KIB)

    g = at("g", [P, T, HID], F32, R_Y)
    g_hi = at("g_hi", [P, T, HID], F32R, R_Y + 20 * KIB)
    g_lo = at("g_lo", [P, T, HID], F32R, R_Y + 40 * KIB)
    gw = at("gw", [P, 2 * HID], F32, R_Y + 60 * KIB)
    gate_scratch = at("gate_scratch", [P, HID], F32, R_Y + 64 * KIB)
    b1_all = at("b1_all", [P, HID], F32, R_Y + 60 * KIB)
    PIECE = HALF * 4
    piece = [R_X + 16 * KIB + n * PIECE for n in range(6)]
    piece += [R_Y + 66 * KIB + n * PIECE for n in range(2 * SLOTS - 6)]
    assert piece[-1] + PIECE <= R_W
    mask = [at(f"mask{k}", [P, HALF], F32, piece[2 * k]) for k in range(SLOTS)]
    mask_lo = [at(f"mask_lo{k}", [P, HALF], F32R, piece[2 * k]) for k in range(SLOTS)]
    mask_hi = [at(f"mask_hi{k}", [P, HALF], F32R, piece[2 * k + 1]) for k in range(SLOTS)]

    y_all = at("y_all", [P, T, 2, D], F32R, R_Y + 64 * KIB)
    y_hi = [y_all[:, s, 0, :] for s in range(T)]
    y_lo = [y_all[:, s, 1, :] for s in range(T)]
    cnt2 = [at(f"cnt2_{k}", [P, GC], F32R, R_X + k * GC * 4) for k in range(SLOTS)]
    cnt2_last = [at(f"cnt2_last{k}", [P, GC], F32R, R_X + 24 * KIB + k * GC * 4) for k in range(SLOTS)]
    att_all = [at(f"att_all{n}", [P, D], F32, R_X + (8 + 4 * n) * KIB) for n in range(2)]
    top = at("top", [P, GC], F32R, R_X + 24 * KIB + SLOTS * GC * 4)
    low = at("low", [P, GC], F32R, R_X + 25 * KIB + SLOTS * GC * 4)
    slot = [R_X + 16 * KIB + 2 * KIB * s if s < 4 else R_Y + 2 * KIB * s for s in range(T)]
    att_e = [at(f"att_e{s}", [P, GC], F32, slot[s]) for s in range(T)]
    att_lo = [at(f"att_lo{s}", [P, GC], F32R, slot[s]) for s in range(T)]
    att_hi = [at(f"att_hi{s}", [P, GC], F32R, slot[s] + KIB) for s in range(T)]
    al_all = at("al_all", [P, NP], F32, R_X)
    e_part = at("e_part", [P, GC], F32, R_X + 5 * KIB)
    e_sum = at("e_sum", [P, GC], F32, R_X + 6 * KIB)
    gat_sums = [at(f"gat_sums{j}", [P, D], F32, R_Y + (32 + 4 * j) * KIB) for j in range(GRP)]
    elu_neg = [at(f"elu_neg{j}", [P, D], F32, R_Y + (40 + 4 * j) * KIB) for j in range(GRP)]

    countT = at("countT", [P, T, NP], I16, R_C)
    count = at("count", [P, T, NP], I16, R_C)

    o = [R_W]

    def build(name, shape, dtype):
        size = 4 if dtype in (F32, I32) else 2
        for n in shape[1:]:
            size *= n
        offset = o[0]
        o[0] += -(-size // 32) * 32
        assert o[0] <= R_C, name
        return at(name, shape, dtype, offset)

    onehot = [[build(f"onehot{c}_{j}", [P, NP], BF16) for j in range(QW)] for c in range(2)]
    onehot += [[at(f"onehot{c}_{j}", [P, NP], BF16, R_Y + 20 * KIB + ((c - 2) * QW + j) * NP * 2) for j in range(QW)]
               for c in range(2, CHUNKS)]
    sel = [build(f"sel{b}", [P, 4, QW * CHUNKS, WIN], BF16) for b in range(2)]
    iota_f = build("iota_f", [P, NP], F32)
    iota_h = build("iota_h", [P, NP], F16)
    count_f = [build(f"count_f{b}", [P, NP], F32) for b in range(2)]
    count_row = [build(f"count_row{b}", [P, NP], I16) for b in range(2)]
    weight_row = [build(f"weight_row{b}", [P, D], F32) for b in range(2)]
    ends_raw = [build(f"ends_raw{b}", [P, 2, QW * CHUNKS], I32) for b in range(2)]
    ends = [build(f"ends{b}", [P, 2, QW * CHUNKS], F32) for b in range(2)]
    ew = [build(f"ew{b}", [P, QW * CHUNKS], F32) for b in range(2)]
    ew_rest = [build(f"ew_rest{b}", [P, 2, QW * CHUNKS], F32) for b in range(2)]
    ew_part = [build(f"ew_part{b}", [P, 3, QW * CHUNKS], BF16) for b in range(2)]
    DG = 8
    dst_raw = at("dst_raw", [P, EC], I32, R_W + 60 * KIB)
    dst_h = at("dst_h", [P, EC], F16, R_W + 61 * KIB)
    below = at("below", [P, EC, WINDOWS], BF16, R_W + 40 * KIB)

    ident = small("ident", [P, P], F32)
    ones = small("ones", [P, P], F32)

    zeros = small("zeros", [P, P], BF16)
    stats = [small(f"stats{b}", [P, 2, 6], F32) for b in range(2)]
    mv = [small(f"mv{b}", [P, 2], F32) for b in range(2)]
    ln = [small(f"ln{b}", [P, 6], F32) for b in range(2)]
    deg = small("deg", [P, T], F32)
    norm = small("norm", [P, 2, T], F32)
    norm_root = small("norm_root", [P, 2, T], F32)
    norm_step = small("norm_step", [P, 2, T], F32)
    dis = small("dis", [P, 2, T], F32)
    ones_h = small("ones_h", [P, 2], BF16)
    below_n = small("below_n", [P, WINDOWS], F32)
    firsts = small("firsts", [P, WINDOWS], F16)
    starts = small("starts", [P, WINDOWS], I32)
    captured = small("captured", [P, 1], F32)
    complete = small("complete", [P, 1], I32)
    gb = small("gb", [P, GATES], F32)
    u = small("u", [P, T], F32)
    v = small("v", [P, T], F32)
    al = small("al", [P, T], F32)
    ar = small("ar", [P, T], F32)
    al_col = [small(f"al_col{b}", [P, 2], F32) for b in range(2)]
    rden = small("rden", [P, GRP, 2], F32)
    row_all = small("row_all", [P, D], F32)
    gb_col = small("gb_col", [P, 1], F32)


    consts_landed = sem("consts_landed")
    iota_done = sem("iota_done")
    firsts_done = sem("firsts_done")
    dst_ready = sem("dst_ready")
    consts_done = sem("consts_done")

    xin_landed = sems("xin_landed", 2)
    ln_chain = sem("ln_chain")
    var_ready = sem("var_ready")
    root_ready = sem("root_ready")
    scale_ready = sem("scale_ready")
    h_ready = sem("h_ready")
    h_transposed = sems("h_transposed", 2)
    hT_hi_ready = sem("hT_hi_ready")
    hT_lo_ready = sem("hT_lo_ready")
    product_ready = sems("product_ready", 2)
    product_read = sems("product_read", 2)
    w_landed = sems("w_landed", 4)
    w_hi_ready = sem("w_hi_ready")
    w_lo_ready = sem("w_lo_ready")
    res_landed = sems("res_landed", 2)
    res_added = sem("res_added")
    stored = sems("stored", 2)

    class Dense:

        def __init__(self, n):
            self.n = n

        def pairs(self, i):
            return HT * self.n + i

        def tiles(self, t):
            return T * self.n + t

    dense = [Dense(n) for n in range(4)]
    LN_STEPS = 7

    dst_landed = sem("dst_landed")
    below_chain = sem("below_chain")
    below_ready = sem("below_ready")
    below_summed = sem("below_summed")
    starts_ready = sem("starts_ready")
    ends_landed = sems("ends_landed", 2)
    ends_ready = sem("ends_ready")
    sel_ready = sem("sel_ready")
    parts_chain = sem("parts_chain")
    wsel_ready = sem("wsel_ready")
    onehot_ready = sem("onehot_ready")
    onehot_used = sems("onehot_used", CHUNKS)
    counts_ready = sem("counts_ready")
    counts_copied = sem("counts_copied")
    weights_copied = sem("weights_copied")
    count_transposed = sems("count_transposed", 2)
    countT_ready = sem("countT_ready")
    count_row_ready = sem("count_row_ready")
    count_stored = sems("count_stored", 2)
    weights_stored = sems("weights_stored", 2)
    captured_ready = sem("captured_ready")
    captured_summed = sem("captured_summed")
    complete_ready = sem("complete_ready")
    gen_landed = sem("gen_landed")
    gen_chain = sem("gen_chain")
    gen_ready = sem("gen_ready")
    gen_used = sem("gen_used")
    gen_summed = sem("gen_summed")
    gen_copied = sem("gen_copied")
    gen_transposed = sem("gen_transposed")
    gen_countT_ready = sem("gen_countT_ready")
    gen_row_ready = sem("gen_row_ready")
    gen_stored = sem("gen_stored")
    built = sem("built")
    norm_chain = sem("norm_chain")
    norm_root_ready = sem("norm_root_ready")
    tanh_idle = sem("tanh_idle")
    dis_ready = sem("dis_ready")
    gw_landed = sem("gw_landed")
    u_ready = sem("u_ready")
    gates_ready = sem("gates_ready")
    u_spread = sem("u_spread")
    g_hi_ready = sem("g_hi_ready")
    g_lo_ready = sem("g_lo_ready")
    tanh_ready = sem("tanh_ready")
    mask_ready = sem("mask_ready")
    mask_hi_ready = sem("mask_hi_ready")
    mask_lo_ready = sem("mask_lo_ready")
    mask_used = sems("mask_used", SLOTS)
    sum_ready = sem("sum_ready")
    sum_read = sem("sum_read")
    half_landed = sems("half_landed", 4)
    half_added = sem("half_added")
    half_stored = sems("half_stored", 2)
    y_hi_ready = sem("y_hi_ready")
    loops_added = sem("loops_added")
    cnt_ready = sem("cnt_ready")
    cnt_used = sems("cnt_used", SLOTS)
    low_chain = sem("low_chain")
    low_ready = sem("low_ready")
    low_used = sem("low_used")
    agg_ready = sem("agg_ready")
    agg_read = sem("agg_read")
    agg_chain = sem("agg_chain")
    agg_landed = sems("agg_landed", 2)
    agg_stored = sems("agg_stored", 2)
    b2_landed = sem("b2_landed")
    bias1_landed = sem("bias1_landed")
    att_landed = sem("att_landed")
    count_landed = sem("count_landed")
    al_chain = sem("al_chain")
    al_ready = sem("al_ready")
    al_spread = sem("al_spread")
    e_summed = sem("e_summed")
    al_all_ready = sem("al_all_ready")
    logit_ready = sem("logit_ready")
    leaky_ready = sem("leaky_ready")
    exp_ready = sem("exp_ready")
    att_e_ready = sem("att_e_ready")
    att_hi_ready = sem("att_hi_ready")
    att_lo_ready = sem("att_lo_ready")
    att_used = sem("att_used")
    gat_ready = sem("gat_ready")
    gat_read = sem("gat_read")
    den_taken = sem("den_taken")
    elu_added = sem("elu_added")
    gat_pos_ready = sem("gat_pos_ready")
    gat_chain = sem("gat_chain")
    gat_neg_ready = sem("gat_neg_ready")
    gat_exp_ready = sem("gat_exp_ready")
    gat_landed = sems("gat_landed", 2)
    gat_added = sem("gat_added")
    gat_stored = sems("gat_stored", 2)
    al_copied = sem("al_copied")
    gb_chain = sem("gb_chain")

    block = ctx.enter_context(nc.Block())

    NHALF = [1, 2, 2, 2]
    W_RAW = [w1_raw, wt_raw, w_raw, w_raw]
    W_HI = [w1_hi, wt_hi, w_hi, w_hi]
    W_LO = [w1_lo, wt_lo, w_lo, w_lo]
    TRANSPOSED = ps[:, 6 * BANK:8 * BANK]
    PRODUCTS = [ps[:, (2 + 2 * b) * BANK:(4 + 2 * b) * BANK] for b in range(2)]
    PRODUCT = [PRODUCTS, PRODUCTS, PRODUCTS, PRODUCTS[::-1]]


    def rows(t):
        return bass.ds(t * P, P)

    def split_act(act, d, ks):
        for k in ks:
            if k % 2 == 0:
                act.wait_ge(w_landed[k // 2], 16 * (d.n + 1))
            nc.scalar.activation(W_HI[d.n][:, k, :], W_RAW[d.n][:, k, :], ACT.Copy).then_inc(w_hi_ready, 1)

    def split_dve(dve, d, ks):
        for k in ks:
            dve.wait_ge(w_hi_ready, KT * d.n + k + 1)
            nc.vector.tensor_tensor(W_LO[d.n][:, k, :], W_RAW[d.n][:, k, :], W_HI[d.n][:, k, :].bitcast(F32),
                                    ALU.subtract).then_inc(w_lo_ready, 1)

    def stats_dve(dve, d, i, b):
        t = 2 * i + b
        dve.wait_ge(xin_landed[b], 16 * d.pairs(i + 1))
        for half in range(2):
            nc.vector.bn_stats(stats[b][:, half, :], xin[b][:, half * 512:(half + 1) * 512]).then_inc(ln_chain, 1)
        settled(dve, ln_chain, LN_STEPS * d.tiles(t) + 2)
        nc.vector.bn_aggr(mv[b][:, :], stats[b][:, :, :].rearrange("p a s -> p (a s)")).then_inc(ln_chain, 1)
        dve.wait_ge(ln_chain, LN_STEPS * d.tiles(t) + 3)
        nc.vector.tensor_scalar(ln[b][:, 0:1], mv[b][:, 1:2], EPS_LN, None, ALU.add).then_inc(var_ready, 1)

    def scale_dve(dve, d, i, b):
        t = 2 * i + b
        ve, root, r0, q, c, scale = (ln[b][:, j:j + 1] for j in range(6))
        dve.wait_ge(root_ready, d.tiles(t + 1))
        nc.vector.reciprocal(r0, root).then_inc(ln_chain, 1)
        dve.wait_ge(ln_chain, LN_STEPS * d.tiles(t) + 4)
        nc.vector.scalar_tensor_tensor(q, r0, r0, ve, ALU.mult, ALU.mult).then_inc(ln_chain, 1)
        dve.wait_ge(ln_chain, LN_STEPS * d.tiles(t) + 5)
        nc.vector.tensor_scalar(c, q, -0.5, 1.5, ALU.mult, ALU.add).then_inc(ln_chain, 1)
        dve.wait_ge(ln_chain, LN_STEPS * d.tiles(t) + 6)
        nc.vector.tensor_tensor(scale, r0, c, ALU.mult).then_inc(ln_chain, 1)
        dve.wait_ge(ln_chain, LN_STEPS * d.tiles(t) + 7)
        nc.vector.tensor_scalar(q, mv[b][:, 0:1], scale, -1.0, ALU.mult, ALU.mult).then_inc(scale_ready, 1)

    def root_act(act, d, i, b):
        act.wait_ge(var_ready, d.tiles(2 * i + b + 1))
        nc.scalar.activation(ln[b][:, 1:2], ln[b][:, 0:1], ACT.Sqrt).then_inc(root_ready, 1)

    def h_act(act, d, i, b):
        act.wait_ge(scale_ready, d.tiles(2 * i + b + 1))
        nc.scalar.activation(xin[b][:, :], xin[b][:, :], ACT.Relu, bias=ln[b][:, 3:4],
                             scale=ln[b][:, 5:6]).then_inc(h_ready, 1)

    def transposed_act(act, d, i, b):
        t = 2 * i + b
        act.wait_ge(h_transposed[b], d.pairs(i + 1))
        nc.scalar.activation(hT_hi[b][:, :, :].rearrange("p k m -> p (k m)"), TRANSPOSED,
                             ACT.Copy).then_inc(hT_hi_ready, 1)

    def transposed_dve(dve, d, i, b):
        t = 2 * i + b
        dve.wait_ge(hT_hi_ready, d.tiles(t + 1))
        nc.vector.tensor_tensor(hT_lo[b][:, :, :].rearrange("p k m -> p (k m)"), TRANSPOSED,
                                hT_hi[b][:, :, :].rearrange("p k m -> p (k m)").bitcast(F32),
                                ALU.subtract).then_inc(hT_lo_ready, 1)

    def transpose_pe(pe, d, i, b):
        t = 2 * i + b
        pe.wait_ge(h_ready, d.tiles(t + 1))
        pe.wait_ge(hT_lo_ready, d.tiles(t))
        for k in range(KT):
            last = nc.tensor.transpose(TRANSPOSED[:, k * P:(k + 1) * P], xin[b][:, k * P:(k + 1) * P], ident[:, :])
        last.then_inc(h_transposed[b], 1)

    def product_pe(pe, d, i, b, first, transpose_next):
        t = 2 * i + b
        hi, lo = W_HI[d.n], W_LO[d.n]
        pe.wait_ge(hT_lo_ready, d.tiles(t + 1))
        pe.wait_ge(product_read[b], d.pairs(i))
        for k in range(KT):
            if k == KT // 2 and transpose_next is not None:
                transpose_next()
            if first:
                pe.wait_ge(w_lo_ready, KT * d.n + k + 1)
            for left, rights in ((hT_hi[b], (hi, lo)), (hT_lo[b], (hi,))):
                for half in range(NHALF[d.n]):
                    for right in rights:
                        last = nc.tensor.matmul(PRODUCT[d.n][b][:, half * BANK:(half + 1) * BANK], left[:, k, :],
                                                right[:, k, half * BANK:(half + 1) * BANK],
                                                start=(k == 0 and left is hT_hi[b] and right is hi),
                                                stop=(k == KT - 1 and left is hT_lo[b]))
        last.then_inc(product_ready[b], 1)

    def dense_pe(pe, d, nxt=None, free=None, late=None, aside=None):
        if d.n == 0:
            transpose_pe(pe, d, 0, 0)
        if free is not None:
            free(0)
        product_pe(pe, d, 0, 0, True, lambda: transpose_pe(pe, d, 0, 1))
        if free is not None:
            free(1)
        product_pe(pe, d, 0, 1, False, lambda: transpose_pe(pe, d, 1, 0))
        begin = 1
        if aside is not None:
            product_pe(pe, d, 1, 0, False, lambda: transpose_pe(pe, d, 1, 1))
            product_pe(pe, d, 1, 1, False, lambda: (transpose_pe(pe, d, 2, 0), aside()))
            begin = 2
        with pe.Fori(begin, HT - 1) as i:
            product_pe(pe, d, i, 0, False, lambda: transpose_pe(pe, d, i, 1))
            product_pe(pe, d, i, 1, False, lambda: transpose_pe(pe, d, i + 1, 0))
        product_pe(pe, d, HT - 1, 0, False, lambda: transpose_pe(pe, d, HT - 1, 1))
        product_pe(pe, d, HT - 1, 1, False, late if nxt is None else lambda: transpose_pe(pe, nxt, 0, 0))

    def dense_dve(dve, d, finish, nxt=None, late=None, asides=None):
        if d.n == 0:
            stats_dve(dve, d, 0, 0)
            scale_dve(dve, d, 0, 0)
            stats_dve(dve, d, 0, 1)
            scale_dve(dve, d, 0, 1)
            asides[0]()
            transposed_dve(dve, d, 0, 0)
            split_dve(dve, d, range(KT))

        def two_tiles(i, behind=(None, None)):
            for b in range(2):
                stats_dve(dve, d, i + 1, b)
                transposed_dve(dve, d, i + b, 1 - b)
                scale_dve(dve, d, i + 1, b)
                finish(i, b)
                if behind[b] is not None:
                    behind[b]()

        begin = 0
        if asides is not None:
            two_tiles(0, asides[1:3])
            two_tiles(1, asides[3:5])
            begin = 2
        with dve.Fori(begin, HT - 1) as i:
            two_tiles(i)
        if nxt is not None:
            stats_dve(dve, nxt, 0, 0)
        transposed_dve(dve, d, HT - 1, 1)
        if nxt is not None:
            scale_dve(dve, nxt, 0, 0)
            split_dve(dve, nxt, range(KT // 2))
        finish(HT - 1, 0)
        if nxt is not None:
            split_dve(dve, nxt, range(KT // 2, KT))
            transposed_dve(dve, nxt, 0, 0)
            stats_dve(dve, nxt, 0, 1)
            scale_dve(dve, nxt, 0, 1)
        if late is not None:
            late()
        finish(HT - 1, 1)

    def dense_act(act, d, finish, nxt=None, late=None):
        if d.n == 0:
            root_act(act, d, 0, 0)
            h_act(act, d, 0, 0)
            root_act(act, d, 0, 1)
            h_act(act, d, 0, 1)
            transposed_act(act, d, 0, 0)
            split_act(act, d, range(KT))
        with act.Fori(0, HT - 1) as i:
            for b in range(2):
                root_act(act, d, i + 1, b)
                transposed_act(act, d, i + b, 1 - b)
                h_act(act, d, i + 1, b)
                finish(i, b)
        if nxt is not None:
            root_act(act, nxt, 0, 0)
        transposed_act(act, d, HT - 1, 1)
        if nxt is not None:
            act.wait_ge(half_added, T)
            split_act(act, nxt, range(2))
            h_act(act, nxt, 0, 0)
            split_act(act, nxt, range(2, KT // 2))
        finish(HT - 1, 0)
        if nxt is not None:
            split_act(act, nxt, range(KT // 2, KT))
            transposed_act(act, nxt, 0, 0)
            root_act(act, nxt, 0, 1)
            h_act(act, nxt, 0, 1)
        if late is not None:
            late()
        finish(HT - 1, 1)

    def load_weights(eng, d, dram):
        for q in range(4):
            eng.dma_start(W_RAW[d.n][:, 2 * q:2 * q + 2, :],
                          dram[2 * q * P:(2 * q + 2) * P, :].rearrange("(k p) n -> p k n", p=P)
                          ).then_inc(w_landed[q], 16)

    settles = sem("settles")

    def settled(eng, semaphore, value):
        eng.wait_ge(semaphore, value)
        eng.sem_inc(settles, 1)

    @block.sync
    def _(sp):
        d = dense[0]
        sp.dma_start(xin[0][:, :], x[0:P, :]).then_inc(xin_landed[0], 16)
        sp.dma_start(dst_raw[0:EP, :], dst.rearrange("(p c) -> p c", c=EC)).then_inc(dst_landed, 16)
        sp.dma_start(xin[1][:, :], x[P:2 * P, :]).then_inc(xin_landed[1], 16)
        load_weights(sp, d, w1)
        sp.dma_start(b1_all[:, :], b1.partition_broadcast(P)).then_inc(consts_landed, 16)
        sp.dma_start(gb[:, :], gate_b.rearrange("k a -> (k a)").partition_broadcast(P)).then_inc(consts_landed, 16)
        with sp.Fori(1, HT - 1) as i:
            for b in range(2):
                settled(sp, h_transposed[b], d.pairs(i))
                sp.dma_start(xin[b][:, :], x[rows(2 * i + b), :]).then_inc(xin_landed[b], 16)

        def load_edges(i, b):
            for j in range(QW):
                start = sp.value_load(starts[0:1, bass.ds(QW * (2 * i + b) + j, 1)], min_val=0, max_val=E - CAP)
                cols = slice(j * CHUNKS, (j + 1) * CHUNKS)
                for to, of in ((ends_raw[b][:, 0, cols], src), (ends_raw[b][:, 1, cols], dst), (ew[b][:, cols], edge_weight)):
                    sp.dma_start(to, of[bass.ds(start, CAP)].rearrange("(p c) -> p c", c=CHUNKS)).then_inc(ends_landed[b], 16)

        sp.wait_ge(h_transposed[0], d.pairs(HT - 1))
        sp.dma_start(xin[0][:, :], x[(T - 2) * P:(T - 1) * P, :]).then_inc(xin_landed[0], 16)
        sp.wait_ge(starts_ready, 1)
        load_edges(0, 0)
        sp.wait_ge(h_transposed[1], d.pairs(HT - 1))
        sp.dma_start(xin[1][0:N - (T - 1) * P, :], x[(T - 1) * P:N, :]).then_inc(xin_landed[1], 16)

        load_edges(0, 1)
        for b in range(2):
            sp.wait_ge(product_read[b], d.pairs(HT))
        sp.dma_start(gw[:, :], gate_w[0].rearrange("c a -> (c a)").partition_broadcast(P)).then_inc(gw_landed, 16)
        with sp.Fori(1, HT) as i:
            for b in range(2):
                settled(sp, ends_ready, 2 * i + b - 1)
                settled(sp, wsel_ready, 2 * i + b - 1)
                load_edges(i, b)

        sp.wait_ge(complete_ready, 1)
        whole = sp.value_load(complete[0:1, 0:1], min_val=0, max_val=1)
        with sp.If(whole == 0):
            sp.sem_inc(gen_stored, 1)
            with sp.Fori(0, T) as a:
                with sp.Fori(0, GENERAL_CHUNKS) as c:
                    settled(sp, gen_used, a * GENERAL_CHUNKS + c + 1)
                    for to, of in ((ends_raw[0][0:EP, 0, 0:CHUNKS], src), (ends_raw[0][0:EP, 1, 0:CHUNKS], dst),
                                   (ew[0][0:EP, 0:CHUNKS], edge_weight)):
                        sp.dma_start(to, of[bass.ds(c * (EP * CHUNKS), EP * CHUNKS)].rearrange("(p c) -> p c", c=CHUNKS)
                                     ).then_inc(gen_landed, 16)
                settled(sp, gen_row_ready, a + 1)
                sp.dma_start(count_dram[rows(a), :], count_row[0][:, :]).then_inc(gen_stored, 16)
                sp.dma_start(wt_dram[rows(a), :], weight_row[0][:, :]).then_inc(gen_stored, 16)
                settled(sp, gen_stored, 32 * (a + 1) + 1)
        for b in range(2):
            sp.wait_ge(weights_stored[b], 16 * WT_TILES // 2)
            sp.wait_ge(count_stored[b], 16 * HT)
        sp.wait_ge(built, 3)
        load_weights(sp, dense[1], wt_dram)
        with sp.Fori(0, GATES - 1) as r:
            settled(sp, gates_ready, T * (r + 1))
            sp.dma_start(gw[:, :], gate_w[bass.ds(r + 1, 1)].rearrange("k c a -> (k c a)").partition_broadcast(P)
                         ).then_inc(gw_landed, 16)

        d = dense[1]

        def load_x1(i):
            for b in range(2):
                settled(sp, half_stored[b], 16 * (i + 1))
                if not isinstance(i, int) or i > 0:
                    settled(sp, h_transposed[b], d.pairs(i))
                sp.dma_start(xin[b][:, :], x1_dram[rows(2 * i + b), :]).then_inc(xin_landed[b], 16)

        for b in range(2):
            sp.wait_ge(h_transposed[b], d.pairs(0))
        load_x1(0)
        sp.dma_start(row_all[:, :], bias1.partition_broadcast(P)).then_inc(bias1_landed, 16)
        sp.wait_ge(mask_used[SLOTS - 1], 2 * 2 * GATES)
        for q in range(4):
            sp.dma_start(w_raw[:, 2 * q:2 * q + 2, :], w2[2 * q * P:(2 * q + 2) * P, :].rearrange("(k p) n -> p k n", p=P)
                         ).then_inc(w_landed[q], 16)
            load_x1(q + 1)
        d = dense[2]
        with sp.Fori(0, HT) as i:
            for b in range(2):
                settled(sp, stored[b], 16 * dense[1].pairs(i + 1))
                settled(sp, h_transposed[b], d.pairs(i))
                sp.dma_start(xin[b][:, :], x2_dram[rows(2 * i + b), :]).then_inc(xin_landed[b], 16)
        sp.wait_ge(res_added, dense[1].tiles(T))
        sp.dma_start(row_all[:, :], b2.partition_broadcast(P)).then_inc(b2_landed, 16)
        for b in range(2):
            sp.wait_ge(product_ready[b], d.pairs(HT))
        load_weights(sp, dense[3], w3)
        d = dense[3]

        def load_x3(i):
            for b in range(2):
                settled(sp, agg_stored[b], 16 * (i + 1))
                settled(sp, h_transposed[b], d.pairs(i))
                sp.dma_start(xin[b][:, :], x3_dram[rows(2 * i + b), :]).then_inc(xin_landed[b], 16)

        def load_count(i):
            sp.dma_start(count[:, bass.ds(2 * i, 2), :], count_dram[bass.ds(2 * i * P, 2 * P), :].rearrange("(t p) s -> p t s", p=P)
                         ).then_inc(count_landed, 16)

        sp.wait_ge(cnt_used[SLOTS - 1], 2 * (GROUPS - 1))
        load_x3(0)
        load_x3(1)
        sp.wait_ge(agg_read, 2 * GRP + T)
        with sp.Fori(2, HT) as i:
            load_x3(i)
            load_count(i - 2)
        load_count(HT - 2)
        load_count(HT - 1)

        def load3(i, b):
            sp.dma_start(xres[b][:, :], x3_dram[rows(2 * i + b), :]).then_inc(gat_landed[b], 16)

        def store3(i, b):
            settled(sp, gat_added, 2 * i + b + 1)
            sp.dma_start(out[rows(2 * i + b), :], xres[b][:, :]).then_inc(gat_stored[b], 16)
            settled(sp, gat_stored[b], 16 * (i + 1))

        sp.wait_ge(al_ready, T)
        load3(0, 0)
        load3(0, 1)
        with sp.Fori(0, HT - 1) as i:
            for b in range(2):
                store3(i, b)
                load3(i + 1, b)
        store3(HT - 1, 0)
        for half in range(2):
            sp.wait_ge(gat_added, T + half)
            cols = slice(half * HID, (half + 1) * HID)
            sp.dma_start(out[(T - 1) * P:N, cols], xres[1][0:N - (T - 1) * P, cols]).then_inc(gat_stored[1], 16)
        sp.wait_ge(gat_stored[1], 16 * (HT + 1))

    @block.gpsimd
    def _(pool):
        nc.gpsimd.memset(ones[:, :], 1.0).then_inc(consts_done, 1)
        nc.gpsimd.memset(zeros[:, :], 0.0).then_inc(consts_done, 1)
        pool.wait_ge(consts_done, 1)
        nc.gpsimd.affine_select(out=ident[:, :], in_=ones[:, :], pattern=[[-1, P]], compare_op=ALU.is_equal, fill=0.0,
                                base=0, channel_multiplier=1).then_inc(consts_done, 1)
        nc.gpsimd.memset(ones_h[:, :], 1.0).then_inc(consts_done, 1)
        nc.gpsimd.iota(firsts[:, :], [[WIN, WINDOWS]], base=0, channel_multiplier=0,
                       allow_small_or_imprecise_dtypes=True).then_inc(firsts_done, 1)
        pool.wait_ge(dst_landed, 16)
        nc.gpsimd.tensor_copy(dst_h[0:EP, :], dst_raw[0:EP, :]).then_inc(dst_ready, 1)
        nc.gpsimd.iota(iota_f[:, :], [[1, NP]], base=0, channel_multiplier=0,
                       allow_small_or_imprecise_dtypes=True).then_inc(iota_done, 1)
        pool.wait_ge(iota_done, 1)
        nc.gpsimd.tensor_copy(iota_h[:, :], iota_f[:, :]).then_inc(iota_done, 1)

        d = dense[0]

        def first_half(i, b, n):
            if not isinstance(i, int) or i > 0:
                settled(pool, stored[b], 16 * d.pairs(i))
            pool.dma_start(xres[b][0:n, 0:HID], x[bass.ds((2 * i + b) * P, n), 0:HID]).then_inc(res_landed[b], 16)
            settled(pool, res_landed[b], 16 * d.pairs(i + 1))
            settled(pool, product_read[b], d.pairs(i + 1))
            nc.gpsimd.tensor_tensor(xres[b][:, 0:HID], xres[b][:, 0:HID], g[:, bass.ds(2 * i + b, 1), :].rearrange("p a n -> p (a n)"),
                                    ALU.add).then_inc(res_added, 1)
            settled(pool, res_added, d.tiles(2 * i + b + 1))
            pool.dma_start(x1_dram[rows(2 * i + b), 0:HID], xres[b][:, 0:HID]).then_inc(stored[b], 16)

        first_half(0, 0, P)
        first_half(0, 1, P)
        with pool.Fori(1, HT - 1) as i:
            first_half(i, 0, P)
            first_half(i, 1, P)
        PARTS = 5

        def weight_parts(i, b):
            a = 2 * i + b
            settled(pool, ends_landed[b], 16 * 3 * QW * (i + 1))
            settled(pool, sel_ready, a + 1)
            whole, rest, part = ew[b], ew_rest[b], ew_part[b]
            nc.gpsimd.tensor_copy(part[:, 0, :], whole[:, :]).then_inc(parts_chain, 1)
            settled(pool, parts_chain, PARTS * a + 1)
            nc.gpsimd.tensor_tensor(rest[:, 0, :], whole[:, :], part[:, 0, :], ALU.subtract).then_inc(parts_chain, 1)
            settled(pool, parts_chain, PARTS * a + 2)
            nc.gpsimd.tensor_copy(part[:, 1, :], rest[:, 0, :]).then_inc(parts_chain, 1)
            settled(pool, parts_chain, PARTS * a + 3)
            nc.gpsimd.tensor_tensor(rest[:, 1, :], rest[:, 0, :], part[:, 1, :], ALU.subtract).then_inc(parts_chain, 1)
            settled(pool, parts_chain, PARTS * a + 4)
            nc.gpsimd.tensor_copy(part[:, 2, :], rest[:, 1, :]).then_inc(parts_chain, 1)
            settled(pool, parts_chain, PARTS * a + 5)
            for k in range(3):
                last = nc.gpsimd.tensor_tensor(sel[b][:, 1 + k, :, :], sel[b][:, 0, :, :],
                                               part[:, k, :].unsqueeze(2).to_broadcast([P, QW * CHUNKS, WIN]), ALU.mult)
            last.then_inc(wsel_ready, 1)

        weight_parts(0, 0)
        first_half(HT - 1, 0, P)

        def store_rows(i, b, weights):
            a = 2 * i + b
            settled(pool, counts_copied, a + 1)
            if not isinstance(i, int) or i > 0:
                settled(pool, count_stored[b], 16 * i)
            nc.gpsimd.tensor_copy(count_row[b][:, :], count_f[b][:, :]).then_inc(count_row_ready, 1)
            settled(pool, count_row_ready, a + 1)
            pool.dma_start(count_dram[rows(a), :], count_row[b][:, :]).then_inc(count_stored[b], 16)
            if weights:
                settled(pool, weights_copied, a + 1)
                pool.dma_start(wt_dram[rows(a), :], weight_row[b][:, :]).then_inc(weights_stored[b], 16)

        weight_parts(0, 1)
        store_rows(0, 0, True)
        weight_parts(1, 0)
        store_rows(0, 1, True)
        with pool.Fori(1, WT_TILES // 2 - 1) as i:
            weight_parts(i, 1)
            store_rows(i, 0, True)
            weight_parts(i + 1, 0)
            store_rows(i, 1, True)
        weight_parts(WT_TILES // 2 - 1, 1)
        store_rows(WT_TILES // 2 - 1, 0, True)
        store_rows(WT_TILES // 2 - 1, 1, True)
        store_rows(HT - 1, 0, False)
        store_rows(HT - 1, 1, False)
        first_half(HT - 1, 1, N - (T - 1) * P)

        pool.wait_ge(complete_ready, 1)
        whole = pool.value_load(complete[0:1, 0:1], min_val=0, max_val=1)
        with pool.If(whole == 0):
            for b in range(2):
                pool.wait_ge(count_stored[b], 16 * HT)
            with pool.Fori(0, T) as a:
                settled(pool, gen_copied, 2 * (a + 1) + 1)
                nc.gpsimd.tensor_copy(count_row[0][:, :], count_f[0][:, :]).then_inc(gen_row_ready, 1)
        pool.sem_inc(built, 1)

        half = [xres[c % 2][:, c // 2 * HID:(c // 2 + 1) * HID] for c in range(4)]

        def load_half(t):
            n = min(P, N - t * P)
            pool.dma_start(half[t % 4][0:n, :], x[t * P:t * P + n, HID:D]).then_inc(half_landed[t % 4], 16)

        for b in range(2):
            pool.wait_ge(stored[b], 16 * d.pairs(HT))
        for t in range(4):
            load_half(t)
        for t in range(T):
            pool.wait_ge(half_landed[t % 4], 16 * (t // 4 + 1))
            pool.wait_ge(sum_read, T * (GATES - 1) + t + 1)
            nc.gpsimd.tensor_tensor(half[t % 4], half[t % 4], g[:, t, :], ALU.add).then_inc(half_added, 1)
            pool.wait_ge(half_added, t + 1)
            pool.dma_start(x1_dram[t * P:(t + 1) * P, HID:D], half[t % 4]).then_inc(half_stored[t % 2], 16)
            if 1 <= t < T - 3:
                pool.wait_ge(half_stored[(t - 1) % 2], 16 * ((t - 1) // 2 + 1))
                load_half(t + 3)

        d = dense[1]

        def load1(i, b):
            pool.dma_start(xres[b][:, :], x1_dram[rows(2 * i + b), :]).then_inc(res_landed[b], 16)

        def store1(i, b):
            t = 2 * i + b
            settled(pool, product_read[b], d.pairs(i + 1))
            nc.gpsimd.tensor_tensor(xres[b][:, :], xres[b][:, :], row_all[:, :], ALU.add).then_inc(res_added, 1)
            settled(pool, res_added, d.tiles(t + 1))
            pool.dma_start(x2_dram[rows(t), :], xres[b][:, :]).then_inc(stored[b], 16)
            settled(pool, stored[b], 16 * d.pairs(i + 1))

        pool.wait_ge(bias1_landed, 16)
        for b in range(2):
            pool.wait_ge(half_stored[b], 16 * HT)
            load1(0, b)
        with pool.Fori(0, HT - 1) as i:
            for b in range(2):
                store1(i, b)
                load1(i + 1, b)
        store1(HT - 1, 0)
        store1(HT - 1, 1)

        def load2(i, b):
            pool.dma_start(xres[b][:, :], x2_dram[rows(2 * i + b), :]).then_inc(agg_landed[b], 16)

        def store2(i, b):
            settled(pool, agg_read, 2 * GRP + 2 * i + b + 1)
            pool.dma_start(x3_dram[rows(2 * i + b), :], xres[b][:, :]).then_inc(agg_stored[b], 16)
            settled(pool, agg_stored[b], 16 * (i + 1))

        load2(0, 0)
        load2(0, 1)
        with pool.Fori(0, HT - 1) as i:
            for b in range(2):
                store2(i, b)
                load2(i + 1, b)
        for b in range(2):
            store2(HT - 1, b)
            pool.dma_start(att_all[b][:, :], att[0, b * D:(b + 1) * D].partition_broadcast(P)).then_inc(att_landed, 16)


        def sum_e(grp, s, first):
            n = T * grp + s
            settled(pool, att_e_ready, n + 1)
            if not first or s > 0:
                settled(pool, e_summed, n)
            if s == 0:
                nc.gpsimd.tensor_copy(e_part[:, :], att_e[s][:, :]).then_inc(e_summed, 1)
            elif s < T - 1:
                nc.gpsimd.tensor_tensor(e_part[:, :], e_part[:, :], att_e[s][:, :], ALU.add).then_inc(e_summed, 1)
            else:
                if not first:
                    settled(pool, gat_ready, GRP * grp)
                nc.gpsimd.tensor_tensor(e_sum[:, :], e_part[:, :], att_e[s][:, :], ALU.add).then_inc(e_summed, 1)

        for s in range(T):
            sum_e(0, s, True)
        with pool.Fori(1, GROUPS) as grp:
            for s in range(T):
                sum_e(grp, s, False)

    COUNTS = ps[:, 0:NP]
    WEIGHTS = ps[:, 3 * BANK:3 * BANK + D]
    COUNT_T = ps[:, 5 * BANK:5 * BANK + NP]
    BLOCKS = [(0, BANK), (BANK, 2 * BANK), (2 * BANK, NP)]
    SUMS = [ps[:, k * BANK:(k + 1) * BANK] for k in range(HT)]
    U_ALL = ps[:, HT * BANK:HT * BANK + HALF]
    AGG2 = [[ps[:, (4 * c + 2 * j) * BANK:(4 * c + 2 * j + 2) * BANK] for j in range(GRP)] for c in range(2)]
    AL_FIRST = T - 2
    EARLY = 2
    AGG = [ps[:, 4 * j * BANK:(4 * j + 2) * BANK] for j in range(GRP)]
    DEN = [ps[:, (2 + j) * BANK:(2 + j) * BANK + 2] for j in range(GRP)]


    @block.scalar
    def _(act):
        dense_act(act, dense[0], lambda i, b: None)

        def take_rows(i, b, weights):
            a = 2 * i + b
            act.wait_ge(count_transposed[b], i)
            act.wait_ge(count_row_ready, 2 * i)
            if weights:
                act.wait_ge(counts_ready, a + 1)
            else:
                act.wait_ge(onehot_used[CHUNKS - 1], a + 1)
            nc.scalar.activation(count_f[b][:, :], COUNTS, ACT.Copy,
                                 accum_out=deg[:, bass.ds(a, 1)]).then_inc(counts_copied, 1)
            if weights:
                act.wait_ge(onehot_used[CHUNKS - 1], a + 1)
                act.wait_ge(weights_stored[b], 16 * i)
                nc.scalar.activation(weight_row[b][:, :], WEIGHTS, ACT.Copy).then_inc(weights_copied, 1)
            act.wait_ge(count_transposed[b], i + 1)
            nc.scalar.activation(countT[:, :, bass.ds(a * P, P)], COUNT_T.rearrange("p (s n) -> p s n", n=P),
                                 ACT.Copy).then_inc(countT_ready, 1)

        take_rows(0, 0, True)
        take_rows(0, 1, True)
        with act.Fori(1, WT_TILES // 2) as i:
            take_rows(i, 0, True)
            take_rows(i, 1, True)
        take_rows(HT - 1, 0, False)
        take_rows(HT - 1, 1, False)

        act.wait_ge(complete_ready, 1)
        whole = act.value_load(complete[0:1, 0:1], min_val=0, max_val=1)
        with act.If(whole == 0):
            act.wait_ge(count_row_ready, T)
            for b in range(2):
                act.wait_ge(weights_stored[b], 16 * WT_TILES // 2)
            act.sem_inc(gen_copied, 1)
            act.sem_inc(gen_countT_ready, 1)
            with act.Fori(0, T) as a:
                act.wait_ge(gen_summed, a + 1)
                act.wait_ge(gen_stored, 32 * a + 1)
                nc.scalar.activation(count_f[0][:, :], COUNTS, ACT.Copy,
                                     accum_out=deg[:, bass.ds(a, 1)]).then_inc(gen_copied, 1)
                nc.scalar.activation(weight_row[0][:, :], WEIGHTS, ACT.Copy).then_inc(gen_copied, 1)
                act.wait_ge(gen_transposed, a + 1)
                nc.scalar.activation(countT[:, :, bass.ds(a * P, P)], COUNT_T.rearrange("p (s n) -> p s n", n=P),
                                     ACT.Copy).then_inc(gen_countT_ready, 1)
            act.wait_ge(gen_countT_ready, T + 1)
        act.sem_inc(built, 1)

        act.wait_ge(norm_chain, 2)
        nc.scalar.activation(norm_root[:, :, :], norm[:, :, :], ACT.Sqrt).then_inc(norm_root_ready, 1)
        nc.scalar.activation(rden[:, 0, 0:1], zeros[:, 0:1], ACT.Tanh).then_inc(tanh_idle, 1)

        def g_split(t):
            nc.scalar.activation(g_hi[:, t, :], g[:, t, :], ACT.Identity,
                                 scale=dis[:, 0, t:t + 1]).then_inc(g_hi_ready, 1)

        def tanh(q, r, h, s):
            k = s % SLOTS
            act.wait_ge(mask_used[k], 2 * q + s // SLOTS)
            if s == 0:
                act.wait_ge(u_spread, q + 1)
            if h == 0:
                act.wait_ge(gates_ready, T * r + s + 1)
            nc.scalar.activation(mask[k][:, :], U_ALL, ACT.Tanh, bias=v[:, s:s + 1]).then_inc(tanh_ready, 1)

        def mask_hi_of(q, s):
            k = s % SLOTS
            act.wait_ge(mask_ready, T * q + s + 1)
            nc.scalar.activation(mask_hi[k][:, :], mask[k][:, :], ACT.Copy).then_inc(mask_hi_ready, 1)

        def half_act(q, r, h, split, last=False):
            for s in range(T):
                if s < T - 1:
                    mask_hi_of(q, s + 1)
                elif not last:
                    mask_hi_of(q + 1, 0)
                if s < T - TANH_LEAD:
                    tanh(q, r, h, s + TANH_LEAD)
                elif not last:
                    tanh(q + 1, r + h, 1 - h, s + TANH_LEAD - T)
                if isinstance(q, int) and q == 0 and s + 2 < T:
                    g_split(s + 2)
                if last:
                    if 1 <= s <= KT // 2:
                        split_act(act, dense[1], [2 * s - 2, 2 * s - 1])
                    if s == T - TANH_LEAD:
                        root_act(act, dense[1], 0, 0)
                    if s == T - TANH_LEAD + 1:
                        root_act(act, dense[1], 0, 1)
                    if s >= T - TANH_LEAD + 1:
                        h_act(act, dense[1], 0, s - (T - TANH_LEAD + 1))
                if not split:
                    continue
                if h == 1 and s >= HT:
                    t = s - HT
                    act.wait_ge(sum_read, HT * q - HT + t + 1)
                    act.wait_ge(mask_used[t % SLOTS], 2 * q + 1)
                    g_split(t)
                if h == 0 and 1 <= s < 1 + HT:
                    act.wait_ge(sum_read, HT * q - HT + s)
                    g_split(s - 1 + HT)

        act.wait_ge(dis_ready, 1)
        for b in range(2):
            act.wait_ge(product_ready[b], dense[0].pairs(HT))
            act.wait_ge(product_read[b], dense[0].pairs(HT))
        tanh(0, 0, 0, 0)
        g_split(0)
        mask_hi_of(0, 0)
        g_split(1)
        for s in range(1, TANH_LEAD):
            tanh(0, 0, 0, s)
        half_act(0, 0, 0, False)
        with act.Fori(0, GATES - 1) as r:
            half_act(2 * r + 1, r, 1, True)
            half_act(2 * r + 2, r + 1, 0, True)
        half_act(2 * GATES - 1, GATES - 1, 1, False, last=True)

        transposed_act(act, dense[1], 0, 0)

        dense_act(act, dense[1], lambda i, b: None, dense[2])

        def y_act(d, i, b):
            t = 2 * i + b
            act.wait_ge(product_ready[b], d.pairs(i + 1))
            if d.n == 2:
                nc.scalar.activation(y_all[:, bass.ds(t, 1), 0, :].rearrange("p a n -> p (a n)"), PRODUCT[d.n][b], ACT.Identity,
                                     scale=dis[:, 1, bass.ds(t, 1)]).then_inc(y_hi_ready, 1)
            else:
                nc.scalar.activation(y_all[:, bass.ds(t, 1), 0, :].rearrange("p a n -> p (a n)"), PRODUCT[d.n][b],
                                     ACT.Copy).then_inc(y_hi_ready, 1)

        def counts_act(grp, s, ring=cnt2):
            act.wait_ge(cnt_used[s % SLOTS], 2 * grp + s // SLOTS)
            nc.scalar.activation(ring[s % SLOTS][:, :], countT[:, s, bass.ds(grp * GC, GC)],
                                 ACT.Copy).then_inc(cnt_ready, 1)

        def first_counts():
            act.wait_ge(h_transposed[1], dense[2].pairs(HT))
            act.wait_ge(loops_added, T)
            for s in range(SLOTS):
                counts_act(0, s)

        dense_act(act, dense[2], lambda i, b: y_act(dense[2], i, b), late=first_counts)
        for s in range(SLOTS, T):
            counts_act(0, s)
        for s in range(T):
            counts_act(1, s)
        split_act(act, dense[3], range(KT))
        with act.Fori(2, GROUPS - 1) as grp:
            for s in range(T):
                counts_act(grp, s)
        for s in range(T):
            counts_act(GROUPS - 1, s, cnt2_last)
            if s >= T - 2:
                root_act(act, dense[3], 0, s - (T - 2))
                h_act(act, dense[3], 0, s - (T - 2))
        transposed_act(act, dense[3], 0, 0)

        def exps(grp, s):
            act.wait_ge(leaky_ready, T * grp + s + 1)
            nc.scalar.activation(att_e[s][:, :], att_e[s][:, :], ACT.Exp, scale=-1.0).then_inc(exp_ready, 1)

        def att_hi_of(grp, s):
            act.wait_ge(att_e_ready, T * grp + s + 1)
            nc.scalar.activation(att_hi[s][:, :], att_e[s][:, :], ACT.Copy).then_inc(att_hi_ready, 1)

        ALL = slice(0, D)

        def gat_take(m, j, cols=ALL, first=True):
            act.wait_ge(gat_ready, m + 1)
            if first:
                nc.scalar.activation(rden[:, j, 0:1], DEN[j][:, 0:1], ACT.Copy).then_inc(den_taken, 1)
            nc.scalar.activation(gat_sums[j][:, cols], AGG[j][:, cols], ACT.Copy).then_inc(gat_read, 1)

        def elu_act(m, j, cols=ALL):
            act.wait_ge(gat_neg_ready, m + 1)
            nc.scalar.activation(elu_neg[j][:, cols], elu_neg[j][:, cols], ACT.Exp).then_inc(gat_exp_ready, 1)
            nc.scalar.activation(gat_sums[j][:, cols], gat_sums[j][:, cols], ACT.Relu,
                                 scale=rden[:, j, 1:2]).then_inc(gat_pos_ready, 1)

        def attention_act(grp, steps, first, last):
            for s in steps:
                if s < T - 1:
                    exps(grp, s + 1)
                elif not last:
                    exps(grp + 1, 0)
                att_hi_of(grp, s)
                if first and s == HT + 2:
                    act.wait_ge(al_spread, 2)
                    nc.scalar.activation(al_all[:, AL_FIRST * P:NP], TRANSPOSED[:, 0:NP - AL_FIRST * P],
                                         ACT.Copy).then_inc(al_all_ready, 1)
                if not first and s == 2:
                    for j in range(GRP):
                        gat_take(GRP * (grp - 1) + j, j)
                if not first and s in (5, 6):
                    elu_act(GRP * (grp - 1) + s - 5, s - 5)

        def attention_start():
            act.wait_ge(al_spread, 1)
            nc.scalar.activation(al_all[:, 0:AL_FIRST * P], TRANSPOSED, ACT.Copy).then_inc(al_all_ready, 1)
            exps(0, 0)
            attention_act(0, range(EARLY), True, False)

        dense_act(act, dense[3], lambda i, b: y_act(dense[3], i, b), late=attention_start)
        attention_act(0, range(EARLY, T), True, False)
        with act.Fori(1, GROUPS - 1) as grp:
            attention_act(grp, range(T), False, False)
        attention_act(GROUPS - 1, range(T), False, True)
        gat_take(T - 2, 0)
        elu_act(T - 2, 0)
        for half in range(2):
            cols = slice(half * HID, (half + 1) * HID)
            gat_take(T - 1 + half, 1, cols, half == 0)
            elu_act(T - 1 + half, 1, cols)

    @block.vector
    def _(dve):
        dve.wait_ge(consts_done, 4)
        d0 = dense[0]

        def x1(i, b):
            if isinstance(i, int) and i == HT - 1 and b == 0:
                dve.wait_ge(iota_done, 2)
                select(0, 0)
            dve.wait_ge(consts_landed, 32)
            dve.wait_ge(product_ready[b], d0.pairs(i + 1))
            nc.vector.tensor_tensor(g[:, bass.ds(2 * i + b, 1), :].rearrange("p a n -> p (a n)"), PRODUCT[0][b][:, 0:HID],
                                    b1_all[:, :], ALU.add).then_inc(product_read[b], 1)

        def select(i, b):
            a = 2 * i + b
            dve.wait_ge(ends_landed[b], 16 * 3 * QW * (i + 1))
            if not isinstance(i, int) or i > 0:
                dve.wait_ge(onehot_used[CHUNKS - 1], a - 1)
            nc.vector.tensor_copy(ends[b][:, :, :], ends_raw[b][:, :, :]).then_inc(ends_ready, 1)
            dve.wait_ge(ends_ready, a + 1)
            nc.vector.tensor_tensor(
                sel[b][:, 0, :, :].rearrange("p (j c) i -> p j c i", c=CHUNKS),
                ends[b][:, 1, :].rearrange("p (j c) -> p j c", c=CHUNKS).unsqueeze(3).to_broadcast([P, QW, CHUNKS, WIN]),
                iota_f[:, bass.ds(a * P, P)].rearrange("p (j i) -> p j i", i=WIN).unsqueeze(2).to_broadcast([P, QW, CHUNKS, WIN]),
                ALU.is_equal).then_inc(sel_ready, 1)

        def onehots(i, b, nxt, chunks=range(CHUNKS), behind=None):
            for c in chunks:
                dve.wait_ge(onehot_used[c], 2 * i + b)
                for j in range(QW):
                    last = nc.vector.tensor_scalar(onehot[c][j][:, :], iota_h[:, :], ends[b][:, 0, j * CHUNKS + c:j * CHUNKS + c + 1],
                                                   None, ALU.is_equal)
                last.then_inc(onehot_ready, 1)
                if behind is not None:
                    behind(c)
                if c == CHUNKS - 1 and nxt is not None:
                    select(*nxt)

        def edges_below(quarter):
            n = EC // 4
            cols = slice(quarter * n, (quarter + 1) * n)
            dve.wait_ge(firsts_done, 1)
            dve.wait_ge(dst_ready, 1)
            nc.vector.tensor_tensor(below[0:EP, cols, :], dst_h[0:EP, cols].unsqueeze(2).to_broadcast([EP, n, WINDOWS]),
                                    firsts[0:EP, :].unsqueeze(1).to_broadcast([EP, n, WINDOWS]),
                                    ALU.is_lt).then_inc(below_ready, 1)

        def window_starts():
            dve.wait_ge(below_summed, 1)
            nc.vector.tensor_reduce(below_n[0:1, :], ps[0:1, 0:DG * WINDOWS].rearrange("p (c w) -> p w c", w=WINDOWS), AX_X,
                                    ALU.add).then_inc(below_chain, 1)
            dve.wait_ge(below_chain, 1)
            nc.vector.tensor_scalar(starts[0:1, :], below_n[0:1, :], float(E - CAP), None, ALU.min).then_inc(starts_ready, 1)

        def first_selections():
            onehots(0, 0, None, range(2))

        dense_dve(dve, d0, x1, asides=[lambda q=q: edges_below(q) for q in range(4)] + [window_starts], late=first_selections)

        onehots(0, 0, (0, 1), range(2, CHUNKS))
        onehots(0, 1, (1, 0))
        with dve.Fori(1, HT - 2) as i:
            onehots(i, 0, (i, 1))
            onehots(i, 1, (i + 1, 0))

        def gates(t, count):
            if not isinstance(count, int) or count > 0:
                dve.wait_ge(gates_ready, count)
            nc.vector.tensor_tensor_reduce(gate_scratch[:, :], g[:, t, :], gw[:, 0:HID], 1.0, 0.0, ALU.mult, ALU.add,
                                           u[:, t:t + 1]).then_inc(u_ready, 1)
            dve.wait_ge(u_ready, count + 1)
            nc.vector.tensor_tensor_reduce(gate_scratch[:, :], g[:, t, :], gw[:, HID:2 * HID], 1.0, gb_col[:, 0:1], ALU.mult, ALU.add,
                                           v[:, t:t + 1]).then_inc(gates_ready, 1)

        def g_rest(t, done):
            dve.wait_ge(g_hi_ready, done + 1)
            nc.vector.scalar_tensor_tensor(g_lo[:, t, :], g[:, t, :], dis[:, 0, t:t + 1], g_hi[:, t, :].bitcast(F32),
                                           ALU.mult, ALU.subtract).then_inc(g_lo_ready, 1)

        dve.wait_ge(gw_landed, 16)
        nc.vector.tensor_copy(gb_col[:, :], gb[:, 0:1]).then_inc(gb_chain, 1)
        dve.wait_ge(gb_chain, 1)
        onehots(HT - 2, 0, (HT - 2, 1), behind=lambda c: gates(c, c))
        onehots(HT - 2, 1, (HT - 1, 0))
        onehots(HT - 1, 0, (HT - 1, 1))
        onehots(HT - 1, 1, None)

        dve.wait_ge(counts_copied, T)
        nc.vector.reduce_sum(captured[:, :], deg[:, :], AX_X).then_inc(captured_ready, 1)
        dve.wait_ge(captured_summed, 1)
        nc.vector.tensor_scalar(complete[:, :], ps[:, 0:1], float(E), None, ALU.is_equal).then_inc(complete_ready, 1)
        dve.wait_ge(complete_ready, 1)
        whole = dve.value_load(complete[0:1, 0:1], min_val=0, max_val=1)
        with dve.If(whole == 0):
            dsel = sel[0][:, :, :, :].rearrange("p k a i -> p k (a i)").rearrange("p k (c m) -> p k c m", m=P)
            STEPS = 8
            with dve.Fori(0, T) as a:
                with dve.Fori(0, GENERAL_CHUNKS) as c:
                    n = a * GENERAL_CHUNKS + c
                    dve.wait_ge(gen_landed, 48 * (n + 1))
                    dve.wait_ge(gen_used, n + 1)
                    nc.vector.tensor_copy(ends[0][0:EP, :, 0:CHUNKS], ends_raw[0][0:EP, :, 0:CHUNKS]).then_inc(gen_chain, 1)
                    nc.vector.tensor_copy(ew_part[0][0:EP, 0, 0:CHUNKS], ew[0][0:EP, 0:CHUNKS]).then_inc(gen_chain, 1)
                    dve.wait_ge(gen_chain, STEPS * n + 2)
                    nc.vector.tensor_tensor(ew_rest[0][0:EP, 0, 0:CHUNKS], ew[0][0:EP, 0:CHUNKS], ew_part[0][0:EP, 0, 0:CHUNKS],
                                            ALU.subtract).then_inc(gen_chain, 1)
                    dve.wait_ge(gen_chain, STEPS * n + 3)
                    nc.vector.tensor_copy(ew_part[0][0:EP, 1, 0:CHUNKS], ew_rest[0][0:EP, 0, 0:CHUNKS]).then_inc(gen_chain, 1)
                    dve.wait_ge(gen_chain, STEPS * n + 4)
                    nc.vector.tensor_tensor(ew_rest[0][0:EP, 1, 0:CHUNKS], ew_rest[0][0:EP, 0, 0:CHUNKS], ew_part[0][0:EP, 1, 0:CHUNKS],
                                            ALU.subtract).then_inc(gen_chain, 1)
                    dve.wait_ge(gen_chain, STEPS * n + 5)
                    nc.vector.tensor_copy(ew_part[0][0:EP, 2, 0:CHUNKS], ew_rest[0][0:EP, 1, 0:CHUNKS]).then_inc(gen_chain, 1)
                    nc.vector.tensor_tensor(
                        dsel[0:EP, 0], ends[0][0:EP, 1, 0:CHUNKS].unsqueeze(2).to_broadcast([EP, CHUNKS, P]),
                        iota_f[0:EP, bass.ds(a * P, P)].unsqueeze(1).to_broadcast([EP, CHUNKS, P]),
                        ALU.is_equal).then_inc(gen_chain, 1)
                    dve.wait_ge(gen_chain, STEPS * n + 7)
                    for k in range(3):
                        last = nc.vector.tensor_tensor(dsel[0:EP, 1 + k], dsel[0:EP, 0],
                                                       ew_part[0][0:EP, k, 0:CHUNKS].unsqueeze(2).to_broadcast([EP, CHUNKS, P]),
                                                       ALU.mult)
                    last.then_inc(gen_chain, 1)
                    for q in range(CHUNKS):
                        last = nc.vector.tensor_scalar(onehot[q // QW][q % QW][0:EP, :], iota_h[0:EP, :], ends[0][0:EP, 0, q:q + 1],
                                                       None, ALU.is_equal)
                    last.then_inc(gen_ready, 1)
            dve.wait_ge(gen_copied, 2 * T + 1)
            dve.wait_ge(gen_countT_ready, T + 1)

        dve.wait_ge(countT_ready, T)
        nc.vector.tensor_scalar(norm[:, 0, :], deg[:, :], 1.0, None, ALU.max).then_inc(norm_chain, 1)
        nc.vector.tensor_scalar(norm[:, 1, :], deg[:, :], 1.0, None, ALU.add).then_inc(norm_chain, 1)
        dve.wait_ge(norm_root_ready, 1)
        nc.vector.reciprocal(dis[:, :, :], norm_root[:, :, :]).then_inc(norm_chain, 1)
        dve.wait_ge(norm_chain, 3)
        nc.vector.tensor_tensor(norm_step[:, :, :], dis[:, :, :], dis[:, :, :], ALU.mult).then_inc(norm_chain, 1)
        dve.wait_ge(norm_chain, 4)
        nc.vector.tensor_tensor(norm_step[:, :, :], norm_step[:, :, :], norm[:, :, :], ALU.mult).then_inc(norm_chain, 1)
        dve.wait_ge(norm_chain, 5)
        nc.vector.tensor_scalar(norm_step[:, :, :], norm_step[:, :, :], -0.5, 1.5, ALU.mult, ALU.add).then_inc(norm_chain, 1)
        dve.wait_ge(norm_chain, 6)
        nc.vector.tensor_tensor(dis[:, :, :], dis[:, :, :], norm_step[:, :, :], ALU.mult).then_inc(dis_ready, 1)
        dve.wait_ge(dis_ready, 1)

        def mask_of(q, h, s):
            k = s % SLOTS
            dve.wait_ge(tanh_ready, T * q + s + 1)
            nc.vector.tensor_tensor(mask[k][:, :], mask[k][:, :], countT[:, s, h * HALF:(h + 1) * HALF], ALU.mult).then_inc(mask_ready, 1)

        def mask_rest(q, s):
            k = s % SLOTS
            dve.wait_ge(mask_hi_ready, T * q + s + 1)
            nc.vector.tensor_tensor(mask_lo[k][:, :], mask[k][:, :], mask_hi[k][:, :].bitcast(F32), ALU.subtract).then_inc(mask_lo_ready, 1)

        def take_sums(q, h):
            for dd in range(HT):
                t = HT * h + dd
                if dd < HT - 1:
                    dve.wait_ge(sum_ready, (HT - 1) * q + dd + 1)
                else:
                    dve.wait_ge(mask_used[SLOTS - 1], 2 * q + 2)
                nc.vector.scalar_tensor_tensor(g[:, t, :], SUMS[dd], dis[:, 0, t:t + 1], g[:, t, :],
                                               ALU.mult, ALU.add).then_inc(sum_read, 1)

        def half_dve(q, h, nxt, last=False):
            if nxt is not None:
                dve.wait_ge(gw_landed, 16 * (nxt + 1))
                if h == 1:
                    nc.vector.tensor_copy(gb_col[:, :], gb[:, bass.ds(nxt, 1)]).then_inc(gb_chain, 1)
            for s in range(T):
                if s < T - 2:
                    mask_of(q, h, s + 2)
                elif not last:
                    mask_of(q + 1, 1 - h, s + 2 - T)
                if not (isinstance(q, int) and q == 0 and s == 0):
                    mask_rest(q, s)
                if last:
                    if 1 <= s <= KT // 2:
                        split_dve(dve, dense[1], [2 * s - 2, 2 * s - 1])
                    if s == T - TANH_LEAD - 1:
                        stats_dve(dve, dense[1], 0, 0)
                    if s == T - TANH_LEAD:
                        scale_dve(dve, dense[1], 0, 0)
                        stats_dve(dve, dense[1], 0, 1)
                    if s == T - TANH_LEAD + 1:
                        scale_dve(dve, dense[1], 0, 1)
                if s == 0 and not (isinstance(q, int) and q == 0):
                    take_sums(q - 1, 1 - h)
                if isinstance(q, int) and q == 0:
                    if s < HT:
                        gates(s + HT, s + HT)
                    if s + 2 < T:
                        g_rest(s + 2, s + 2)
                if nxt is None:
                    continue
                if 1 <= s < 1 + HT:
                    t = s - 1 + (HT if h == 0 else 0)
                    if s == 1:
                        dve.wait_ge(sum_read, HT * q)
                        dve.wait_ge(gb_chain, nxt + 1)
                        dve.wait_ge(u_spread, q + 1)
                    gates(t, T * nxt + t)
                    if h == 0:
                        g_rest(t, T * nxt + t)
                if h == 1 and s >= HT:
                    g_rest(s - HT, T * nxt + s - HT)

        mask_of(0, 0, 0)
        g_rest(0, 0)
        mask_rest(0, 0)
        mask_of(0, 0, 1)
        g_rest(1, 1)
        half_dve(0, 0, None)
        dve.wait_ge(res_added, dense[0].tiles(T))
        with dve.Fori(0, GATES - 1) as r:
            half_dve(2 * r + 1, 1, r + 1)
            half_dve(2 * r + 2, 0, r + 1)
        half_dve(2 * GATES - 1, 1, None, last=True)
        transposed_dve(dve, dense[1], 0, 0)
        take_sums(2 * GATES - 1, 1)

        d1 = dense[1]

        def residual(i, b):
            dve.wait_ge(res_landed[b], 16 * d1.pairs(i + 1))
            dve.wait_ge(product_ready[b], d1.pairs(i + 1))
            nc.vector.tensor_tensor(xres[b][:, :], PRODUCT[1][b], xres[b][:, :], ALU.add).then_inc(product_read[b], 1)

        dense_dve(dve, d1, residual, dense[2])

        d2 = dense[2]

        def y_rest(i, b):
            t = 2 * i + b
            dve.wait_ge(y_hi_ready, t + 1)
            nc.vector.scalar_tensor_tensor(y_all[:, bass.ds(t, 1), 1, :].rearrange("p a n -> p (a n)"), PRODUCT[2][b], dis[:, 1, bass.ds(t, 1)],
                                           y_all[:, bass.ds(t, 1), 0, :].rearrange("p a n -> p (a n)").bitcast(F32),
                                           ALU.mult, ALU.subtract).then_inc(product_read[b], 1)

        def self_loops():
            for t in range(T):
                nc.vector.tensor_tensor(countT[:, t, t * P:(t + 1) * P], countT[:, t, t * P:(t + 1) * P], ident[:, :],
                                        ALU.add).then_inc(loops_added, 1)

        dense_dve(dve, d2, y_rest, late=self_loops)

        def gcn_out(grp, j):
            t = GRP * grp + j
            sums = AGG2[grp % 2][j]
            if j == 0:
                dve.wait_ge(agg_ready, grp + 1)
            else:
                dve.wait_ge(cnt_used[SLOTS - 1], 2 * grp + 2)
            nc.vector.scalar_tensor_tensor(sums, sums, dis[:, 1, t:t + 1], row_all[:, :], ALU.mult, ALU.add).then_inc(agg_chain, 1)
            dve.wait_ge(agg_chain, t + 1)
            dve.wait_ge(agg_landed[j], 16 * (grp + 1))
            nc.vector.scalar_tensor_tensor(xres[j][:, :], sums, 0.0, xres[j][:, :], ALU.max, ALU.add).then_inc(agg_read, 1)

        def low_counts(grp):
            with dve.If(whole == 0):
                with dve.Fori(0, T) as s:
                    dve.wait_ge(low_used, T * grp + s + 1)
                    nc.vector.tensor_copy(top[:, :], countT[:, bass.ds(s, 1), grp * GC:(grp + 1) * GC].rearrange("p a n -> p (a n)")
                                          ).then_inc(low_chain, 1)
                    dve.wait_ge(low_chain, T * grp + s + 1)
                    nc.vector.tensor_tensor(low[:, :], countT[:, bass.ds(s, 1), grp * GC:(grp + 1) * GC].rearrange("p a n -> p (a n)"),
                                            top[:, :].bitcast(F32), ALU.subtract).then_inc(low_ready, 1)

        dve.wait_ge(loops_added, T)
        dve.wait_ge(b2_landed, 16)
        dve.sem_inc(agg_read, 2 * GRP)
        for grp in range(GROUPS):
            if grp == 2:
                split_dve(dve, dense[3], range(KT))
            if grp == GROUPS - 1:
                for b in range(2):
                    stats_dve(dve, dense[3], 0, b)
                    scale_dve(dve, dense[3], 0, b)
                transposed_dve(dve, dense[3], 0, 0)
            low_counts(grp)
            for j in range(GRP):
                gcn_out(grp, j)

        d3 = dense[3]

        def scores(i, b):
            t = 2 * i + b
            dve.wait_ge(att_landed, 32)
            dve.wait_ge(y_hi_ready, T + t + 1)
            nc.vector.tensor_tensor_reduce(row_all[:, :], PRODUCT[3][b], att_all[0][:, :], 1.0, 0.0, ALU.mult, ALU.add,
                                           al_col[b][:, 0:1]).then_inc(al_chain, 1)
            dve.wait_ge(al_chain, 2 * t + 1)
            nc.vector.tensor_tensor_reduce(row_all[:, :], PRODUCT[3][b], att_all[1][:, :], 1.0, 0.0, ALU.mult, ALU.add,
                                           al_col[b][:, 1:2]).then_inc(al_chain, 1)
            nc.vector.tensor_tensor(y_all[:, bass.ds(t, 1), 1, :].rearrange("p a n -> p (a n)"), PRODUCT[3][b],
                                    y_all[:, bass.ds(t, 1), 0, :].rearrange("p a n -> p (a n)").bitcast(F32),
                                    ALU.subtract).then_inc(product_read[b], 1)
            dve.wait_ge(al_chain, 2 * t + 2)
            nc.vector.tensor_copy(al[:, bass.ds(t, 1)], al_col[b][:, 0:1]).then_inc(al_copied, 1)
            nc.vector.tensor_copy(ar[:, bass.ds(t, 1)], al_col[b][:, 1:2]).then_inc(al_ready, 1)

        def logits(grp, s):
            if not isinstance(grp, int) or grp > 0:
                dve.wait_ge(att_used, T * (grp - 1) + s + 1)
            nc.vector.tensor_scalar(att_e[s][:, :], al_all[:, bass.ds(grp * GC, GC)], ar[:, s:s + 1], None, ALU.add).then_inc(logit_ready, 1)
            dve.wait_ge(logit_ready, T * grp + s + 1)
            nc.vector.scalar_tensor_tensor(att_e[s][:, :], att_e[s][:, :], SLOPE, att_e[s][:, :], ALU.mult, ALU.max).then_inc(leaky_ready, 1)

        def att_of(grp, s):
            dve.wait_ge(exp_ready, T * grp + s + 1)
            nc.vector.tensor_tensor(att_e[s][:, :], att_e[s][:, :], count[:, s, bass.ds(grp * GC, GC)], ALU.mult).then_inc(att_e_ready, 1)

        def att_rest(grp, s):
            dve.wait_ge(att_hi_ready, T * grp + s + 1)
            dve.wait_ge(e_summed, T * grp + s + 1)
            nc.vector.tensor_tensor(att_lo[s][:, :], att_e[s][:, :], att_hi[s][:, :].bitcast(F32), ALU.subtract).then_inc(att_lo_ready, 1)

        GAT_STEPS = 2
        ALL = slice(0, D)

        def elu_start(m, j, cols=ALL, first=True):
            if first:
                dve.wait_ge(den_taken, m + 1)
                nc.vector.tensor_scalar(rden[:, j, 0:1], rden[:, j, 0:1], EPS_GAT, None, ALU.add).then_inc(gat_chain, 1)
                dve.wait_ge(gat_chain, GAT_STEPS * m + 1)
                nc.vector.reciprocal(rden[:, j, 1:2], rden[:, j, 0:1]).then_inc(gat_chain, 1)
                dve.wait_ge(gat_chain, GAT_STEPS * m + 2)
            dve.wait_ge(gat_read, m + 1)
            nc.vector.tensor_scalar(elu_neg[j][:, cols], gat_sums[j][:, cols], rden[:, j, 1:2], 0.0, ALU.mult, ALU.min
                                    ).then_inc(gat_neg_ready, 1)

        def elu_end(m, grp, j, cols=ALL):
            dve.wait_ge(gat_landed[j], 16 * (grp + 1))
            dve.wait_ge(gat_exp_ready, m + 1)
            nc.vector.scalar_tensor_tensor(elu_neg[j][:, cols], elu_neg[j][:, cols], -1.0, xres[j][:, cols], ALU.add, ALU.add
                                           ).then_inc(elu_added, 1)
            dve.wait_ge(elu_added, m + 1)
            dve.wait_ge(gat_pos_ready, m + 1)
            nc.vector.tensor_tensor(xres[j][:, cols], elu_neg[j][:, cols], gat_sums[j][:, cols], ALU.add).then_inc(gat_added, 1)

        def attention_dve(grp, steps, first, last):
            for s in steps:
                if s < T - 2:
                    logits(grp, s + 2)
                elif not last:
                    if s == T - 2 and not first:
                        dve.wait_ge(al_all_ready, 2)
                    logits(grp + 1, s + 2 - T)
                if s < T - 1:
                    att_of(grp, s + 1)
                elif not last:
                    att_of(grp + 1, 0)
                att_rest(grp, s)
                if not first and s == 4:
                    for j in range(GRP):
                        elu_start(GRP * (grp - 1) + j, j)
                if not first and s in (7, 8):
                    elu_end(GRP * (grp - 1) + s - 7, grp - 1, s - 7)

        def attention_start():
            dve.wait_ge(al_ready, AL_FIRST)
            dve.wait_ge(count_landed, 16 * HT)
            dve.wait_ge(al_all_ready, 1)
            logits(0, 0)
            logits(0, 1)
            att_of(0, 0)
            attention_dve(0, range(EARLY), True, False)

        dense_dve(dve, d3, scores, late=attention_start)
        dve.wait_ge(al_ready, T)
        attention_dve(0, range(EARLY, T), True, False)
        with dve.Fori(1, GROUPS - 1) as grp:
            attention_dve(grp, range(T), False, False)
        attention_dve(GROUPS - 1, range(T), False, True)
        elu_start(T - 2, 0)
        elu_end(T - 2, GROUPS - 1, 0)
        for half in range(2):
            cols = slice(half * HID, (half + 1) * HID)
            elu_start(T - 1 + half, 1, cols, half == 0)
            elu_end(T - 1 + half, GROUPS - 1, 1, cols)

    @block.tensor
    def _(pe):
        pe.wait_ge(consts_done, 4)

        def sum_below():
            pe.wait_ge(below_ready, 4)
            for c in range(0, EC, DG):
                last = nc.tensor.matmul(ps[0:1, 0:DG * WINDOWS], ones_h[0:EP, 0:1], below[0:EP, c:c + DG, :].rearrange("p c w -> p (c w)"),
                                        start=(c == 0), stop=(c == EC - DG))
            last.then_inc(below_summed, 1)

        dense_pe(pe, dense[0], aside=sum_below)
        for b in range(2):
            pe.wait_ge(product_read[b], dense[0].pairs(HT))

        def rows_pe(i, b, weights):
            a = 2 * i + b
            pe.wait_ge(wsel_ready if weights else sel_ready, a + 1)
            pe.wait_ge(counts_copied, a)
            for c in range(CHUNKS):
                pe.wait_ge(onehot_ready, CHUNKS * a + c + 1)
                for lo, hi in BLOCKS:
                    for j in range(QW):
                        last = nc.tensor.matmul(COUNTS[j * WIN:(j + 1) * WIN, lo:hi], sel[b][:, 0, j * CHUNKS + c, :],
                                                onehot[c][j][:, lo:hi], start=(c == 0), stop=(c == CHUNKS - 1))
                if weights:
                    if c == CHUNKS - 1:
                        last.then_inc(counts_ready, 1)
                    if c == 0:
                        pe.wait_ge(weights_copied, a)
                    for lo, hi in BLOCKS[:2]:
                        for k in range(3):
                            for j in range(QW):
                                last = nc.tensor.matmul(WEIGHTS[j * WIN:(j + 1) * WIN, lo:hi], sel[b][:, 1 + k, j * CHUNKS + c, :],
                                                        onehot[c][j][:, lo:hi], start=(c == 0 and k == 0),
                                                        stop=(c == CHUNKS - 1 and k == 2))
                last.then_inc(onehot_used[c], 1)
            pe.wait_ge(counts_copied, a + 1)
            pe.wait_ge(countT_ready, a)
            for s in range(T):
                last = nc.tensor.transpose(COUNT_T[:, s * P:(s + 1) * P], count_f[b][:, s * P:(s + 1) * P], ident[:, :])
            last.then_inc(count_transposed[b], 1)

        rows_pe(0, 0, True)
        rows_pe(0, 1, True)
        with pe.Fori(1, WT_TILES // 2) as i:
            rows_pe(i, 0, True)
            rows_pe(i, 1, True)
        rows_pe(HT - 1, 0, False)
        rows_pe(HT - 1, 1, False)
        pe.wait_ge(captured_ready, 1)
        nc.tensor.matmul(ps[:, 0:1], ones[:, :], captured[:, :], start=True, stop=True).then_inc(captured_summed, 1)

        pe.wait_ge(complete_ready, 1)
        whole = pe.value_load(complete[0:1, 0:1], min_val=0, max_val=1)
        with pe.If(whole == 0):
            pe.sem_inc(gen_used, 1)
            dsel = sel[0][:, :, :, :].rearrange("p k a i -> p k (a i)").rearrange("p k (c m) -> p k c m", m=P)
            with pe.Fori(0, T) as a:
                pe.wait_ge(gen_copied, 2 * a + 1)
                for part, blocks in ((COUNTS, BLOCKS), (WEIGHTS, BLOCKS[:2])):
                    for lo, hi in blocks:
                        nc.tensor.matmul(part[:, lo:hi], zeros[:, :], iota_h[:, lo:hi], start=True, stop=False, skip_group_check=True)
                with pe.Fori(0, GENERAL_CHUNKS) as c:
                    n = a * GENERAL_CHUNKS + c
                    pe.wait_ge(gen_ready, n + 1)
                    for q in range(CHUNKS):
                        right = onehot[q // QW][q % QW]
                        for lo, hi in BLOCKS:
                            last = nc.tensor.matmul(COUNTS[:, lo:hi], dsel[0:EP, 0, q, :], right[0:EP, lo:hi], start=False, stop=False, skip_group_check=True)
                        for lo, hi in BLOCKS[:2]:
                            for k in range(3):
                                last = nc.tensor.matmul(WEIGHTS[:, lo:hi], dsel[0:EP, 1 + k, q, :], right[0:EP, lo:hi], start=False, stop=False, skip_group_check=True)
                    last.then_inc(gen_used, 1)
                for part, blocks in ((COUNTS, BLOCKS), (WEIGHTS, BLOCKS[:2])):
                    for lo, hi in blocks:
                        last = nc.tensor.matmul(part[:, lo:hi], zeros[:, :], iota_h[:, lo:hi], start=False, stop=True, skip_group_check=True)
                last.then_inc(gen_summed, 1)
                pe.wait_ge(gen_copied, 2 * a + 2)
                pe.wait_ge(gen_countT_ready, a + 1)
                for s in range(T):
                    last = nc.tensor.transpose(COUNT_T[:, s * P:(s + 1) * P], count_f[0][:, s * P:(s + 1) * P], ident[:, :])
                last.then_inc(gen_transposed, 1)
            pe.wait_ge(gen_copied, 2 * T + 1)
            pe.wait_ge(gen_countT_ready, T + 1)
        pe.sem_inc(built, 1)

        def spread_u(q, h):
            pe.wait_ge(u_ready, HT * q + HT)
            pe.wait_ge(tanh_ready, 2 * HT * q)
            for dd in range(HT):
                last = nc.tensor.matmul(U_ALL[:, dd * P:(dd + 1) * P], u[:, h * HT + dd:h * HT + dd + 1].to_broadcast([P, P]), ident[:, :],
                                        start=True, stop=True)
            last.then_inc(u_spread, 1)

        def half_pe(q, r, h):
            for s in range(T):
                k = s % SLOTS
                if s == HT + 2 and not is_last(q):
                    spread_u(q + 1, 1 - h)
                if s == T - 1 and is_last(q):
                    pe.wait_ge(tanh_ready, 2 * GATES * T)
                    transpose_pe(pe, dense[1], 0, 0)
                if h == 0:
                    pe.wait_ge(g_lo_ready, T * r + s + 1)
                pe.wait_ge(mask_lo_ready, 2 * HT * q + s + 1)
                for dd in range(HT):
                    if s == 0:
                        pe.wait_ge(sum_read, HT * q - HT + dd + 1) if q_has_before(q) else None
                    cols = slice(dd * P, (dd + 1) * P)
                    nc.tensor.matmul(SUMS[dd], mask_hi[k][:, cols], g_hi[:, s, :], start=(s == 0), stop=False)
                    nc.tensor.matmul(SUMS[dd], mask_hi[k][:, cols], g_lo[:, s, :], start=False, stop=False)
                    last = nc.tensor.matmul(SUMS[dd], mask_lo[k][:, cols], g_hi[:, s, :], start=False, stop=(s == T - 1))
                    if s == T - 1 and dd < HT - 1:
                        last.then_inc(sum_ready, 1)
                last.then_inc(mask_used[k], 1)

        def q_has_before(q):
            return not (isinstance(q, int) and q == 0)

        def is_last(q):
            return isinstance(q, int) and q == 2 * GATES - 1

        pe.wait_ge(countT_ready, T)
        spread_u(0, 0)
        half_pe(0, 0, 0)
        with pe.Fori(0, GATES - 1) as r:
            half_pe(2 * r + 1, r, 1)
            half_pe(2 * r + 2, r + 1, 0)
        half_pe(2 * GATES - 1, GATES - 1, 1)

        dense_pe(pe, dense[1], dense[2], lambda b: pe.wait_ge(sum_read, T * GATES - 1 + b))
        dense_pe(pe, dense[2])

        def low_pe(grp, sums):
            with pe.If(whole == 0):
                with pe.Fori(0, T) as s:
                    pe.wait_ge(low_ready, T * grp + s + 1)
                    for j in range(GRP):
                        for n in range(2):
                            for part in range(2):
                                last = nc.tensor.matmul(
                                    sums[j][:, n * BANK:(n + 1) * BANK], low[:, j * P:(j + 1) * P],
                                    y_all[:, bass.ds(s, 1), part, n * BANK:(n + 1) * BANK].rearrange("p a n -> p (a n)"),
                                    start=False, stop=False, skip_group_check=True)
                    last.then_inc(low_used, 1)

        pe.sem_inc(low_used, 1)

        def gcn_pe(grp, sums, ring=cnt2):
            for s in range(T):
                k = s % SLOTS
                if s == T - 1:
                    low_pe(grp, sums)
                if s == T - 2 and isinstance(grp, int):
                    transpose_pe(pe, dense[3], 0, 0)
                pe.wait_ge(product_read[s % 2], dense[2].pairs(s // 2 + 1))
                pe.wait_ge(cnt_ready, T * grp + s + 1)
                for j in range(GRP):
                    if s == 0:
                        pe.wait_ge(agg_read, GRP * grp + j + 1)
                        pe.wait_ge(product_read[0], dense[2].pairs(HT))
                    left = ring[k][:, j * P:(j + 1) * P]
                    for n in range(2):
                        out_n = sums[j][:, n * BANK:(n + 1) * BANK]
                        nc.tensor.matmul(out_n, left, y_hi[s][:, n * BANK:(n + 1) * BANK], start=(s == 0), stop=False)
                        last = nc.tensor.matmul(out_n, left, y_lo[s][:, n * BANK:(n + 1) * BANK], start=False, stop=(s == T - 1))
                    if s == T - 1 and j == 0:
                        last.then_inc(agg_ready, 1)
                last.then_inc(cnt_used[k], 1)

        with pe.Fori(0, GROUPS // 2) as i:
            gcn_pe(2 * i, AGG2[0])
            gcn_pe(2 * i + 1, AGG2[1])
        gcn_pe(GROUPS - 1, AGG2[0], cnt2_last)

        def spread_al(tiles):
            pe.wait_ge(al_copied, tiles[-1] + 1)
            for t in tiles:
                last = nc.tensor.matmul(TRANSPOSED[:, (t - tiles[0]) * P:(t - tiles[0] + 1) * P],
                                        al[:, t:t + 1].to_broadcast([P, P]), ident[:, :], start=True, stop=True)
            last.then_inc(al_spread, 1)

        dense_pe(pe, dense[3], free=lambda b: pe.wait_ge(agg_read, 2 * GRP + T - GRP * (1 - b)), late=lambda: spread_al(range(AL_FIRST)))

        def gat_step(s, j, ns):
            cols = slice(j * P, (j + 1) * P)
            for left, rights in ((att_hi[s][:, cols], (y_hi[s], y_lo[s])), (att_lo[s][:, cols], (y_hi[s],))):
                for n in ns:
                    for right in rights:
                        last = nc.tensor.matmul(AGG[j][:, n * BANK:(n + 1) * BANK], left, right[:, n * BANK:(n + 1) * BANK],
                                                start=(s == 0 and len(rights) == 2 and right is y_hi[s]),
                                                stop=(s == T - 1 and len(rights) == 1))
            return last

        def row_sums(j):
            return nc.tensor.matmul(DEN[j], e_sum[:, j * P:(j + 1) * P], ones[:, 0:2], start=True, stop=True)

        def gat_pe(grp, first):
            for s in range(T):
                if first:
                    pe.wait_ge(product_read[s % 2], dense[3].pairs(s // 2 + 1))
                    if s == HT:
                        pe.wait_ge(al_all_ready, 1)
                        spread_al(range(AL_FIRST, T))
                pe.wait_ge(att_lo_ready, T * grp + s + 1)
                for j in range(GRP):
                    if s == 0 and not first:
                        pe.wait_ge(gat_read, GRP * grp - GRP + j + 1)
                    last = gat_step(s, j, range(2))
                    if j == GRP - 1:
                        last.then_inc(att_used, 1)
                    if s == T - 1:
                        row_sums(j).then_inc(gat_ready, 1)

        gat_pe(0, True)
        with pe.Fori(1, GROUPS - 1) as grp:
            gat_pe(grp, False)
        for s in range(T):
            pe.wait_ge(att_lo_ready, T * (GROUPS - 1) + s + 1)
            if s == 0:
                pe.wait_ge(gat_read, T - GRP)
            gat_step(s, 0, range(2))
            last = gat_step(s, 1, [0])
        row_sums(0)
        row_sums(1).then_inc(gat_ready, 2)
        for s in range(T):
            last = gat_step(s, 1, [1])
        last.then_inc(gat_ready, 1)

    ctx.close()


_INS = ["x", "src", "dst", "edge_weight", "L0_gnn_W1", "L0_gnn_b1", "L0_gnn_gate_w", "L0_gnn_gate_b", "L1_gnn_bias",
        "L2_gnn_W", "L2_gnn_b", "L3_gnn_W", "L3_gnn_a"]


def kernel(**inputs):
    import numpy as np
    import concourse.bacc as bacc
    from concourse.bass_utils import run_bass_kernel_spmd

    nc = bacc.Bacc("TRN2", target_bir_lowering=False, num_devices=1)
    arrays, args = {}, []
    for name in _INS:
        a = np.ascontiguousarray(inputs[name])
        arrays[f"in_{name}"] = a
        args.append(nc.dram_tensor(f"in_{name}", a.shape, mybir.dt.from_np(a.dtype), kind="ExternalInput").ap())
    out = nc.dram_tensor("out_x", (N, D), F32, kind="ExternalOutput").ap()
    build_program(nc, *args, out)
    r = run_bass_kernel_spmd(nc, [arrays], core_ids=[0])
    return r.results[0]["out_x"]
```
